# Optimizing a Trainium2 kernel written in Bass

```python
import numpy as np
import jax
import jax.numpy as jnp

def _softmax(x, axis=-1):
    return jax.nn.softmax(x, axis=axis)

def _gelu(x):
    return jax.nn.gelu(x, approximate=True)

def _silu(x):
    return jax.nn.silu(x)

def _sigmoid(x):
    return jax.nn.sigmoid(x)

def _layernorm(x, axis=-1, eps=1e-05):
    m = jnp.mean(x, axis=axis, keepdims=True)
    v = jnp.var(x, axis=axis, keepdims=True)
    return (x - m) / jnp.sqrt(v + eps)

def _scatter_add(tgt, idx, src, axis=0):
    return tgt.at[idx].add(src)

def _segment_sum(src, seg, n):
    return jax.ops.segment_sum(src, seg, n)
kernel_name = 'mk_gnn_resnorm_d4_gnn_r8_e509a9'

def setup_inputs(seed: int=0):
    np.random.seed(seed)
    _w = jnp.asarray

    def _rec_inputs():
        import jax
        import jax.numpy as jnp
        _gk = jax.random.key(seed)
        x = -0.0002117 + 1 * jax.random.normal(jax.random.fold_in(_gk, 1), (6250, 256), jnp.float32)
        _s = jax.random.randint(jax.random.fold_in(_gk, 2), (50000,), 0, 6250, jnp.int32)
        _d = jax.random.randint(jax.random.fold_in(_gk, 3), (50000,), 0, 6250, jnp.int32)
        _loop = jnp.arange(6250, dtype=jnp.int32)
        src = jnp.concatenate([_s, _d, _loop])
        dst = jnp.concatenate([_d, _s, _loop])
        _o = jnp.argsort(dst, stable=True)
        src = src[_o]
        dst = dst[_o]
        edge_type_16 = jax.random.randint(jax.random.fold_in(_gk, 13), (106250,), 0, 16, jnp.int32)
        edge_weight1 = jax.random.uniform(jax.random.fold_in(_gk, 14), (106250, 1), jnp.float32, 0.0, 0.999998)
        return (x, src, dst, edge_type_16, edge_weight1)
    x, src, dst, edge_type_16, edge_weight1 = _rec_inputs()

    def _L0_gnn_setup():
        import jax, jax.numpy as jnp
        import numpy as np
        NEG_SLOPE = 0.2
        N_NODES = 12500
        N_EDGES = 200000
        IN_CH = 256
        HEADS = 4
        OUT_CH = 64
        key = jax.random.key(seed)
        k1, k2, k3, k4, k5 = jax.random.split(key, 5)
        x = jax.random.normal(k1, (N_NODES, IN_CH), dtype=jnp.float32)
        edge_index = jax.random.randint(k2, (2, N_EDGES), 0, N_NODES, dtype=jnp.int64)
        W = jax.random.normal(k3, (IN_CH, HEADS * OUT_CH), dtype=jnp.float32) / np.sqrt(IN_CH)
        att_src = jax.random.normal(k4, (HEADS, OUT_CH), dtype=jnp.float32) / np.sqrt(OUT_CH)
        att_dst = jax.random.normal(k5, (HEADS, OUT_CH), dtype=jnp.float32) / np.sqrt(OUT_CH)
        bias = jnp.zeros((HEADS * OUT_CH,), dtype=jnp.float32)
        return {'graph_node_features': x, 'edge_index': edge_index, 'W': W, 'att_src': att_src, 'att_dst': att_dst, 'bias': bias}
    _L0_gnn_all = _L0_gnn_setup()
    _L0_gnn_in = {k: v for k, v in _L0_gnn_all.items() if k in ('W', 'att_src', 'att_dst', 'bias')}
    del _L0_gnn_all

    def _L1_gnn_setup():
        import jax, jax.numpy as jnp
        import numpy as np
        N_NODES = 12500
        N_EDGES = 37500
        DIM = 256
        LN_EPS = 1e-05
        key = jax.random.key(seed)
        ks = jax.random.split(key, 4)
        scale = 1.0 / np.sqrt(DIM)
        h = jax.random.normal(ks[0], (N_NODES, DIM), dtype=jnp.float32)
        edge_index = jax.random.randint(ks[1], (2, N_EDGES), 0, N_NODES, dtype=jnp.int64)
        W1 = jax.random.normal(ks[2], (DIM, DIM), dtype=jnp.float32) * scale
        b1 = jnp.zeros((DIM,), dtype=jnp.float32)
        W2 = jax.random.normal(ks[3], (DIM, DIM), dtype=jnp.float32) * scale
        b2 = jnp.zeros((DIM,), dtype=jnp.float32)
        eps = jnp.zeros((), dtype=jnp.float32)
        gamma = jnp.ones((DIM,), dtype=jnp.float32)
        beta = jnp.zeros((DIM,), dtype=jnp.float32)
        return {'h': h, 'edge_index': edge_index, 'W1': W1, 'b1': b1, 'W2': W2, 'b2': b2, 'eps': eps, 'gamma': gamma, 'beta': beta}
    _L1_gnn_all = _L1_gnn_setup()
    _L1_gnn_in = {k: v for k, v in _L1_gnn_all.items() if k in ('W1', 'b1', 'W2', 'b2', 'eps', 'gamma', 'beta')}
    del _L1_gnn_all

    def _L2_gnn_setup():
        import jax, jax.numpy as jnp
        import numpy as np
        N, E = (6250, 100000)
        H, C_IN, C_HID, C_OUT = (4, 256, 64, 64)
        NEG_SLOPE = 0.2

        def leaky_relu(x, s=NEG_SLOPE):
            return jnp.where(x >= 0, x, s * x)

        def gat_conv(x, src, dst, W, att_src, att_dst, bias, n_nodes):
            Hh, Cc = (att_src.shape[1], att_src.shape[2])
            h = (x @ W).reshape(n_nodes, Hh, Cc)
            a_src = (h * att_src).sum(-1)
            a_dst = (h * att_dst).sum(-1)
            alpha = leaky_relu(a_src[src] + a_dst[dst])
            m = jax.ops.segment_max(alpha, dst, num_segments=n_nodes)
            e = jnp.exp(alpha - m[dst])
            denom = jax.ops.segment_sum(e, dst, num_segments=n_nodes)
            w = e / jnp.clip(denom, 1e-16)[dst]
            out = jax.ops.segment_sum(w[:, :, None] * h[src], dst, num_segments=n_nodes)
            return out.reshape(n_nodes, Hh * Cc) + bias
        key = jax.random.key(seed)
        ks = jax.random.split(key, 10)
        glorot = lambda k, shp: jax.random.normal(k, shp, jnp.float32) * np.sqrt(2.0 / (shp[0] + shp[-1]))
        return {'x': jax.random.normal(ks[0], (N, C_IN), jnp.float32), 'edge_index': jax.random.randint(ks[1], (2, E), 0, N, jnp.int32), 'W1': glorot(ks[2], (C_IN, H * C_HID)), 'att_src1': glorot(ks[3], (1, H, C_HID)), 'att_dst1': glorot(ks[4], (1, H, C_HID)), 'b1': jnp.zeros((H * C_HID,), jnp.float32), 'W2': glorot(ks[5], (H * C_HID, H * C_OUT)), 'att_src2': glorot(ks[6], (1, H, C_OUT)), 'att_dst2': glorot(ks[7], (1, H, C_OUT)), 'b2': jnp.zeros((H * C_OUT,), jnp.float32)}
    _L2_gnn_all = _L2_gnn_setup()
    _L2_gnn_in = {k: v for k, v in _L2_gnn_all.items() if k in ('W1', 'att_src1', 'att_dst1', 'b1', 'W2', 'att_src2', 'att_dst2', 'b2')}
    del _L2_gnn_all

    def _L3_gnn_setup():
        import jax, jax.numpy as jnp
        import numpy as np
        N_NODES = 2500
        N_EDGES = 40000
        NUM_RELS = 16
        IN_FEAT = 256
        OUT_FEAT = 256
        key = jax.random.key(seed)
        k_h, k_w, k_n, k_s, k_d, k_r = jax.random.split(key, 6)
        h = jax.random.normal(k_h, (N_NODES, IN_FEAT), dtype=jnp.float32)
        weight = jax.random.normal(k_w, (NUM_RELS, IN_FEAT, OUT_FEAT), dtype=jnp.float32)
        norm = jax.random.uniform(k_n, (N_EDGES, 1), dtype=jnp.float32)
        src = jax.random.randint(k_s, (N_EDGES,), 0, N_NODES, dtype=jnp.int32)
        dst = jax.random.randint(k_d, (N_EDGES,), 0, N_NODES, dtype=jnp.int32)
        rel_type = jax.random.randint(k_r, (N_EDGES,), 0, NUM_RELS, dtype=jnp.int32)
        return {'h': h, 'weight': weight, 'norm': norm, 'src': src, 'dst': dst, 'rel_type': rel_type}
    _L3_gnn_all = _L3_gnn_setup()
    _L3_gnn_in = {k: v for k, v in _L3_gnn_all.items() if k in ('weight',)}
    del _L3_gnn_all
    return {'x': x, 'src': src, 'dst': dst, 'edge_type_16': edge_type_16, 'edge_weight1': edge_weight1, 'L0_gnn_W': _L0_gnn_in['W'], 'L0_gnn_att_src': _L0_gnn_in['att_src'], 'L0_gnn_att_dst': _L0_gnn_in['att_dst'], 'L0_gnn_bias': _L0_gnn_in['bias'], 'L1_gnn_W1': _L1_gnn_in['W1'], 'L1_gnn_b1': _L1_gnn_in['b1'], 'L1_gnn_W2': _L1_gnn_in['W2'], 'L1_gnn_b2': _L1_gnn_in['b2'], 'L1_gnn_eps': _L1_gnn_in['eps'], 'L1_gnn_gamma': _L1_gnn_in['gamma'], 'L1_gnn_beta': _L1_gnn_in['beta'], 'L2_gnn_W1': _L2_gnn_in['W1'], 'L2_gnn_att_src1': _L2_gnn_in['att_src1'], 'L2_gnn_att_dst1': _L2_gnn_in['att_dst1'], 'L2_gnn_b1': _L2_gnn_in['b1'], 'L2_gnn_W2': _L2_gnn_in['W2'], 'L2_gnn_att_src2': _L2_gnn_in['att_src2'], 'L2_gnn_att_dst2': _L2_gnn_in['att_dst2'], 'L2_gnn_b2': _L2_gnn_in['b2'], 'L3_gnn_weight': _L3_gnn_in['weight']}

def reference(x, src, dst, edge_type_16, edge_weight1, L0_gnn_W, L0_gnn_att_src, L0_gnn_att_dst, L0_gnn_bias, L1_gnn_W1, L1_gnn_b1, L1_gnn_W2, L1_gnn_b2, L1_gnn_eps, L1_gnn_gamma, L1_gnn_beta, L2_gnn_W1, L2_gnn_att_src1, L2_gnn_att_dst1, L2_gnn_b1, L2_gnn_W2, L2_gnn_att_src2, L2_gnn_att_dst2, L2_gnn_b2, L3_gnn_weight):
    import jax
    import jax.numpy as jnp

    def _L0_gnn_ref(graph_node_features, edge_index, W, att_src, att_dst, bias):
        import jax, jax.numpy as jnp
        import numpy as np
        NEG_SLOPE = 0.2
        N_NODES = 12500
        N_EDGES = 200000
        IN_CH = 256
        HEADS = 4
        OUT_CH = 64
        x = graph_node_features
        N = x.shape[0]
        H, C = att_src.shape
        x_lin = (x @ W).reshape(N, H, C)
        a_src = jnp.einsum('nhc,hc->nh', x_lin, att_src)
        a_dst = jnp.einsum('nhc,hc->nh', x_lin, att_dst)
        loop = jnp.arange(N, dtype=edge_index.dtype)
        src = jnp.concatenate([edge_index[0], loop])
        dst = jnp.concatenate([edge_index[1], loop])
        alpha = jax.nn.leaky_relu(a_src[src] + a_dst[dst], NEG_SLOPE)
        amax = jax.ops.segment_max(alpha, dst, num_segments=N)
        amax = jnp.where(jnp.isfinite(amax), amax, 0.0)
        ex = jnp.exp(alpha - amax[dst])
        denom = jax.ops.segment_sum(ex, dst, num_segments=N)
        alpha_n = ex / (denom[dst] + 1e-16)
        msg = x_lin[src] * alpha_n[:, :, None]
        out = jax.ops.segment_sum(msg, dst, num_segments=N)
        return out.reshape(N, H * C) + bias

    def _L1_gnn_ref(h, edge_index, W1, b1, W2, b2, eps, gamma, beta):
        import jax, jax.numpy as jnp
        import numpy as np
        N_NODES = 12500
        N_EDGES = 37500
        DIM = 256
        LN_EPS = 1e-05
        src, dst = (edge_index[0], edge_index[1])
        agg = jax.ops.segment_sum(h[src], dst, num_segments=h.shape[0])
        z = (1.0 + eps) * h + agg
        z = jax.nn.relu(z @ W1 + b1) @ W2 + b2
        r = z + h
        mu = jnp.mean(r, axis=-1, keepdims=True)
        var = jnp.mean(jnp.square(r - mu), axis=-1, keepdims=True)
        ln = (r - mu) * jax.lax.rsqrt(var + LN_EPS) * gamma + beta
        return jax.nn.relu(ln)

    def _L2_gnn_ref(x, edge_index, W1, att_src1, att_dst1, b1, W2, att_src2, att_dst2, b2):
        import jax, jax.numpy as jnp
        import numpy as np
        N, E = (6250, 100000)
        H, C_IN, C_HID, C_OUT = (4, 256, 64, 64)
        NEG_SLOPE = 0.2

        def leaky_relu(x, s=NEG_SLOPE):
            return jnp.where(x >= 0, x, s * x)

        def gat_conv(x, src, dst, W, att_src, att_dst, bias, n_nodes):
            Hh, Cc = (att_src.shape[1], att_src.shape[2])
            h = (x @ W).reshape(n_nodes, Hh, Cc)
            a_src = (h * att_src).sum(-1)
            a_dst = (h * att_dst).sum(-1)
            alpha = leaky_relu(a_src[src] + a_dst[dst])
            m = jax.ops.segment_max(alpha, dst, num_segments=n_nodes)
            e = jnp.exp(alpha - m[dst])
            denom = jax.ops.segment_sum(e, dst, num_segments=n_nodes)
            w = e / jnp.clip(denom, 1e-16)[dst]
            out = jax.ops.segment_sum(w[:, :, None] * h[src], dst, num_segments=n_nodes)
            return out.reshape(n_nodes, Hh * Cc) + bias
        n = x.shape[0]
        loops = jnp.arange(n, dtype=edge_index.dtype)
        src = jnp.concatenate([edge_index[0], loops])
        dst = jnp.concatenate([edge_index[1], loops])
        h1 = gat_conv(x, src, dst, W1, att_src1, att_dst1, b1, n)
        h1 = jax.nn.relu(h1)
        out = gat_conv(h1, src, dst, W2, att_src2, att_dst2, b2, n)
        return out

    def _L3_gnn_ref(h, weight, norm, src, dst, rel_type):
        import jax, jax.numpy as jnp
        import numpy as np
        N_NODES = 2500
        N_EDGES = 40000
        NUM_RELS = 16
        IN_FEAT = 256
        OUT_FEAT = 256
        transformed = jnp.einsum('ni,rio->rno', h, weight)
        msg = transformed[rel_type, src] * norm
        out = jax.ops.segment_sum(msg, dst, num_segments=h.shape[0])
        return out
    edge_index = jnp.stack([src, dst])
    x = _layernorm(x + _L0_gnn_ref(x, edge_index, L0_gnn_W, L0_gnn_att_src, L0_gnn_att_dst, L0_gnn_bias), axis=-1)
    x = _layernorm(x + _L1_gnn_ref(x, edge_index, L1_gnn_W1, L1_gnn_b1, L1_gnn_W2, L1_gnn_b2, L1_gnn_eps, L1_gnn_gamma, L1_gnn_beta), axis=-1)
    x = _layernorm(x + _L2_gnn_ref(x, edge_index, L2_gnn_W1, L2_gnn_att_src1, L2_gnn_att_dst1, L2_gnn_b1, L2_gnn_W2, L2_gnn_att_src2, L2_gnn_att_dst2, L2_gnn_b2), axis=-1)
    x = _layernorm(x + _L3_gnn_ref(x, L3_gnn_weight, edge_weight1, src, dst, edge_type_16), axis=-1)
    return x

_drawn_inputs = setup_inputs


def setup_inputs(seed=0):
    import zlib

    import numpy as np

    out = dict(_drawn_inputs(seed))
    spreads = {'L0_gnn_bias': (0.0, 0.1),
     'L1_gnn_b1': (0.0, 0.702),
     'L1_gnn_b2': (0.0, 0.41),
     'L1_gnn_gamma': (1.0, 0.2),
     'L1_gnn_beta': (0.0, 0.1),
     'L2_gnn_b1': (0.0, 0.1),
     'L2_gnn_b2': (0.0, 0.1)}
    factors = {'L2_gnn_att_dst1': 3.524, 'L2_gnn_att_src2': 4.429, 'L2_gnn_att_dst2': 8.0}
    for name, (base, spread) in spreads.items():
        noise = np.random.default_rng([zlib.crc32(name.encode()), seed]).standard_normal(out[name].shape)
        drawn = base * np.exp(spread * noise) if base else spread * noise
        out[name] = jnp.asarray(drawn.astype(out[name].dtype))
    for name, factor in factors.items():
        out[name] = (out[name] * factor).astype(out[name].dtype)
    return out
```

```python
from contextlib import ExitStack

import concourse.bass as bass
from concourse import mybir

FP32 = mybir.dt.float32
BF16 = mybir.dt.bfloat16
I32 = mybir.dt.int32
U32 = mybir.dt.uint32
ALU = mybir.AluOpType
ACT = mybir.ActivationFunctionType
AX = mybir.AxisListType
ENG = mybir.EngineType

P = 128
NODES, EDGES, DIM = 6250, 106250, 256
HEADS, CH = 4, 64
RELS = 16
BLOCKS = -(-NODES // P)
LAST = NODES - (BLOCKS - 1) * P
PADN = BLOCKS * P
TILES = -(-EDGES // P)
TAIL = EDGES - (TILES - 1) * P
STEPS = TILES + BLOCKS - 1
K = 8
BATCHES = -(-STEPS // K)
STEPP = BATCHES * K
CHUNKS = -(-STEPP // P)
CPAD = CHUNKS * P
SLOTS = 4
HC = CH + 3
ROW = HEADS * HC
AC = CH + 2
GROUP = 7
GROUPS = BLOCKS // GROUP
BIG = 1.0e30
NOWHERE = 1 << 20
LN_EPS = 1e-5
SLOPE = 0.2
SKIP = "block numbers are counts of 48 comparisons, so 0..48"


def flat(ap):
    return ap.rearrange("p a b -> p (a b)")


class Memory(ExitStack):

    def __init__(self, nc):
        super().__init__()
        self.nc = nc

    def sb(self, name, shape, dtype):
        return self.enter_context(self.nc.sbuf_tensor(f"sb_{name}", shape, dtype))

    def ps(self, name, shape):
        return self.enter_context(self.nc.psum_tensor(f"ps_{name}", shape, FP32))


class Own:

    def __init__(self, sem, base=0):
        self.sem, self.n, self.base = sem, 0, base

    def inc(self, ins):
        self.n += 1
        ins.then_inc(self.sem, 1)
        return self.base + self.n

    def step(self, eng, ins):
        eng.wait_ge(self.sem, self.inc(ins))


def lay_out_walk(nc, sem, g, src, dst, etype, weight):
    W = 3 * P + 1
    tab = nc.dram_tensor("edge_table", [TILES + 1, W], I32).ap()
    wtab = nc.dram_tensor("weight_table", [TILES + 1, P], FP32).ap()
    full = (TILES - 1) * P
    with Memory(nc) as sb:
        fill_i = sb.sb("w_fill_i", [1, 4 * P], I32)
        fill_f = sb.sb("w_fill_f", [1, 2 * P], FP32)
        first_i = sb.sb("w_first_i", [1, TILES], I32)
        first_f = sb.sb("w_first_f", [1, TILES], FP32)
        ones = sb.sb("w_ones", [P, P], FP32)
        thr = sb.sb("w_thr", [P, 1], FP32)
        pid = sb.sb("w_pid", [P, 1], FP32)
        cmp = sb.sb("w_cmp", [P, TILES], FP32)
        cnt = sb.sb("w_cnt", [P, 4], FP32)
        sidx = sb.sb("w_sidx", [P, CPAD + 1], FP32)
        ind = sb.sb("w_ind", [P, CPAD + 1], FP32)
        bcol = sb.sb("w_bcol", [P, 2 * CHUNKS], FP32)
        newt = sb.sb("w_newt", [P, CHUNKS], FP32)
        sid = sb.sb("w_sid", [P, CHUNKS], FP32)
        tid_f = sb.sb("w_tid_f", [P, CHUNKS], FP32)
        tid = sb.sb("w_tid", [P, CHUNKS], U32)
        rowi = sb.sb("w_rowi", [P, CHUNKS, W], I32)
        roww = sb.sb("w_roww", [P, CHUNKS, P], FP32)
        room = flat(g.X[:, :, :])
        arr = room[:, 0:7 * CPAD].rearrange("p (a c e) -> p a c e", a=7, c=CHUNKS)
        rowf = room[:, 7 * CPAD:7 * CPAD + CHUNKS * W].rearrange("p (c e) -> p c e", c=CHUNKS)
        mrow = sb.sb("w_mrow", [P, CHUNKS, P + 1], FP32)
        dlb = sb.sb("w_dlb", [P, CHUNKS, P], BF16)
        small = sb.sb("w_small", [P, 3, CHUNKS], FP32)
        p_first = sb.ps("w_p_first", [P, 1024])
        p_bcol = sb.ps("w_p_bcol", [P, 512])
        p_brow = sb.ps("w_p_brow", [1, 1024])
        p_tr = sb.ps("w_p_tr", [P, 2, 512])
        filled, first_in, const = sem("w_filled"), sem("w_first_in"), sem("w_const")
        tabbed, first_bc, starts = sem("w_tabbed"), sem("w_first_bc"), sem("w_starts")
        bdone, tids, rows_in = sem("w_bdone"), sem("w_tids"), sem("w_rows_in")
        own, marked, turned = sem("w_own"), sem("w_marked"), sem("w_turned")
        saved, stored = sem("w_saved"), sem("w_stored")
        NARR = 7
        with nc.Block() as block:

            @block.gpsimd
            def _(pool):
                pool.memset(fill_i[:, 0:2 * P], 0).then_inc(filled, 1)
                pool.memset(fill_i[:, 2 * P:4 * P], NOWHERE).then_inc(filled, 1)
                pool.memset(fill_f[:, :], 0.0).then_inc(filled, 1)
                pool.memset(ones[:, :], 1.0).then_inc(const, 1)
                pool.iota(thr[:, :], [[0, 1]], base=P, channel_multiplier=P,
                          allow_small_or_imprecise_dtypes=True).then_inc(const, 1)
                pool.iota(pid[:, :], [[0, 1]], base=0, channel_multiplier=1,
                          allow_small_or_imprecise_dtypes=True).then_inc(const, 1)
                pool.iota(sidx[:, :], [[1, CPAD + 1]], base=-1, channel_multiplier=0,
                          allow_small_or_imprecise_dtypes=True).then_inc(const, 1)
                pool.iota(sid[:, :], [[P, CHUNKS]], base=0, channel_multiplier=1,
                          allow_small_or_imprecise_dtypes=True).then_inc(const, 1)
                pool.iota(g.iota_f[:, :], [[1, P]], base=0, channel_multiplier=0,
                          allow_small_or_imprecise_dtypes=True).then_inc(const, 1)
                pool.iota(g.iota_p[:, :], [[0, 1]], base=0, channel_multiplier=1,
                          allow_small_or_imprecise_dtypes=True).then_inc(const, 1)
                pool.memset(g.ones32[:, :], 1.0).then_inc(const, 1)
                pool.memset(g.ident[:, :], 0.0).then_inc(const, 1)
                pool.wait_ge(const, 9)
                pool.affine_select(out=g.ident[:, :], in_=g.ident[:, :], compare_op=ALU.not_equal,
                                   fill=1.0, base=0, pattern=[[-1, P]], channel_multiplier=1)\
                    .then_inc(const, 1)
                pool.wait_ge(tids, 1)
                pool.wait_ge(tabbed, 16 * 17)
                for c in range(CHUNKS):
                    off = bass.IndirectOffsetOnAxis(ap=tid[:, c:c + 1], axis=0)
                    pool.indirect_dma_start(out=rowi[:, c, :], out_offset=None, in_=tab,
                                            in_offset=off).then_inc(rows_in, 16)
                    pool.indirect_dma_start(out=roww[:, c, :], out_offset=None, in_=wtab,
                                            in_offset=off).then_inc(rows_in, 16)
                pool.wait_ge(rows_in, 32 * CHUNKS)

            @block.sync
            def _(sp):
                sp.dma_start(first_i[:, :], dst.rearrange("(a n) -> a n", a=1)[:, 0:EDGES:P],
                             allow_slow_non_contiguous=True)\
                    .then_inc(first_in, 16)
                for at, a in ((0, src), (P, etype), (2 * P + 1, dst)):
                    sp.dma_start(tab[0:TILES - 1, at:at + P],
                                 a[0:full].rearrange("(t e) -> t e", e=P)).then_inc(tabbed, 16)
                    sp.dma_start(tab[TILES - 1:TILES, at:at + TAIL],
                                 a[full:EDGES].rearrange("(t e) -> t e", t=1)).then_inc(tabbed, 16)
                sp.dma_start(tab[1:TILES, 2 * P:2 * P + 1],
                             dst[P - 1:full].rearrange("(t e) -> t e", e=1)[0:full - P + 1:P, :],
                             allow_slow_non_contiguous=True)\
                    .then_inc(tabbed, 16)
                sp.dma_start(wtab[0:TILES - 1, :],
                             weight[0:full, 0].rearrange("(t e) -> t e", e=P)).then_inc(tabbed, 16)
                sp.dma_start(wtab[TILES - 1:TILES, 0:TAIL],
                             weight[full:EDGES, 0].rearrange("(t e) -> t e", t=1))\
                    .then_inc(tabbed, 16)
                sp.wait_ge(filled, 3)
                sp.dma_start(tab[TILES - 1:TILES, TAIL:P], fill_i[:, 0:P - TAIL]).then_inc(tabbed, 16)
                sp.dma_start(tab[TILES - 1:TILES, P + TAIL:2 * P], fill_i[:, 0:P - TAIL])\
                    .then_inc(tabbed, 16)
                sp.dma_start(tab[TILES - 1:TILES, 2 * P + 1 + TAIL:W],
                             fill_i[:, 2 * P:3 * P - TAIL]).then_inc(tabbed, 16)
                sp.dma_start(wtab[TILES - 1:TILES, TAIL:P], fill_f[:, 0:P - TAIL])\
                    .then_inc(tabbed, 16)
                sp.dma_start(tab[TILES:TILES + 1, 0:2 * P], fill_i[:, 0:2 * P]).then_inc(tabbed, 16)
                sp.dma_start(tab[TILES:TILES + 1, 2 * P:W], fill_i[:, 2 * P:3 * P + 1])\
                    .then_inc(tabbed, 16)
                sp.dma_start(tab[0:1, 2 * P:2 * P + 1], fill_i[:, 3 * P + 2:3 * P + 3])\
                    .then_inc(tabbed, 16)
                sp.dma_start(wtab[TILES:TILES + 1, :], fill_f[:, P:2 * P]).then_inc(tabbed, 16)
                sp.wait_ge(marked, 1)
                for h in range(HEADS):
                    sp.dma_start(g.marks[:, h, :].rearrange("(c p) e -> p c e", p=P), mrow[:, :, :])\
                        .then_inc(stored, 16)
                sp.dma_start(g.places.rearrange("(c p) e -> p c e", p=P), dlb[:, :, :])\
                    .then_inc(stored, 16)
                sp.wait_ge(stored, 16 * (HEADS + 1))

            @block.tensor
            def _(pe):
                pe.wait_ge(const, 1)
                pe.wait_ge(own, 1)
                for a in range(0, TILES, 512):
                    z = min(a + 512, TILES)
                    last = nc.tensor.matmul(p_first[:, a:z], ones[0:1, :], first_f[0:1, a:z],
                                            start=True, stop=True)
                last.then_inc(first_bc, 1)
                pe.wait_ge(starts, 1)
                for c in range(CHUNKS):
                    for late in (0, 1):
                        nc.tensor.matmul(p_bcol[:, 2 * c + late:2 * c + late + 1],
                                         ind[0:BLOCKS - 1, c * P + late:(c + 1) * P + late],
                                         ones[0:BLOCKS - 1, 0:1], start=True, stop=True)
                for a in range(0, STEPP, 512):
                    z = min(a + 512, STEPP)
                    last = nc.tensor.matmul(p_brow[0:1, a:z], ones[0:BLOCKS - 1, 0:1],
                                            ind[0:BLOCKS - 1, a + 1:z + 1], start=True, stop=True)
                last.then_inc(bdone, 1)
                pe.wait_ge(marked, 1)
                pe.wait_ge(const, 10)
                n = 0
                for a in range(NARR):
                    for c in range(CHUNKS):
                        if n >= 2:
                            pe.wait_ge(saved, n - 1)
                        nc.tensor.transpose(p_tr[:, n % 2, 0:P], arr[:, a, c, :], g.ident[:, :])\
                            .then_inc(turned, 1)
                        n += 1

            @block.scalar
            def _(act):
                n = 0
                for a in range(NARR):
                    out = (g.rows, g.rel_rows, g.place, g.edge_w, g.follows, g.starts, g.opens)[a]
                    for c in range(CHUNKS):
                        z = min((c + 1) * P, STEPP)
                        n += 1
                        act.wait_ge(turned, n)
                        act.activation(out[:, c * P:z], p_tr[:, (n - 1) % 2, 0:z - c * P],
                                       ACT.Copy).then_inc(saved, 1)

            @block.vector
            def _(dve):
                w = Own(own)
                dve.wait_ge(first_in, 16)
                w.step(dve, dve.tensor_copy(first_f[:, :], first_i[:, :]))
                dve.wait_ge(const, 8)
                dve.wait_ge(first_bc, 1)
                for n, a in enumerate(range(0, TILES, 512)):
                    z = min(a + 512, TILES)
                    w.step(dve, dve.tensor_scalar(cmp[:, a:z], p_first[:, a:z], thr[:, 0:1], None,
                                                  ALU.is_lt, ALU.add, accum_out=cnt[:, n:n + 1]))
                w.step(dve, dve.tensor_tensor(cnt[:, 0:1], cnt[:, 0:1], cnt[:, 1:2], ALU.add))
                w.step(dve, dve.tensor_scalar(cnt[:, 2:3], cnt[:, 0:1], 1.0, pid[:, 0:1],
                                              ALU.max, ALU.add))
                dve.tensor_scalar(ind[:, :], sidx[:, :], cnt[:, 2:3], None, ALU.is_ge)\
                    .then_inc(starts, 1)
                dve.wait_ge(bdone, 1)
                w.step(dve, dve.tensor_copy(bcol[:, :], p_bcol[:, 0:2 * CHUNKS]))
                w.step(dve, dve.tensor_copy(g.block_of[0:1, :], p_brow[0:1, 0:STEPP]))
                b = bcol[:, :].rearrange("p (c l) -> p c l", l=2)
                w.step(dve, dve.tensor_tensor(tid_f[:, :], sid[:, :], b[:, :, 1], ALU.subtract))
                w.step(dve, dve.tensor_scalar(tid_f[:, :], tid_f[:, :], float(TILES), None, ALU.min))
                dve.tensor_copy(tid[:, :], tid_f[:, :]).then_inc(tids, 1)
                w.step(dve, dve.tensor_tensor(newt[:, :], b[:, :, 0], b[:, :, 1], ALU.is_equal))
                dve.wait_ge(rows_in, 32 * CHUNKS)
                w.step(dve, dve.tensor_copy(rowf[:, :, :], rowi[:, :, :]))
                srcs, types = rowf[:, :, 0:P], rowf[:, :, P:2 * P]
                prev, dsts = rowf[:, :, 2 * P:3 * P], rowf[:, :, 2 * P + 1:W]
                first = rowf[:, :, 2 * P + 1:2 * P + 2]
                rows_a, rel_a, place_a, w_a, foll_a, st_a, op_a = (arr[:, a] for a in range(NARR))
                cont, one, gate = small[:, 0], small[:, 1], small[:, 2]
                w.step(dve, dve.tensor_tensor(cont, rowf[:, :, 2 * P], rowf[:, :, 2 * P + 1],
                                              ALU.is_equal))
                w.step(dve, dve.tensor_tensor(cont, cont, newt[:, :], ALU.mult))
                w.step(dve, dve.tensor_tensor(one, rowf[:, :, 2 * P + 1], rowf[:, :, W - 1],
                                              ALU.is_equal))
                w.step(dve, dve.tensor_tensor(one, one, cont, ALU.mult))
                w.step(dve, dve.tensor_scalar(gate, one, BIG, -BIG, ALU.mult, ALU.add))
                w.step(dve, dve.tensor_copy(rows_a, srcs))
                w.step(dve, dve.scalar_tensor_tensor(out=rel_a, in0=types, scalar=float(PADN),
                                                     in1=srcs, op0=ALU.mult, op1=ALU.add))
                w.step(dve, dve.tensor_scalar(tid_f[:, :], b[:, :, 1], -float(P), None, ALU.mult))
                for c in range(CHUNKS):
                    w.step(dve, dve.tensor_scalar(place_a[:, c, :], dsts[:, c, :], tid_f[:, c:c + 1],
                                                  None, ALU.add))
                w.step(dve, dve.tensor_copy(w_a, roww[:, :, :]))
                w.step(dve, dve.tensor_scalar(dlb[:, :, :], place_a, -1.0, float(P), ALU.max, ALU.min))
                w.step(dve, dve.tensor_tensor(st_a, dsts, prev, ALU.not_equal))
                w.step(dve, dve.memset(mrow[:, :, P:P + 1], 0.0))
                w.step(dve, dve.tensor_scalar(mrow[:, :, 0:P], st_a, -BIG, None, ALU.mult))
                for c in range(CHUNKS):
                    w.step(dve, dve.tensor_scalar(foll_a[:, c, :], dsts[:, c, :], first[:, c, :],
                                                  cont[:, c:c + 1], ALU.is_equal, ALU.mult))
                w.step(dve, dve.tensor_scalar(foll_a, foll_a, BIG, -BIG, ALU.mult, ALU.add))
                w.step(dve, dve.memset(op_a, 0.0))
                w.step(dve, dve.tensor_copy(op_a[:, :, 0], cont))
                w.step(dve, dve.tensor_copy(g.gate_col[:, :], gate))
                dve.drain().then_inc(marked, 1)
        gd, gt, gs = sem("w_gate_diag"), sem("w_gate_turned"), sem("w_gate_saved")
        with nc.Block() as block:

            @block.vector
            def _(dve):
                for c in range(CHUNKS):
                    z = min((c + 1) * P, STEPP)
                    if c:
                        dve.wait_ge(gs, c)
                    dve.tensor_scalar(cmp[:, 0:P], g.ident[:, :], g.gate_col[:, c:c + 1], None,
                                      ALU.mult).then_inc(gd, 1)
                    dve.wait_ge(gt, c + 1)
                    dve.tensor_copy(g.gate[:, c * P:z], p_first[:, 0:z - c * P]).then_inc(gs, 1)

            @block.tensor
            def _(pe):
                for c in range(CHUNKS):
                    pe.wait_ge(gd, c + 1)
                    nc.tensor.matmul(p_first[:, 0:P], ones[:, :], cmp[:, 0:P], start=True,
                                     stop=True).then_inc(gt, 1)


def load_nodes(nc, sem, g, x):
    cleared, loaded = sem("x_cleared"), sem("x_loaded")
    with nc.Block() as block:

        @block.vector
        def _(dve):
            dve.memset(g.X[:, BLOCKS - 1, :], 0.0).then_inc(cleared, 1)

        @block.sync
        def _(sp):
            full = (BLOCKS - 1) * P
            sp.dma_start(g.X[:, 0:BLOCKS - 1, :], x[0:full, :].rearrange("(b p) d -> p b d", p=P))\
                .then_inc(loaded, 16)
            sp.wait_ge(cleared, 1)
            sp.dma_start(g.X[0:LAST, BLOCKS - 1, :], x[full:NODES, :]).then_inc(loaded, 16)
            sp.wait_ge(loaded, 32)


FROM = 1


def free_at(c, k):
    return c * GROUP + (max(k - 1, 0) + FROM)


def through(c, k):
    return c * GROUP + (k + 1 + FROM)


def project(nc, sem, g, tag, y, W, att_src, att_dst):
    with Memory(nc) as sb:
        w_sb = sb.sb(f"{tag}_w", [P, 2, DIM], FP32)
        wx = sb.sb(f"{tag}_wx", [P, 2, DIM + 2 * HEADS], FP32)
        att = sb.sb(f"{tag}_att", [P, 2, DIM], FP32)
        prod = sb.sb(f"{tag}_prod", [P, 2, DIM], FP32)
        yT = sb.sb(f"{tag}_yt", [P, 2, DIM], FP32)
        y_in = sb.sb(f"{tag}_y_in", [P, GROUP, DIM], FP32)
        rows = sb.sb(f"{tag}_rows", [P, GROUP, ROW], FP32)
        v = sb.sb(f"{tag}_v", [P, BLOCKS, 2 * HEADS], FP32)
        rest = sb.sb(f"{tag}_rest", [P, BLOCKS, 2 * HEADS], FP32)
        p_t = sb.ps(f"{tag}_pt", [P, 2, 512])
        p_y = sb.ps(f"{tag}_py", [P, 2, 512])
        loaded, ready, own = sem(f"{tag}_loaded"), sem(f"{tag}_ready"), sem(f"{tag}_own")
        turned, copied = sem(f"{tag}_turned"), sem(f"{tag}_copied")
        mult, evac, put = sem(f"{tag}_mult"), sem(f"{tag}_evac"), sem(f"{tag}_put")
        vsaved, rows_free = sem(f"{tag}_vsaved"), sem(f"{tag}_rows_free")
        PARTS = ((0, GROUP // 2 + 1), (GROUP // 2 + 1, GROUP))
        y_ok = [sem(f"{tag}_y_ok{i}") for i in range(2)]
        H65 = CH + 1
        with nc.Block() as block:

            @block.gpsimd
            def _(pool):
                for s in (turned, copied, mult, evac, vsaved, rows_free):
                    pool.sem_inc(s, FROM)
                with pool.Fori(0, GROUPS) as c:
                    pool.wait_ge(put, c * 16 + 16)
                    pool.sem_inc(rows_free, 1)

            @block.sync
            def _(sp):
                sp.dma_start(w_sb[:, :, :], W.rearrange("(k p) n -> p k n", p=P)).then_inc(loaded, 16)
                for i, a in enumerate((att_src, att_dst)):
                    sp.dma_start(att[:, i, :], a.partition_broadcast(P)).then_inc(loaded, 16)
                with sp.Fori(0, GROUPS) as c:
                    for i, (a, z) in enumerate(PARTS):
                        sp.wait_ge(turned, c * GROUP + FROM)
                        sp.dma_start(y_in[:, a:z, :], y[:, bass.ds(c * GROUP + a, z - a), 0:DIM])\
                            .then_inc(y_ok[i], 16)
                    sp.wait_ge(evac, through(c, GROUP - 1))
                    sp.dma_start(g.table[bass.ds(c * (GROUP * P), GROUP * P), :]
                                 .rearrange("(b p) r -> p b r", p=P), rows[:, :, :])\
                        .then_inc(put, 16)
                sp.wait_ge(put, 16 * GROUPS)

            @block.tensor
            def _(pe):
                pe.wait_ge(ready, 1)
                with pe.Fori(0, GROUPS) as c:
                    for k in range(GROUP + 1):
                        if k < GROUP:
                            for i, (a, z) in enumerate(PARTS):
                                if k == a:
                                    pe.wait_ge(y_ok[i], c * 16 + 16)
                            pe.wait_ge(copied, free_at(c, k))
                            for i in range(2):
                                last = nc.tensor.transpose(p_t[:, k % 2, i * P:(i + 1) * P],
                                                           y_in[:, k, i * P:(i + 1) * P],
                                                           g.ident[:, :])
                            last.then_inc(turned, 1)
                        if k:
                            pe.wait_ge(copied, through(c, k - 1))
                            pe.wait_ge(vsaved, free_at(c, k - 1))
                            for i in range(2):
                                last = nc.tensor.matmul(p_y[:, (k - 1) % 2, 0:DIM + 2 * HEADS],
                                                        yT[:, (k - 1) % 2, i * P:(i + 1) * P],
                                                        wx[:, i, :], start=(i == 0), stop=(i == 1))
                            last.then_inc(mult, 1)

            @block.scalar
            def _(act):
                act.wait_ge(ready, 1)
                with act.Fori(0, GROUPS) as c:
                    for k in range(GROUP + 1):
                        if k < GROUP:
                            act.wait_ge(turned, through(c, k))
                            act.wait_ge(mult, free_at(c, k))
                            act.activation(yT[:, k % 2, :], p_t[:, k % 2, 0:DIM], ACT.Copy)\
                                .then_inc(copied, 1)
                        if k:
                            if k == 1:
                                act.wait_ge(rows_free, c + FROM)
                            act.wait_ge(mult, through(c, k - 1))
                            act.activation(
                                rows[:, k - 1, :].rearrange("p (h r) -> p h r", h=HEADS)[:, :, 0:H65],
                                p_y[:, (k - 1) % 2, 0:HEADS * H65]
                                .rearrange("p (h r) -> p h r", h=HEADS), ACT.Copy).then_inc(evac, 1)

            @block.vector
            def _(dve):
                w = Own(own)
                r = rows[:, :, :].rearrange("p b (h r) -> p (b h) r", h=HEADS)
                w.step(dve, dve.memset(r[:, :, CH + 1:CH + 2], 1.0))
                w.step(dve, dve.memset(r[:, :, CH + 2:CH + 3], 0.0))
                dve.wait_ge(loaded, 48)
                for k in range(2):
                    w.step(dve, dve.tensor_copy(
                        wx[:, k, 0:HEADS * H65].rearrange("p (h r) -> p h r", h=HEADS)[:, :, 1:H65],
                        w_sb[:, k, :].rearrange("p (h r) -> p h r", h=HEADS)))
                for i in range(2):
                    for k in range(2):
                        w.step(dve, dve.tensor_tensor(prod[:, k, :], w_sb[:, k, :], att[:, i, :],
                                                      ALU.mult))
                        out = (wx[:, k, 0:HEADS * H65:H65], wx[:, k, HEADS * H65:])[i]
                        w.step(dve, dve.tensor_reduce(
                            out, prod[:, k, :].rearrange("p (h r) -> p h r", h=HEADS), AX.X, ALU.add))
                dve.drain().then_inc(ready, 1)
                with dve.Fori(0, GROUPS) as c:
                    for k in range(GROUP):
                        dve.wait_ge(evac, through(c, k))
                        at = bass.ds(c * GROUP + k, 1)
                        dve.tensor_copy(v[:, at, 0:HEADS].rearrange("p a b -> p (a b)"),
                                        p_y[:, k % 2, 0:HEADS * H65:H65])
                        dve.tensor_copy(v[:, at, HEADS:].rearrange("p a b -> p (a b)"),
                                        p_y[:, k % 2, HEADS * H65:HEADS * H65 + HEADS])\
                            .then_inc(vsaved, 1)
                dve.wait_ge(vsaved, BLOCKS + FROM)
                sc = g.scores[:, :, :, :]
                w.step(dve, dve.tensor_copy(sc[:, :, 0, :], v[:, :, :]))
                w.step(dve, dve.tensor_tensor(rest[:, :, :], v[:, :, :], sc[:, :, 0, :], ALU.subtract))
                w.step(dve, dve.tensor_copy(sc[:, :, 1, :], rest[:, :, :]))
                w.step(dve, dve.tensor_tensor(rest[:, :, :], rest[:, :, :], sc[:, :, 1, :],
                                              ALU.subtract))
                w.step(dve, dve.tensor_copy(sc[:, :, 2, :], rest[:, :, :]))


def aggregate_attention(nc, sem, g, tag):
    OHS = 4
    with Memory(nc) as sb:
        G = sb.sb(f"{tag}_rows", [P, SLOTS, K, ROW], FP32)
        idx = sb.sb(f"{tag}_idx", [P, SLOTS, K], U32)
        marks = sb.sb(f"{tag}_marks", [K * HEADS, SLOTS, P + 1], FP32)
        places = sb.sb(f"{tag}_places", [P, SLOTS, K * P], BF16)
        turned01 = sb.sb(f"{tag}_turned01", [P, 2, K * P], BF16)
        onehot = sb.sb(f"{tag}_onehot", [P, OHS, P], FP32)
        D = sb.sb(f"{tag}_node_scores", [P, K, 2 * HEADS], FP32)
        sm = sb.sb(f"{tag}_sm", [P, K, HEADS], FP32)
        fwd = sb.sb(f"{tag}_fwd", [K * HEADS, P], FP32)
        seg = sb.sb(f"{tag}_seg", [K * HEADS, P], FP32)
        diag = sb.sb(f"{tag}_diag", [K * HEADS, K * HEADS], FP32)
        C = sb.sb(f"{tag}_carry", [P, 2, HEADS, K + 1], FP32)
        cap = sb.sb(f"{tag}_cap", [P, K, HEADS], FP32)
        top = sb.sb(f"{tag}_top", [P, K, HEADS], FP32)
        A = sb.sb(f"{tag}_alpha", [P, 4, K, HEADS], FP32)
        A2 = sb.sb(f"{tag}_alpha2", [P, 4, K * HEADS], FP32)
        dif = sb.sb(f"{tag}_dif", [P, 3, K * HEADS], FP32)
        ex = sb.sb(f"{tag}_ex", [P, 2, 3, K * HEADS], FP32)
        scale = sb.sb(f"{tag}_scale", [P, 2, HEADS], FP32)
        p_sum = sb.ps(f"{tag}_psum", [P, OHS, 512])
        p_node = sb.ps(f"{tag}_pnode", [P, 2, 512])
        p_seg = sb.ps(f"{tag}_pseg", [P, 512])
        p_top = sb.ps(f"{tag}_ptop", [P, 512])
        idx_ok = sem(f"{tag}_idx_ok")
        rows_in = [sem(f"{tag}_rows_in{b}") for b in range(SLOTS)]
        marks_in = [sem(f"{tag}_marks_in{b}") for b in range(SLOTS)]
        t01_ok, node_ok, sm_ok = sem(f"{tag}_t01"), sem(f"{tag}_node"), sem(f"{tag}_sm_ok")
        pseg_ok, seg_ok, diag_ok = sem(f"{tag}_pseg"), sem(f"{tag}_seg_ok"), sem(f"{tag}_diag_ok")
        top_ok, dif_ok, ex_ok = sem(f"{tag}_top_ok"), sem(f"{tag}_dif_ok"), sem(f"{tag}_ex_ok")
        extra_ok = sem(f"{tag}_extra_ok")
        weighted = sem(f"{tag}_weighted")
        onehot_ok = sem(f"{tag}_onehot_ok")
        summed = sem(f"{tag}_summed")
        added = sem(f"{tag}_added")
        own, begun = sem(f"{tag}_own"), sem(f"{tag}_begun")
        FREE = SLOTS * K
        NCH, PRE = 25, 18
        LOOPS = (BATCHES - 2) // SLOTS
        assert LOOPS * SLOTS + 2 == BATCHES and SLOTS % 2 == 0

        def all_batches(eng, turn):
            with eng.Fori(0, LOOPS) as i:
                for b in range(SLOTS):
                    turn(i * SLOTS + b, i, b)
            for b in range(2):
                turn(LOOPS * SLOTS + b, LOOPS, b)

        def blocks_of(q, engine):
            at = q * K
            _, vals = nc.values_load_multi_w_load_instructions(
                g.block_of[0:1, bass.ds(at, K)], engines=[engine], min_val=0, max_val=BLOCKS - 1,
                skip_runtime_bounds_check_because=SKIP)
            return vals

        def heads(t):
            return t.rearrange("p (h r) -> p h r", h=HEADS)

        def of_batch(b):
            return G[:, b, :, :].rearrange("p k (h r) -> p k h r", h=HEADS)

        def along(t, n):
            return t.unsqueeze(2).to_broadcast([P, K, n])

        with nc.Block() as block:

            @block.gpsimd
            def _(pool):
                pool.sem_inc(summed, FREE)
                pool.sem_inc(added, OHS)
                pool.memset(idx[:, :, :], 0).then_inc(begun, 1)
                pool.wait_ge(begun, 1)

                def gather(q, i, b):
                    pool.wait_ge(summed, q * K + K)
                    pool.tensor_copy(idx[:, b, :], g.rows[:, bass.ds(q * K, K)]).then_inc(idx_ok, 1)
                    pool.wait_ge(idx_ok, q + 1)
                    pool.sem_inc(begun, 1)
                    for k in range(K):
                        pool.indirect_dma_start(
                            out=G[:, b, k, :], out_offset=None, in_=g.table,
                            in_offset=bass.IndirectOffsetOnAxis(ap=idx[:, b, k:k + 1], axis=0))\
                            .then_inc(rows_in[b], 16)

                all_batches(pool, gather)

            @block.sync
            def _(sp):
                def load(q, i, b):
                    sp.wait_ge(summed, q * K + K)
                    sp.dma_start(marks[:, b, :],
                                 g.marks[bass.ds(q * K, K), :, :].rearrange("k h e -> (k h) e"))\
                        .then_inc(marks_in[b], 16)
                    sp.dma_start(places[:, b, :],
                                 g.places[bass.ds(q * K, K), :].rearrange("k e -> (k e)")
                                 .partition_broadcast(P)).then_inc(marks_in[b], 16)

                all_batches(sp, load)

            @block.tensor
            def _(pe):
                def node_scores(q, b):
                    blk = blocks_of(q, ENG.PE)
                    pe.wait_ge(t01_ok, q + 1)
                    for k in range(K):
                        last = nc.tensor.matmul(
                            p_node[:, b % 2, k * 6 * HEADS:(k + 1) * 6 * HEADS],
                            turned01[:, b % 2, k * P:(k + 1) * P],
                            g.scores[:, bass.ds(blk[k], 1), :, :].rearrange("p a t h -> p (a t h)"),
                            start=True, stop=True)
                    last.then_inc(node_ok, 1)

                def turn_scores(q):
                    pe.wait_ge(sm_ok, q + 1)
                    nc.tensor.transpose(p_seg[0:K * HEADS, 0:P],
                                        sm[:, :, :].rearrange("p k h -> p (k h)"), g.ident[:, :])\
                        .then_inc(pseg_ok, 1)

                def turn_tops(q):
                    pe.wait_ge(diag_ok, q + 1)
                    nc.tensor.matmul(p_top[:, K * HEADS:2 * K * HEADS], g.ones32[:, :], diag[:, :],
                                     start=True, stop=True)
                    nc.tensor.transpose(p_top[:, 0:K * HEADS], seg[:, :],
                                        g.ident[0:K * HEADS, 0:K * HEADS]).then_inc(top_ok, 1)

                def sum_up(q, b, k):
                    pe.wait_ge(onehot_ok, q * K + k + 1)
                    pe.wait_ge(weighted, q * K + k + 1)
                    pe.wait_ge(added, q * K + k + 1)
                    nc.tensor.matmul(p_sum[:, k % OHS, 0:ROW], onehot[:, k % OHS, :], G[:, b, k, :],
                                     start=True, stop=True).then_inc(summed, 1)

                def turn(q, b, more=True):
                    for k in range(K):
                        sum_up(q, b, k)
                        if more and k == 0:
                            node_scores(q + 1, b + 1)
                        if more and k == 2:
                            turn_scores(q + 1)
                        if more and k == 4:
                            turn_tops(q + 1)

                node_scores(0, 0)
                turn_scores(0)
                turn_tops(0)
                with pe.Fori(0, LOOPS) as i:
                    for b in range(SLOTS):
                        turn(i * SLOTS + b, b)
                turn(BATCHES - 2, 0)
                turn(BATCHES - 1, 1, more=False)

            @block.scalar
            def _(act):
                def weigh(q, i, b):
                    act.wait_ge(dif_ok, q + 1)
                    act.activation(ex[:, b % 2, :, :], dif[:, :, :], ACT.Exp).then_inc(ex_ok, 1)
                    act.wait_ge(ex_ok, q + 1)
                    act.wait_ge(extra_ok, q + 1)
                    for k in range(K):
                        for h in range(HEADS):
                            part = G[:, b, k, h * HC + 1:(h + 1) * HC - 1]
                            last = act.activation(part, part, ACT.Copy,
                                                  scale=ex[:, b % 2, 0, k * HEADS + h:k * HEADS + h + 1])
                        last.then_inc(weighted, 1)

                all_batches(act, weigh)

            @block.vector
            def _(dve):
                def compare(q, b):
                    dve.tensor_scalar(turned01[:, b % 2, :], places[:, b, :],
                                      g.iota_p[:, 0:1], None, ALU.is_equal).then_inc(t01_ok, 1)

                def own_scores(q, i, b, w):
                    dve.wait_ge(node_ok, q + 1)
                    w.step(dve, dve.tensor_reduce(
                        D[:, :, :],
                        p_node[:, b % 2, 0:6 * K * HEADS]
                        .rearrange("p (k t h) -> p k h t", k=K, t=3), AX.X, ALU.add))
                    dve.wait_ge(rows_in[b], i * (16 * K) + 16 * K)
                    dve.tensor_tensor(sm[:, :, :], of_batch(b)[:, :, :, 0], D[:, :, 0:HEADS],
                                      ALU.max).then_inc(sm_ok, 1)

                def scans(q, b, w):
                    dve.wait_ge(pseg_ok, q + 1)
                    w.step(dve, dve.tensor_tensor_scan(fwd[:, :], marks[:, b, 0:P],
                                                       p_seg[0:K * HEADS, 0:P], -BIG,
                                                       ALU.add, ALU.max))
                    w.step(dve, dve.tensor_tensor_scan(seg[:, ::-1], marks[:, b, P:0:-1],
                                                       fwd[:, ::-1], -BIG, ALU.add, ALU.max))
                    dve.tensor_scalar(diag[:, :], g.ident[0:K * HEADS, 0:K * HEADS],
                                      seg[:, P - 1:P], None, ALU.mult).then_inc(diag_ok, 1)

                def maxima(q, b, w):
                    cur, old = b % 2, (b + 1) % 2
                    w.step(dve, dve.tensor_copy(C[:, cur, :, 0], C[:, old, :, K]))
                    dve.wait_ge(top_ok, q + 1)
                    for h in range(HEADS):
                        w.inc(dve.tensor_tensor_scan(
                            C[:, cur, h, 1:K + 1], g.gate[:, bass.ds(q * K, K)],
                            p_top[:, K * HEADS + h:2 * K * HEADS:HEADS], C[:, cur, h, 0:1],
                            ALU.add, ALU.max))
                    dve.wait_ge(own, w.base + w.n)
                    before = C[:, cur, :, 0:K].rearrange("p h k -> p k h")
                    w.step(dve, dve.tensor_tensor(
                        cap[:, :, :], along(g.follows[:, bass.ds(q * K, K)], HEADS), before, ALU.add))
                    w.step(dve, dve.tensor_tensor(
                        top[:, :, :], cap[:, :, :],
                        p_top[:, 0:K * HEADS].rearrange("p (k h) -> p k h", h=HEADS), ALU.max))
                    dst = D[:, :, HEADS:]
                    w.inc(dve.tensor_tensor(A[:, 0, :, :], of_batch(b)[:, :, :, 0], dst, ALU.add))
                    w.inc(dve.tensor_tensor(A[:, 1, :, :], before, dst, ALU.add))
                    w.inc(dve.tensor_tensor(A[:, 2, :, :], D[:, :, 0:HEADS], dst, ALU.add))
                    w.step(dve, dve.tensor_tensor(A[:, 3, :, :], top[:, :, :], dst, ALU.add))
                    a = A[:, :, :, :].rearrange("p a k h -> p a (k h)")
                    w.step(dve, dve.scalar_tensor_tensor(out=A2[:, :, :], in0=a, scalar=SLOPE, in1=a,
                                                         op0=ALU.mult, op1=ALU.max))
                    w.step(dve, dve.tensor_tensor(
                        dif[:, :, :], A2[:, 0:3, :],
                        A2[:, 3:4, :].to_broadcast([P, 3, K * HEADS]), ALU.subtract))
                    dve.tensor_scalar(dif[:, :, :], dif[:, :, :], 0.0, None, ALU.min)\
                        .then_inc(dif_ok, 1)

                def extras(q, b, w):
                    dve.wait_ge(ex_ok, q + 1)
                    e = ex[:, b % 2, :, :].rearrange("p a (k h) -> p a k h", h=HEADS)
                    w.step(dve, dve.tensor_tensor(
                        of_batch(b)[:, :, :, 0], e[:, 2], along(g.starts[:, bass.ds(q * K, K)], HEADS),
                        ALU.mult))
                    dve.scalar_tensor_tensor(
                        out=of_batch(b)[:, :, :, HC - 1], in0=e[:, 1], scalar=-1.0,
                        in1=along(g.opens[:, bass.ds(q * K, K)], HEADS), op0=ALU.add, op1=ALU.mult)\
                        .then_inc(extra_ok, 1)

                def make_onehot(q, k):
                    s = q * K + k
                    dve.wait_ge(summed, s + (FREE - OHS + 1))
                    dve.tensor_scalar(onehot[:, k % OHS, :], g.iota_f[:, :],
                                      g.place[:, bass.ds(s, 1)], None, ALU.is_equal)\
                        .then_inc(onehot_ok, 1)

                def add(q, k, blk, w):
                    s = q * K + k
                    dve.wait_ge(summed, s + (FREE + 1))
                    part = heads(p_sum[:, k % OHS, 0:ROW])
                    w.step(dve, dve.tensor_scalar(scale[:, k % 2, :], part[:, :, HC - 1], 1.0, None,
                                                  ALU.add))
                    dve.wait_ge(added, s + OHS)
                    acc = g.sums[:, bass.ds(blk, 1), :].rearrange("p a (h r) -> p (a h) r", h=HEADS)
                    for h in range(HEADS):
                        last = dve.scalar_tensor_tensor(
                            out=acc[:, h, :], in0=acc[:, h, :], scalar=scale[:, k % 2, h:h + 1],
                            in1=part[:, h, 0:AC], op0=ALU.mult, op1=ALU.add)
                    last.then_inc(added, 1)

                def turn(q, i, b, more=True, last=False):
                    w = Own(own, q * NCH + PRE)
                    blk = blocks_of(q, ENG.DVE)
                    for k in range(K):
                        if not (last and k + 2 >= K):
                            make_onehot(q, k + 2)
                        add(q, k, blk[k], w)
                        if more:
                            n, m = (q + 1, (b + 1) % SLOTS)
                            j = i if b + 1 < SLOTS else i + 1
                            if k == 0:
                                dve.wait_ge(marks_in[m], j * 32 + 32)
                                compare(n, m)
                            if k == 1:
                                own_scores(n, j, m, w)
                            if k == 3:
                                scans(n, m, w)
                            if k == 5:
                                maxima(n, m, w)
                            if k == 7:
                                extras(n, m, w)
                    assert w.n == NCH or not more, w.n

                w = Own(own, 0)
                dve.memset(g.sums[:, :, :], 0.0)
                w.step(dve, dve.memset(C[:, 1, :, :], -BIG))
                dve.drain()
                dve.wait_ge(added, OHS)
                dve.wait_ge(marks_in[0], 32)
                compare(0, 0)
                own_scores(0, 0, 0, w)
                scans(0, 0, w)
                maxima(0, 0, w)
                extras(0, 0, w)
                assert w.n == PRE, w.n
                make_onehot(0, 0)
                make_onehot(0, 1)
                with dve.Fori(0, LOOPS) as i:
                    for b in range(SLOTS):
                        turn(i * SLOTS + b, i, b)
                turn(BATCHES - 2, LOOPS, 0)
                turn(BATCHES - 1, LOOPS, 1, more=False, last=True)


def aggregate(nc, sem, g, tag, table, rows, weights):
    OHS = 4
    with Memory(nc) as sb:
        G = sb.sb(f"{tag}_rows", [P, SLOTS, K, DIM], FP32)
        idx = sb.sb(f"{tag}_idx", [P, SLOTS, K], U32)
        onehot = sb.sb(f"{tag}_onehot", [P, OHS, P], FP32)
        p_sum = sb.ps(f"{tag}_psum", [P, OHS, 512])
        idx_ok, begun = sem(f"{tag}_idx_ok"), sem(f"{tag}_begun")
        rows_in = [sem(f"{tag}_rows_in{b}") for b in range(SLOTS)]
        onehot_ok = sem(f"{tag}_onehot_ok")
        summed = sem(f"{tag}_summed")
        added = sem(f"{tag}_added")
        FREE = SLOTS * K
        LOOPS = (BATCHES - 2) // SLOTS

        def all_batches(eng, turn):
            with eng.Fori(0, LOOPS) as i:
                for b in range(SLOTS):
                    turn(i * SLOTS + b, i, b)
            for b in range(2):
                turn(LOOPS * SLOTS + b, LOOPS, b)

        with nc.Block() as block:

            @block.gpsimd
            def _(pool):
                pool.sem_inc(summed, FREE)
                pool.sem_inc(added, OHS)
                pool.memset(idx[:, :, :], 0).then_inc(begun, 1)
                pool.wait_ge(begun, 1)

                def gather(q, i, b):
                    pool.wait_ge(summed, q * K + K)
                    pool.tensor_copy(idx[:, b, :], rows[:, bass.ds(q * K, K)]).then_inc(idx_ok, 1)
                    pool.wait_ge(idx_ok, q + 1)
                    pool.sem_inc(begun, 1)
                    for k in range(K):
                        pool.indirect_dma_start(
                            out=G[:, b, k, :], out_offset=None, in_=table,
                            in_offset=bass.IndirectOffsetOnAxis(ap=idx[:, b, k:k + 1], axis=0))\
                            .then_inc(rows_in[b], 16)

                all_batches(pool, gather)

            @block.tensor
            def _(pe):
                def turn(q, i, b):
                    pe.wait_ge(rows_in[b], i * (16 * K) + 16 * K)
                    for k in range(K):
                        pe.wait_ge(onehot_ok, q * K + k + 1)
                        pe.wait_ge(added, q * K + k + 1)
                        nc.tensor.matmul(p_sum[:, k % OHS, 0:DIM], onehot[:, k % OHS, :],
                                         G[:, b, k, :], start=True, stop=True).then_inc(summed, 1)

                all_batches(pe, turn)

            @block.vector
            def _(dve):
                def make_onehot(q, k):
                    s = q * K + k
                    dve.wait_ge(summed, s + (FREE - OHS + 1))
                    if weights is None:
                        dve.tensor_scalar(onehot[:, k % OHS, :], g.iota_f[:, :],
                                          g.place[:, bass.ds(s, 1)], None, ALU.is_equal)\
                            .then_inc(onehot_ok, 1)
                    else:
                        dve.tensor_scalar(onehot[:, k % OHS, :], g.iota_f[:, :],
                                          g.place[:, bass.ds(s, 1)], weights[:, bass.ds(s, 1)],
                                          ALU.is_equal, ALU.mult).then_inc(onehot_ok, 1)

                def turn(q, i, b, last=False):
                    _, blk = nc.values_load_multi_w_load_instructions(
                        g.block_of[0:1, bass.ds(q * K, K)], engines=[ENG.DVE], min_val=0,
                        max_val=BLOCKS - 1, skip_runtime_bounds_check_because=SKIP)
                    for k in range(K):
                        if not (last and k + 2 >= K):
                            make_onehot(q, k + 2)
                        s = q * K + k
                        dve.wait_ge(summed, s + (FREE + 1))
                        dve.wait_ge(added, s + OHS)
                        acc = flat(g.sums[:, bass.ds(blk[k], 1), 0:DIM])
                        dve.tensor_tensor(acc, acc, p_sum[:, k % OHS, 0:DIM], ALU.add)\
                            .then_inc(added, 1)

                dve.memset(g.sums[:, :, :], 0.0)
                dve.drain()
                dve.wait_ge(added, OHS)
                make_onehot(0, 0)
                make_onehot(0, 1)
                with dve.Fori(0, LOOPS) as i:
                    for b in range(SLOTS):
                        turn(i * SLOTS + b, i, b)
                turn(BATCHES - 2, LOOPS, 0)
                turn(BATCHES - 1, LOOPS, 1, last=True)


class Norm:
    STEPS = 3 * GROUP + 2

    def __init__(self, nc, sem, sb, tag, per_group):
        self.nc, self.per = nc, per_group
        self.stats = sb.sb(f"{tag}_stats", [P, GROUP, 6], FP32)
        self.mv = sb.sb(f"{tag}_mv", [P, GROUP, 2], FP32)
        self.std = sb.sb(f"{tag}_std", [P, GROUP], FP32)
        self.inv = sb.sb(f"{tag}_inv", [P, GROUP], FP32)
        self.shift = sb.sb(f"{tag}_shift", [P, GROUP], FP32)
        self.var_ok, self.std_ok = sem(f"{tag}_var_ok"), sem(f"{tag}_std_ok")
        self.held = sem(f"{tag}_held")

    def vector(self, dve, w, c, n, y):
        dve.sem_inc(self.held, 1)
        for k in range(GROUP):
            w.inc(dve.bn_stats(self.stats[:, k, :], y(k)))
        dve.wait_ge(w.sem, w.base + w.n)
        dve.sem_inc(self.held, 1)
        for k in range(GROUP):
            w.inc(dve.bn_aggr(self.mv[:, k, :], self.stats[:, k, :]))
        dve.wait_ge(w.sem, w.base + w.n)
        dve.tensor_scalar(self.std[:, :], self.mv[:, :, 1], LN_EPS, None, ALU.add)\
            .then_inc(self.var_ok, 1)
        dve.wait_ge(self.std_ok, c * self.per + n + 1)
        w.step(dve, dve.reciprocal(self.inv[:, :], self.std[:, :]))
        w.step(dve, dve.scalar_tensor_tensor(out=self.shift[:, :], in0=self.mv[:, :, 0], scalar=-1.0,
                                             in1=self.inv[:, :], op0=ALU.mult, op1=ALU.mult))
        for k in range(GROUP):
            w.inc(dve.tensor_scalar(y(k), y(k), self.inv[:, k:k + 1], self.shift[:, k:k + 1],
                                    ALU.mult, ALU.add))
        dve.wait_ge(w.sem, w.base + w.n)

    def scalar(self, act, c, n):
        act.wait_ge(self.var_ok, c * self.per + n + 1)
        act.activation(self.std[:, :], self.std[:, :], ACT.Sqrt).then_inc(self.std_ok, 1)


def finish_attention(nc, sem, g, tag, bias, guard, norm, store):
    with Memory(nc) as sb:
        own_rows = sb.sb(f"{tag}_own_rows", [P, GROUP, ROW], FP32)
        T = sb.sb(f"{tag}_t", [P, GROUP, DIM], FP32)
        bias_sb = sb.sb(f"{tag}_bias", [P, DIM], FP32)
        den = sb.sb(f"{tag}_den", [P, GROUP * HEADS], FP32)
        lone = sb.sb(f"{tag}_lone", [P, GROUP * HEADS], FP32)
        self_w = sb.sb(f"{tag}_self_w", [P, GROUP * HEADS], FP32)
        bias_in, rows_in, rows_used = sem(f"{tag}_bias_in"), sem(f"{tag}_rows_in"), sem(f"{tag}_used")
        own, done, stored = sem(f"{tag}_own"), sem(f"{tag}_done"), sem(f"{tag}_stored")
        ln = Norm(nc, sem, sb, tag, 1) if norm else None
        NV = 9 + (Norm.STEPS + 1 if norm else 0)
        with nc.Block() as block:

            @block.gpsimd
            def _(pool):
                pool.sem_inc(rows_used, FROM)

            @block.sync
            def _(sp):
                sp.dma_start(bias_sb[:, :], bias.partition_broadcast(P)).then_inc(bias_in, 16)
                with sp.Fori(0, GROUPS) as c:
                    sp.wait_ge(rows_used, c + FROM)
                    sp.dma_start(own_rows[:, :, :],
                                 g.table[bass.ds(c * (GROUP * P), GROUP * P), :]
                                 .rearrange("(b p) r -> p b r", p=P)).then_inc(rows_in, 16)
                    if store:
                        sp.wait_ge(done, c + 1)
                        sp.dma_start(g.nodes[bass.ds(c * (GROUP * P), GROUP * P), :]
                                     .rearrange("(b p) d -> p b d", p=P),
                                     g.X[:, bass.ds(c * GROUP, GROUP), :]).then_inc(stored, 16)
                if store:
                    sp.wait_ge(stored, 16 * GROUPS)

            if norm:
                @block.scalar
                def _(act):
                    with act.Fori(0, GROUPS) as c:
                        ln.scalar(act, c, 0)

            @block.vector
            def _(dve):
                dve.wait_ge(bias_in, 16)
                with dve.Fori(0, GROUPS) as c:
                    w = Own(own, c * NV)
                    blocks = bass.ds(c * GROUP, GROUP)
                    s = g.sums[:, blocks, :].rearrange("p b (h r) -> p (b h) r", h=HEADS)
                    r = own_rows[:, :, :].rearrange("p b (h r) -> p (b h) r", h=HEADS)
                    t = T[:, :, :].rearrange("p b (h r) -> p (b h) r", h=HEADS)

                    def wide(a):
                        return a[:, :].unsqueeze(2).to_broadcast([P, GROUP * HEADS, CH])

                    w.step(dve, dve.tensor_tensor(den[:, :], s[:, :, CH + 1], s[:, :, 0], ALU.add))
                    w.step(dve, dve.tensor_scalar(lone[:, :], den[:, :], 0.5, None, ALU.is_lt))
                    w.step(dve, dve.tensor_tensor(self_w[:, :], s[:, :, 0], lone[:, :], ALU.add))
                    w.step(dve, dve.tensor_tensor(den[:, :], den[:, :], lone[:, :], ALU.add))
                    w.step(dve, dve.tensor_scalar(den[:, :], den[:, :], 1e-16, None, guard))
                    w.step(dve, dve.reciprocal(den[:, :], den[:, :]))
                    dve.wait_ge(rows_in, c * 16 + 16)
                    dve.tensor_tensor(t, r[:, :, 1:CH + 1], wide(self_w), ALU.mult)\
                        .then_inc(rows_used, 1)
                    dve.wait_ge(rows_used, c + 1 + FROM)
                    w.step(dve, dve.tensor_tensor(t, t, s[:, :, 1:CH + 1], ALU.add))
                    w.step(dve, dve.tensor_tensor(t, t, wide(den), ALU.mult))
                    w.step(dve, dve.tensor_tensor(
                        T[:, :, :], T[:, :, :],
                        bias_sb[:, :].unsqueeze(1).to_broadcast([P, GROUP, DIM]), ALU.add))
                    if not norm:
                        dve.tensor_scalar(g.sums[:, blocks, 0:DIM], T[:, :, :], 0.0, None, ALU.max)\
                            .then_inc(done, 1)
                    else:
                        x = g.X[:, blocks, :]
                        w.step(dve, dve.tensor_tensor(x, x, T[:, :, :], ALU.add))
                        ln.vector(dve, w, c, 0,
                                  lambda k: flat(g.X[:, bass.ds(c * GROUP + k, 1), :]))
                        dve.sem_inc(done, 1)
                    assert w.n == NV, w.n


def perceptron(nc, sem, g, W1, b1, W2, b2, eps, gamma, beta):
    with Memory(nc) as sb:
        w1 = sb.sb("mlp_w1", [P, 2, DIM], FP32)
        w2 = sb.sb("mlp_w2", [P, 2, DIM], FP32)
        b1c = sb.sb("mlp_b1", [P, 2], FP32)
        vec = sb.sb("mlp_vec", [P, 3, DIM], FP32)
        one_eps = sb.sb("mlp_eps", [P, 1], FP32)
        Z = sb.sb("mlp_z", [P, GROUP, DIM], FP32)
        R = sb.sb("mlp_r", [P, GROUP, DIM], FP32)
        zT = sb.sb("mlp_zt", [P, 2, DIM], FP32)
        hT = sb.sb("mlp_ht", [P, 2, DIM], FP32)
        p_t = sb.ps("mlp_pt", [P, 2, 512])
        p_h = sb.ps("mlp_ph", [P, 2, 512])
        p_z = sb.ps("mlp_pz", [P, 2, 512])
        loaded, own = sem("mlp_loaded"), sem("mlp_own")
        z_ok, turned, copied = sem("mlp_z_ok"), sem("mlp_turned"), sem("mlp_copied")
        hid, hid_ok, mult, evac = sem("mlp_hid"), sem("mlp_hid_ok"), sem("mlp_mult"), sem("mlp_evac")
        ln = Norm(nc, sem, sb, "mlp_norm", 2)
        NV = 1 + 2 + 1 + 2 * Norm.STEPS
        with nc.Block() as block:

            @block.gpsimd
            def _(pool):
                for s in (turned, copied, hid, hid_ok, mult, evac):
                    pool.sem_inc(s, FROM)

            @block.sync
            def _(sp):
                sp.dma_start(w1[:, :, :], W1.rearrange("(k p) n -> p k n", p=P)).then_inc(loaded, 16)
                sp.dma_start(w2[:, :, :], W2.rearrange("(k p) n -> p k n", p=P)).then_inc(loaded, 16)
                for i in range(2):
                    sp.dma_start(b1c[:, i:i + 1], b1[i * P:(i + 1) * P].rearrange("(p a) -> p a", a=1))\
                        .then_inc(loaded, 16)
                for i, a in enumerate((b2, gamma, beta)):
                    sp.dma_start(vec[:, i, :], a.partition_broadcast(P)).then_inc(loaded, 16)
                sp.dma_start(one_eps[:, :], eps.partition_broadcast(P)).then_inc(loaded, 16)

            @block.tensor
            def _(pe):
                pe.wait_ge(loaded, 16 * 8)
                with pe.Fori(0, GROUPS) as c:
                    pe.wait_ge(z_ok, c + 1)
                    for k in range(GROUP + 2):
                        if k < GROUP:
                            pe.wait_ge(copied, free_at(c, k))
                            for i in range(2):
                                last = nc.tensor.transpose(p_t[:, k % 2, i * P:(i + 1) * P],
                                                           Z[:, k, i * P:(i + 1) * P], g.ident[:, :])
                            last.then_inc(turned, 1)
                        if 1 <= k <= GROUP:
                            j = k - 1
                            pe.wait_ge(copied, through(c, j))
                            pe.wait_ge(hid_ok, free_at(c, j))
                            for o in range(2):
                                for i in range(2):
                                    last = nc.tensor.matmul(
                                        p_h[:, j % 2, o * P:(o + 1) * P], w1[:, i, o * P:(o + 1) * P],
                                        zT[:, j % 2, i * P:(i + 1) * P],
                                        start=(i == 0), stop=(i == 1))
                            last.then_inc(hid, 1)
                        if k >= 2:
                            j = k - 2
                            pe.wait_ge(hid_ok, through(c, j))
                            pe.wait_ge(evac, free_at(c, j))
                            for i in range(2):
                                last = nc.tensor.matmul(p_z[:, j % 2, 0:DIM],
                                                        hT[:, j % 2, i * P:(i + 1) * P],
                                                        w2[:, i, :], start=(i == 0), stop=(i == 1))
                            last.then_inc(mult, 1)

            @block.scalar
            def _(act):
                act.wait_ge(loaded, 16 * 8)
                with act.Fori(0, GROUPS) as c:
                    for k in range(GROUP + 1):
                        if k < GROUP:
                            act.wait_ge(turned, through(c, k))
                            act.wait_ge(hid, free_at(c, k))
                            act.activation(zT[:, k % 2, :], p_t[:, k % 2, 0:DIM], ACT.Copy)\
                                .then_inc(copied, 1)
                        if k:
                            j = k - 1
                            act.wait_ge(hid, through(c, j))
                            act.wait_ge(mult, free_at(c, j))
                            for o in range(2):
                                last = act.activation(hT[:, j % 2, o * P:(o + 1) * P],
                                                      p_h[:, j % 2, o * P:(o + 1) * P], ACT.Relu,
                                                      bias=b1c[:, o:o + 1])
                            last.then_inc(hid_ok, 1)
                    for n in range(2):
                        ln.scalar(act, c, n)

            @block.vector
            def _(dve):
                dve.wait_ge(loaded, 16 * 8)
                o = Own(own)
                o.step(dve, dve.tensor_scalar(one_eps[:, :], one_eps[:, :], 1.0, None, ALU.add))

                def every(i):
                    return vec[:, i:i + 1, :].to_broadcast([P, GROUP, DIM])

                with dve.Fori(0, GROUPS) as c:
                    w = Own(own, c * NV + 1)
                    blocks = bass.ds(c * GROUP, GROUP)
                    x = g.X[:, blocks, :]
                    dve.scalar_tensor_tensor(out=Z[:, :, :], in0=x, scalar=one_eps[:, 0:1],
                                             in1=g.sums[:, blocks, 0:DIM], op0=ALU.mult,
                                             op1=ALU.add).then_inc(z_ok, 1)
                    w.step(dve, dve.tensor_tensor(R[:, :, :], x, every(0), ALU.add))
                    for k in range(GROUP):
                        dve.wait_ge(mult, through(c, k))
                        dve.tensor_tensor(R[:, k, :], R[:, k, :], p_z[:, k % 2, 0:DIM], ALU.add)\
                            .then_inc(evac, 1)
                    dve.wait_ge(evac, through(c, GROUP - 1))
                    ln.vector(dve, w, c, 0, lambda k: R[:, k, :])
                    w.step(dve, dve.tensor_tensor(R[:, :, :], R[:, :, :], every(1), ALU.mult))
                    w.step(dve, dve.tensor_tensor(R[:, :, :], R[:, :, :], every(2), ALU.add))
                    w.step(dve, dve.scalar_tensor_tensor(out=x, in0=R[:, :, :], scalar=0.0, in1=x,
                                                         op0=ALU.max, op1=ALU.add))
                    ln.vector(dve, w, c, 1, lambda k: flat(g.X[:, bass.ds(c * GROUP + k, 1), :]))
                    assert w.n == NV, w.n


def transform(nc, sem, g, weight):
    PAIR = 2
    with Memory(nc) as sb:
        w3 = sb.sb("rel_w", [P, 2, RELS, DIM], FP32)
        x_in = sb.sb("rel_x_in", [P, 2, DIM], FP32)
        xT = sb.sb("rel_xt", [P, 2, DIM], FP32)
        out = sb.sb("rel_out", [P, RELS, DIM], FP32)
        p_t = sb.ps("rel_pt", [P, 2, 512])
        p_y = sb.ps("rel_py", [P, 4, PAIR * DIM])
        loaded, x_ok = sem("rel_loaded"), [sem("rel_x_ok0"), sem("rel_x_ok1")]
        turned, copied, mult = sem("rel_turned"), sem("rel_copied"), sem("rel_mult")
        by_act, by_dve, put = sem("rel_by_act"), sem("rel_by_dve"), [sem("rel_put0"), sem("rel_put1")]
        out_free = [sem("rel_out_free0"), sem("rel_out_free1")]
        NP2 = RELS // PAIR
        HALF = NP2 // 2
        y = g.by_rel.rearrange("(r n) d -> n r d", n=PADN)
        with nc.Block() as block:

            @block.gpsimd
            def _(pool):
                for s in (by_act, by_dve, *out_free):
                    pool.sem_inc(s, FROM)
                with pool.Fori(0, BLOCKS) as j:
                    for half in range(2):
                        pool.wait_ge(put[half], j * 16 + 16)
                        pool.sem_inc(out_free[half], 1)

            @block.sync
            def _(sp):
                for i in range(2):
                    sp.dma_start(w3[:, i, :, :],
                                 weight[:, i * P:(i + 1) * P, :].rearrange("r p d -> p r d"))\
                        .then_inc(loaded, 16)
                def load_x(j, k):
                    sp.dma_start(x_in[:, k, :], flat(g.X[:, bass.ds(j, 1), :])).then_inc(x_ok[k], 16)

                def store(j):
                    for half in range(2):
                        sp.wait_ge(by_act, j * HALF + (half + 1) * (HALF // 2) + FROM)
                        sp.wait_ge(by_dve, j * HALF + (half + 1) * (HALF // 2) + FROM)
                        r = slice(half * RELS // 2, (half + 1) * RELS // 2)
                        sp.dma_start(y[bass.ds(j * P, P), r, :], out[:, r, :]).then_inc(put[half], 16)

                load_x(0, 0)
                load_x(1, 1)
                with sp.Fori(0, BLOCKS // 2 - 1) as i:
                    for k in range(2):
                        sp.wait_ge(turned, i * 2 + k + 1)
                        load_x(i * 2 + k + 2, k)
                        store(i * 2 + k)
                sp.wait_ge(turned, BLOCKS - 2)
                load_x(BLOCKS - 1, 0)
                for j in range(BLOCKS - 3, BLOCKS):
                    store(j)
                for half in range(2):
                    sp.wait_ge(put[half], 16 * BLOCKS)

            @block.tensor
            def _(pe):
                def turn_over(j, u, k):
                    pe.wait_ge(x_ok[k], u * 16 + 16)
                    for i in range(2):
                        last = nc.tensor.transpose(p_t[:, k, i * P:(i + 1) * P],
                                                   x_in[:, k, i * P:(i + 1) * P], g.ident[:, :])
                    last.then_inc(turned, 1)

                def products(j, i, k, more):
                    pe.wait_ge(copied, j + 1)
                    if more:
                        turn_over(j + 1, i + k, 1 - k)
                    for n in range(NP2):
                        reader = (by_act, by_dve)[n % 2]
                        pe.wait_ge(reader, j * HALF + (max(n // 2 - 1, 0) + FROM))
                        for r in range(PAIR):
                            for f in range(2):
                                last = nc.tensor.matmul(
                                    p_y[:, n % 4, r * DIM:(r + 1) * DIM],
                                    xT[:, k, f * P:(f + 1) * P], w3[:, f, n * PAIR + r, :],
                                    start=(f == 0), stop=(f == 1))
                        last.then_inc(mult, 1)

                pe.wait_ge(loaded, 32)
                turn_over(0, 0, 0)
                with pe.Fori(0, BLOCKS // 2) as i:
                    for k in range(2):
                        products(i * 2 + k, i, k, True)
                products(BLOCKS - 1, BLOCKS // 2, 0, False)

            def read_out(eng, copy, mine, sign, j):
                for n in range(mine, NP2, 2):
                    if n in (mine, mine + 4):
                        eng.wait_ge(out_free[n // 4], j + FROM)
                    eng.wait_ge(mult, j * NP2 + n + 1)
                    copy(out[:, n * PAIR:(n + 1) * PAIR, :].rearrange("p r d -> p (r d)"),
                         p_y[:, n % 4, :]).then_inc(sign, 1)

            @block.scalar
            def _(act):
                def copy(a, b):
                    return act.activation(a, b, ACT.Copy)

                def turn(j, k):
                    act.wait_ge(turned, j + 1)
                    copy(xT[:, k, :], p_t[:, k, 0:DIM]).then_inc(copied, 1)

                turn(0, 0)
                with act.Fori(0, BLOCKS // 2) as i:
                    for k in range(2):
                        turn(i * 2 + k + 1, 1 - k)
                        read_out(act, copy, 0, by_act, i * 2 + k)
                read_out(act, copy, 0, by_act, BLOCKS - 1)

            @block.vector
            def _(dve):
                with dve.Fori(0, BLOCKS) as j:
                    read_out(dve, dve.tensor_copy, 1, by_dve, j)


def last_norm(nc, sem, g, out):
    with Memory(nc) as sb:
        own, done, stored = sem("end_own"), sem("end_done"), sem("end_stored")
        ln = Norm(nc, sem, sb, "end", 1)
        NV = 1 + Norm.STEPS
        with nc.Block() as block:

            @block.sync
            def _(sp):
                with sp.Fori(0, GROUPS - 1) as c:
                    sp.wait_ge(done, c + 1)
                    sp.dma_start(out[bass.ds(c * (GROUP * P), GROUP * P), :]
                                 .rearrange("(b p) d -> p b d", p=P),
                                 g.X[:, bass.ds(c * GROUP, GROUP), :]).then_inc(stored, 16)
                sp.wait_ge(done, GROUPS)
                a, z = (GROUPS - 1) * GROUP, BLOCKS - 1
                sp.dma_start(out[a * P:z * P, :].rearrange("(b p) d -> p b d", p=P), g.X[:, a:z, :])\
                    .then_inc(stored, 16)
                sp.dma_start(out[z * P:NODES, :], g.X[0:LAST, z, :]).then_inc(stored, 16)
                sp.wait_ge(stored, 16 * (GROUPS + 1))

            @block.scalar
            def _(act):
                with act.Fori(0, GROUPS) as c:
                    ln.scalar(act, c, 0)

            @block.vector
            def _(dve):
                with dve.Fori(0, GROUPS) as c:
                    w = Own(own, c * NV)
                    x = g.X[:, bass.ds(c * GROUP, GROUP), :]
                    w.step(dve, dve.tensor_tensor(x, x, g.sums[:, bass.ds(c * GROUP, GROUP), 0:DIM],
                                                  ALU.add))
                    ln.vector(dve, w, c, 0, lambda k: flat(g.X[:, bass.ds(c * GROUP + k, 1), :]))
                    dve.sem_inc(done, 1)
                    assert w.n == NV, w.n


class Kept:

    def __init__(self, nc, sb):
        self.X = sb.sb("x", [P, BLOCKS, DIM], FP32)
        self.sums = sb.sb("sums", [P, BLOCKS, HEADS * AC], FP32)
        self.scores = sb.sb("scores", [P, BLOCKS, 3, 2 * HEADS], BF16)
        self.rows = sb.sb("src_rows", [P, STEPP], U32)
        self.rel_rows = sb.sb("rel_rows", [P, STEPP], U32)
        self.place = sb.sb("place", [P, STEPP], FP32)
        self.edge_w = sb.sb("edge_w", [P, STEPP], FP32)
        self.follows = sb.sb("follows", [P, STEPP], FP32)
        self.starts = sb.sb("starts", [P, STEPP], FP32)
        self.opens = sb.sb("opens", [P, STEPP], FP32)
        self.gate = sb.sb("gate", [P, STEPP], FP32)
        self.gate_col = sb.sb("gate_col", [P, CHUNKS], FP32)
        self.block_of = sb.sb("block_of", [1, STEPP], I32)
        self.iota_f = sb.sb("iota_f", [P, P], FP32)
        self.iota_p = sb.sb("iota_p", [P, 1], FP32)
        self.ident = sb.sb("ident", [P, P], FP32)
        self.ones32 = sb.sb("ones32", [K * HEADS, P], FP32)
        self.table = nc.dram_tensor("gat_rows", [PADN, ROW], FP32).ap()
        self.nodes = nc.dram_tensor("node_rows", [PADN, DIM], FP32).ap()
        self.by_rel = nc.dram_tensor("relation_rows", [RELS * PADN, DIM], FP32).ap()
        self.marks = nc.dram_tensor("segment_marks", [CPAD, HEADS, P + 1], FP32).ap()
        self.places = nc.dram_tensor("places_in_block", [CPAD, P], BF16).ap()


def graph_layers(nc, a, out, stages=99):
    keep = Memory(nc)
    with keep as sb:
        used = []

        def sem(name):
            used.append(nc.alloc_semaphore(name))
            return used[-1]

        g = Kept(nc, sb)
        todo = [
            lambda: lay_out_walk(nc, sem, g, a["src"], a["dst"], a["edge_type_16"],
                                 a["edge_weight1"]),
            lambda: load_nodes(nc, sem, g, a["x"]),
            lambda: project(nc, sem, g, "p0", g.X, a["L0_gnn_W"], a["L0_gnn_att_src"]
                            .rearrange("h c -> (h c)"), a["L0_gnn_att_dst"].rearrange("h c -> (h c)")),
            lambda: aggregate_attention(nc, sem, g, "a0"),
            lambda: finish_attention(nc, sem, g, "f0", a["L0_gnn_bias"], ALU.add, True, True),
            lambda: aggregate(nc, sem, g, "a1", g.nodes, g.rows, None),
            lambda: perceptron(nc, sem, g, a["L1_gnn_W1"], a["L1_gnn_b1"], a["L1_gnn_W2"],
                               a["L1_gnn_b2"], a["L1_gnn_eps"], a["L1_gnn_gamma"],
                               a["L1_gnn_beta"]),
            lambda: project(nc, sem, g, "p2", g.X, a["L2_gnn_W1"], a["L2_gnn_att_src1"]
                            .rearrange("a h c -> (a h c)"), a["L2_gnn_att_dst1"]
                            .rearrange("a h c -> (a h c)")),
            lambda: aggregate_attention(nc, sem, g, "a2"),
            lambda: finish_attention(nc, sem, g, "f2", a["L2_gnn_b1"], ALU.max, False, False),
            lambda: project(nc, sem, g, "p3", g.sums, a["L2_gnn_W2"], a["L2_gnn_att_src2"]
                            .rearrange("a h c -> (a h c)"), a["L2_gnn_att_dst2"]
                            .rearrange("a h c -> (a h c)")),
            lambda: aggregate_attention(nc, sem, g, "a3"),
            lambda: finish_attention(nc, sem, g, "f3", a["L2_gnn_b2"], ALU.max, True, False),
            lambda: transform(nc, sem, g, a["L3_gnn_weight"]),
            lambda: aggregate(nc, sem, g, "a4", g.by_rel, g.rel_rows, g.edge_w),
            lambda: last_norm(nc, sem, g, out),
        ]
        for stage in todo[:stages]:
            stage()
            nc.clear_and_free_semaphores(used)
            used.clear()
            nc.all_engine_barrier()
        return g


INPUTS = ["x", "src", "dst", "edge_type_16", "edge_weight1", "L0_gnn_W", "L0_gnn_att_src",
          "L0_gnn_att_dst", "L0_gnn_bias", "L1_gnn_W1", "L1_gnn_b1", "L1_gnn_W2", "L1_gnn_b2",
          "L1_gnn_eps", "L1_gnn_gamma", "L1_gnn_beta", "L2_gnn_W1", "L2_gnn_att_src1",
          "L2_gnn_att_dst1", "L2_gnn_b1", "L2_gnn_W2", "L2_gnn_att_src2", "L2_gnn_att_dst2",
          "L2_gnn_b2", "L3_gnn_weight"]


def kernel(**inputs):
    import numpy as np
    import concourse.bacc as bacc
    from concourse.bass_utils import run_bass_kernel_spmd

    nc = bacc.Bacc("TRN2", target_bir_lowering=False, num_devices=1)
    arrays, args = {}, {}
    for name in INPUTS:
        v = np.ascontiguousarray(np.asarray(inputs[name]))
        if name == "L1_gnn_eps":
            v = v.reshape(1)
        arrays[name] = v
        args[name] = nc.dram_tensor(name, v.shape, mybir.dt.from_np(v.dtype),
                                    kind="ExternalInput").ap()
    out = nc.dram_tensor("out", [NODES, DIM], FP32, kind="ExternalOutput").ap()
    graph_layers(nc, args, out)
    got = run_bass_kernel_spmd(nc, [arrays], core_ids=[0])
    return got.results[0]["out"]
```

```python
from contextlib import ExitStack

import concourse.bass as bass
from concourse import mybir

FP32 = mybir.dt.float32
BF16 = mybir.dt.bfloat16
I32 = mybir.dt.int32
U32 = mybir.dt.uint32
ALU = mybir.AluOpType
ACT = mybir.ActivationFunctionType
AX = mybir.AxisListType
ENG = mybir.EngineType

P = 128
NODES, EDGES, DIM = 6250, 106250, 256
HEADS, CH = 4, 64
RELS = 16
BLOCKS = -(-NODES // P)
LAST = NODES - (BLOCKS - 1) * P
PADN = BLOCKS * P
TILES = -(-EDGES // P)
TAIL = EDGES - (TILES - 1) * P
STEPS = TILES + BLOCKS - 1
K = 8
BATCHES = -(-STEPS // K)
STEPP = BATCHES * K
CHUNKS = -(-STEPP // P)
CPAD = CHUNKS * P
SLOTS = 4
HC = CH + 3
ROW = HEADS * HC
GROUP = 7
GROUPS = BLOCKS // GROUP
BIG = 1.0e30
NOWHERE = 1 << 20
LN_EPS = 1e-5
SLOPE = 0.2
SKIP = "block numbers are counts of 48 comparisons, so 0..48"


def flat(ap):
    return ap.rearrange("p a b -> p (a b)")


class Memory(ExitStack):

    def __init__(self, nc):
        super().__init__()
        self.nc = nc

    def sb(self, name, shape, dtype):
        return self.enter_context(self.nc.sbuf_tensor(f"sb_{name}", shape, dtype))

    def ps(self, name, shape):
        return self.enter_context(self.nc.psum_tensor(f"ps_{name}", shape, FP32))


class Own:

    def __init__(self, sem, base=0):
        self.sem, self.n, self.base = sem, 0, base

    def inc(self, ins):
        self.n += 1
        ins.then_inc(self.sem, 1)
        return self.base + self.n

    def settle(self, eng):
        eng.wait_ge(self.sem, self.base + self.n)

    def step(self, eng, ins):
        self.inc(ins)
        self.settle(eng)


def lay_out_walk(nc, sem, g, src, dst, etype, weight):
    W = 3 * P + 1
    tab = nc.dram_tensor("edge_table", [TILES + 1, W], I32).ap()
    wtab = nc.dram_tensor("weight_table", [TILES + 1, P], FP32).ap()
    full = (TILES - 1) * P
    with Memory(nc) as sb:
        fill_i = sb.sb("w_fill_i", [1, 4 * P], I32)
        fill_f = sb.sb("w_fill_f", [1, 2 * P], FP32)
        first_i = sb.sb("w_first_i", [1, TILES], I32)
        first_f = sb.sb("w_first_f", [1, TILES], FP32)
        ones = sb.sb("w_ones", [P, P], FP32)
        thr = sb.sb("w_thr", [P, 1], FP32)
        pid = sb.sb("w_pid", [P, 1], FP32)
        cmp = sb.sb("w_cmp", [P, TILES], FP32)
        cnt = sb.sb("w_cnt", [P, 4], FP32)
        sidx = sb.sb("w_sidx", [P, CPAD + 1], FP32)
        ind = sb.sb("w_ind", [P, CPAD + 1], FP32)
        bcol = sb.sb("w_bcol", [P, 2 * CHUNKS], FP32)
        newt = sb.sb("w_newt", [P, CHUNKS], FP32)
        sid = sb.sb("w_sid", [P, CHUNKS], FP32)
        tid_f = sb.sb("w_tid_f", [P, CHUNKS], FP32)
        tid = sb.sb("w_tid", [P, CHUNKS], U32)
        rowi = sb.sb("w_rowi", [P, CHUNKS, W], I32)
        roww = sb.sb("w_roww", [P, CHUNKS, P], FP32)
        room = flat(g.X[:, :, :])
        arr = room[:, 0:7 * CPAD].rearrange("p (a c e) -> p a c e", a=7, c=CHUNKS)
        rowf = room[:, 7 * CPAD:7 * CPAD + CHUNKS * W].rearrange("p (c e) -> p c e", c=CHUNKS)
        mrow = sb.sb("w_mrow", [P, CHUNKS, P + 1], FP32)
        dlb = sb.sb("w_dlb", [P, CHUNKS, P], BF16)
        small = sb.sb("w_small", [P, 3, CHUNKS], FP32)
        diags = sb.sb("w_diags", [P, 2, P], FP32)
        along = sb.sb("w_along", [P, 2, STEPP], FP32)
        on_first = sb.sb("w_on_first", [P, 1], FP32)
        p_first = sb.ps("w_p_first", [P, 1024])
        p_bcol = sb.ps("w_p_bcol", [P, 512])
        p_brow = sb.ps("w_p_brow", [1, 1024])
        p_tr = sb.ps("w_p_tr", [P, 2, 512])
        filled, first_in, const = sem("w_filled"), sem("w_first_in"), sem("w_const")
        tabbed, first_bc, starts = sem("w_tabbed"), sem("w_first_bc"), sem("w_starts")
        bdone, tids, rows_in = sem("w_bdone"), sem("w_tids"), sem("w_rows_in")
        own, marked, turned = sem("w_own"), sem("w_marked"), sem("w_turned")
        saved, stored = sem("w_saved"), sem("w_stored")
        NARR = 7
        with nc.Block() as block:

            @block.gpsimd
            def _(pool):
                pool.memset(fill_i[:, 0:2 * P], 0).then_inc(filled, 1)
                pool.memset(fill_i[:, 2 * P:4 * P], NOWHERE).then_inc(filled, 1)
                pool.memset(fill_f[:, :], 0.0).then_inc(filled, 1)
                pool.memset(ones[:, :], 1.0).then_inc(const, 1)
                pool.iota(thr[:, :], [[0, 1]], base=P, channel_multiplier=P,
                          allow_small_or_imprecise_dtypes=True).then_inc(const, 1)
                pool.iota(pid[:, :], [[0, 1]], base=0, channel_multiplier=1,
                          allow_small_or_imprecise_dtypes=True).then_inc(const, 1)
                pool.iota(sidx[:, :], [[1, CPAD + 1]], base=-1, channel_multiplier=0,
                          allow_small_or_imprecise_dtypes=True).then_inc(const, 1)
                pool.iota(sid[:, :], [[P, CHUNKS]], base=0, channel_multiplier=1,
                          allow_small_or_imprecise_dtypes=True).then_inc(const, 1)
                pool.iota(g.iota_f[:, :], [[1, P]], base=0, channel_multiplier=0,
                          allow_small_or_imprecise_dtypes=True).then_inc(const, 1)
                pool.iota(g.iota_p[:, :], [[0, 1]], base=0, channel_multiplier=1,
                          allow_small_or_imprecise_dtypes=True).then_inc(const, 1)
                pool.memset(g.ones32[:, :], 1.0).then_inc(const, 1)
                pool.memset(g.ident[:, :], 0.0).then_inc(const, 1)
                pool.wait_ge(const, 9)
                pool.affine_select(out=g.ident[:, :], in_=g.ident[:, :], compare_op=ALU.not_equal,
                                   fill=1.0, base=0, pattern=[[-1, P]], channel_multiplier=1)\
                    .then_inc(const, 1)
                pool.wait_ge(tids, 1)
                pool.wait_ge(tabbed, 16 * 17)
                for c in range(CHUNKS):
                    off = bass.IndirectOffsetOnAxis(ap=tid[:, c:c + 1], axis=0)
                    pool.indirect_dma_start(out=rowi[:, c, :], out_offset=None, in_=tab,
                                            in_offset=off).then_inc(rows_in, 16)
                    pool.indirect_dma_start(out=roww[:, c, :], out_offset=None, in_=wtab,
                                            in_offset=off).then_inc(rows_in, 16)
                pool.wait_ge(rows_in, 32 * CHUNKS)

            @block.sync
            def _(sp):
                sp.dma_start(first_i[:, :], dst.rearrange("(a n) -> a n", a=1)[:, 0:EDGES:P],
                             allow_slow_non_contiguous=True)\
                    .then_inc(first_in, 16)
                for at, a in ((0, src), (P, etype), (2 * P + 1, dst)):
                    sp.dma_start(tab[0:TILES - 1, at:at + P],
                                 a[0:full].rearrange("(t e) -> t e", e=P)).then_inc(tabbed, 16)
                    sp.dma_start(tab[TILES - 1:TILES, at:at + TAIL],
                                 a[full:EDGES].rearrange("(t e) -> t e", t=1)).then_inc(tabbed, 16)
                sp.dma_start(tab[1:TILES, 2 * P:2 * P + 1],
                             dst[P - 1:full].rearrange("(t e) -> t e", e=1)[0:full - P + 1:P, :],
                             allow_slow_non_contiguous=True)\
                    .then_inc(tabbed, 16)
                sp.dma_start(wtab[0:TILES - 1, :],
                             weight[0:full, 0].rearrange("(t e) -> t e", e=P)).then_inc(tabbed, 16)
                sp.dma_start(wtab[TILES - 1:TILES, 0:TAIL],
                             weight[full:EDGES, 0].rearrange("(t e) -> t e", t=1))\
                    .then_inc(tabbed, 16)
                sp.wait_ge(filled, 3)
                sp.dma_start(tab[TILES - 1:TILES, TAIL:P], fill_i[:, 0:P - TAIL]).then_inc(tabbed, 16)
                sp.dma_start(tab[TILES - 1:TILES, P + TAIL:2 * P], fill_i[:, 0:P - TAIL])\
                    .then_inc(tabbed, 16)
                sp.dma_start(tab[TILES - 1:TILES, 2 * P + 1 + TAIL:W],
                             fill_i[:, 2 * P:3 * P - TAIL]).then_inc(tabbed, 16)
                sp.dma_start(wtab[TILES - 1:TILES, TAIL:P], fill_f[:, 0:P - TAIL])\
                    .then_inc(tabbed, 16)
                sp.dma_start(tab[TILES:TILES + 1, 0:2 * P], fill_i[:, 0:2 * P]).then_inc(tabbed, 16)
                sp.dma_start(tab[TILES:TILES + 1, 2 * P:W], fill_i[:, 2 * P:3 * P + 1])\
                    .then_inc(tabbed, 16)
                sp.dma_start(tab[0:1, 2 * P:2 * P + 1], fill_i[:, 3 * P + 2:3 * P + 3])\
                    .then_inc(tabbed, 16)
                sp.dma_start(wtab[TILES:TILES + 1, :], fill_f[:, P:2 * P]).then_inc(tabbed, 16)
                sp.wait_ge(marked, 1)
                for h in range(HEADS):
                    sp.dma_start(g.marks[:, h, :].rearrange("(c p) e -> p c e", p=P), mrow[:, :, :])\
                        .then_inc(stored, 16)
                sp.dma_start(g.places.rearrange("(c p) e -> p c e", p=P), dlb[:, :, :])\
                    .then_inc(stored, 16)
                sp.wait_ge(stored, 16 * (HEADS + 1))

            @block.tensor
            def _(pe):
                pe.wait_ge(const, 1)
                pe.wait_ge(own, 1)
                for a in range(0, TILES, 512):
                    z = min(a + 512, TILES)
                    last = nc.tensor.matmul(p_first[:, a:z], ones[0:1, :], first_f[0:1, a:z],
                                            start=True, stop=True)
                last.then_inc(first_bc, 1)
                pe.wait_ge(starts, 1)
                for c in range(CHUNKS):
                    for late in (0, 1):
                        nc.tensor.matmul(p_bcol[:, 2 * c + late:2 * c + late + 1],
                                         ind[0:BLOCKS - 1, c * P + late:(c + 1) * P + late],
                                         ones[0:BLOCKS - 1, 0:1], start=True, stop=True)
                for a in range(0, STEPP, 512):
                    z = min(a + 512, STEPP)
                    last = nc.tensor.matmul(p_brow[0:1, a:z], ones[0:BLOCKS - 1, 0:1],
                                            ind[0:BLOCKS - 1, a + 1:z + 1], start=True, stop=True)
                last.then_inc(bdone, 1)
                pe.wait_ge(marked, 1)
                pe.wait_ge(const, 10)
                n = 0
                for a in range(NARR):
                    for c in range(CHUNKS):
                        if n >= 2:
                            pe.wait_ge(saved, n - 1)
                        nc.tensor.transpose(p_tr[:, n % 2, 0:P], arr[:, a, c, :], g.ident[:, :])\
                            .then_inc(turned, 1)
                        n += 1

            @block.scalar
            def _(act):
                n = 0
                for a in range(NARR):
                    out = (g.rows, g.rel_rows, g.place, g.edge_w, g.follows, g.starts, g.ends)[a]
                    for c in range(CHUNKS):
                        z = min((c + 1) * P, STEPP)
                        n += 1
                        act.wait_ge(turned, n)
                        act.activation(out[:, c * P:z], p_tr[:, (n - 1) % 2, 0:z - c * P],
                                       ACT.Copy).then_inc(saved, 1)

            @block.vector
            def _(dve):
                w = Own(own)
                dve.wait_ge(first_in, 16)
                w.step(dve, dve.tensor_copy(first_f[:, :], first_i[:, :]))
                dve.wait_ge(const, 8)
                dve.wait_ge(first_bc, 1)
                for n, a in enumerate(range(0, TILES, 512)):
                    z = min(a + 512, TILES)
                    w.step(dve, dve.tensor_scalar(cmp[:, a:z], p_first[:, a:z], thr[:, 0:1], None,
                                                  ALU.is_lt, ALU.add, accum_out=cnt[:, n:n + 1]))
                w.step(dve, dve.tensor_tensor(cnt[:, 0:1], cnt[:, 0:1], cnt[:, 1:2], ALU.add))
                w.step(dve, dve.tensor_scalar(cnt[:, 2:3], cnt[:, 0:1], 1.0, pid[:, 0:1],
                                              ALU.max, ALU.add))
                dve.tensor_scalar(ind[:, :], sidx[:, :], cnt[:, 2:3], None, ALU.is_ge)\
                    .then_inc(starts, 1)
                dve.wait_ge(bdone, 1)
                w.step(dve, dve.tensor_copy(bcol[:, :], p_bcol[:, 0:2 * CHUNKS]))
                w.step(dve, dve.tensor_copy(g.block_of[0:1, :], p_brow[0:1, 0:STEPP]))
                b = bcol[:, :].rearrange("p (c l) -> p c l", l=2)
                w.step(dve, dve.tensor_tensor(tid_f[:, :], sid[:, :], b[:, :, 1], ALU.subtract))
                w.step(dve, dve.tensor_scalar(tid_f[:, :], tid_f[:, :], float(TILES), None, ALU.min))
                dve.tensor_copy(tid[:, :], tid_f[:, :]).then_inc(tids, 1)
                w.step(dve, dve.tensor_tensor(newt[:, :], b[:, :, 0], b[:, :, 1], ALU.is_equal))
                dve.wait_ge(rows_in, 32 * CHUNKS)
                w.step(dve, dve.tensor_copy(rowf[:, :, :], rowi[:, :, :]))
                srcs, types = rowf[:, :, 0:P], rowf[:, :, P:2 * P]
                prev, dsts = rowf[:, :, 2 * P:3 * P], rowf[:, :, 2 * P + 1:W]
                first = rowf[:, :, 2 * P + 1:2 * P + 2]
                rows_a, rel_a, place_a, w_a, foll_a, st_a, end_a = (arr[:, a] for a in range(NARR))
                cont, one, gate = small[:, 0], small[:, 1], small[:, 2]
                w.step(dve, dve.tensor_tensor(cont, rowf[:, :, 2 * P], rowf[:, :, 2 * P + 1],
                                              ALU.is_equal))
                w.step(dve, dve.tensor_tensor(cont, cont, newt[:, :], ALU.mult))
                w.step(dve, dve.tensor_tensor(one, rowf[:, :, 2 * P + 1], rowf[:, :, W - 1],
                                              ALU.is_equal))
                w.step(dve, dve.tensor_tensor(one, one, cont, ALU.mult))
                w.step(dve, dve.tensor_scalar(gate, one, BIG, -BIG, ALU.mult, ALU.add))
                w.step(dve, dve.tensor_copy(rows_a, srcs))
                w.step(dve, dve.scalar_tensor_tensor(out=rel_a, in0=types, scalar=float(PADN),
                                                     in1=srcs, op0=ALU.mult, op1=ALU.add))
                w.step(dve, dve.tensor_scalar(tid_f[:, :], b[:, :, 1], -float(P), None, ALU.mult))
                for c in range(CHUNKS):
                    w.step(dve, dve.tensor_scalar(place_a[:, c, :], dsts[:, c, :], tid_f[:, c:c + 1],
                                                  None, ALU.add))
                w.step(dve, dve.tensor_copy(w_a, roww[:, :, :]))
                w.step(dve, dve.tensor_scalar(dlb[:, :, :], place_a, -1.0, float(P), ALU.max, ALU.min))
                w.step(dve, dve.tensor_tensor(st_a, dsts, prev, ALU.not_equal))
                w.step(dve, dve.memset(mrow[:, :, P:P + 1], 0.0))
                w.step(dve, dve.tensor_scalar(mrow[:, :, 0:P], st_a, -BIG, None, ALU.mult))
                for c in range(CHUNKS):
                    w.step(dve, dve.tensor_scalar(foll_a[:, c, :], dsts[:, c, :], first[:, c, :],
                                                  cont[:, c:c + 1], ALU.is_equal, ALU.mult))
                w.step(dve, dve.tensor_scalar(foll_a, foll_a, BIG, -BIG, ALU.mult, ALU.add))
                for c in range(CHUNKS):
                    w.step(dve, dve.tensor_scalar(end_a[:, c, :], dsts[:, c, :],
                                                  rowf[:, c, W - 1:W], None, ALU.is_equal))
                w.step(dve, dve.tensor_scalar(end_a, end_a, BIG, -BIG, ALU.mult, ALU.add))
                dve.drain().then_inc(marked, 1)
        gd, gt, gs = sem("w_gate_diag"), sem("w_gate_turned"), sem("w_gate_saved")
        with nc.Block() as block:

            @block.vector
            def _(dve):
                for c in range(CHUNKS):
                    z = min((c + 1) * P, STEPP)
                    for i, what in enumerate((small[:, 2], small[:, 0])):
                        dve.tensor_scalar(diags[:, i, :], g.ident[:, :], what[:, c:c + 1], None,
                                          ALU.mult).then_inc(gd, 1)
                    dve.wait_ge(gt, c + 1)
                    dve.tensor_copy(along[:, :, c * P:z],
                                    p_first[:, 0:2 * P].rearrange("p (i s) -> p i s", i=2)
                                    [:, :, 0:z - c * P]).then_inc(gs, 1)
                dve.wait_ge(gs, CHUNKS)
                by_batch = along[:, 0, :].rearrange("p (q k) -> p q k", k=K)
                for gates, tiles in ((g.gates, by_batch), (g.gates_back, by_batch[:, :, ::-1])):
                    dve.memset(gates[:, :, 0::K + 1], -BIG)
                    for h in range(HEADS):
                        dve.tensor_copy(gates[:, :, h * (K + 1) + 1:(h + 1) * (K + 1)], tiles)
                dve.tensor_scalar(g.goes_on[:, :], along[:, 1, :], BIG, -BIG, ALU.mult, ALU.add)
                dve.tensor_scalar(on_first[:, :], pid[:, :], 0.0, None, ALU.is_equal)\
                    .then_inc(gs, 1)
                dve.wait_ge(gs, CHUNKS + 1)
                dve.tensor_scalar(g.opens[:, :], along[:, 1, 0:STEPP:K], on_first[:, 0:1], None,
                                  ALU.mult)

            @block.tensor
            def _(pe):
                for c in range(CHUNKS):
                    pe.wait_ge(gd, 2 * c + 2)
                    if c:
                        pe.wait_ge(gs, c)
                    for i in range(2):
                        last = nc.tensor.matmul(p_first[:, i * P:(i + 1) * P], ones[:, :],
                                                diags[:, i, :], start=True, stop=True)
                    last.then_inc(gt, 1)


def load_nodes(nc, sem, g, x):
    cleared, loaded = sem("x_cleared"), sem("x_loaded")
    with nc.Block() as block:

        @block.vector
        def _(dve):
            dve.memset(g.X[:, BLOCKS - 1, :], 0.0).then_inc(cleared, 1)

        @block.sync
        def _(sp):
            full = (BLOCKS - 1) * P
            sp.dma_start(g.X[:, 0:BLOCKS - 1, :], x[0:full, :].rearrange("(b p) d -> p b d", p=P))\
                .then_inc(loaded, 16)
            sp.wait_ge(cleared, 1)
            sp.dma_start(g.X[0:LAST, BLOCKS - 1, :], x[full:NODES, :]).then_inc(loaded, 16)
            sp.wait_ge(loaded, 32)


FROM = 1


def free_at(c, k):
    return c * GROUP + (max(k - 1, 0) + FROM)


def through(c, k):
    return c * GROUP + (k + 1 + FROM)


def project(nc, sem, g, tag, y, W, att_src, att_dst):
    with Memory(nc) as sb:
        w_sb = sb.sb(f"{tag}_w", [P, 2, DIM], FP32)
        wx = sb.sb(f"{tag}_wx", [P, 2, DIM + 2 * HEADS], FP32)
        att = sb.sb(f"{tag}_att", [P, 2, DIM], FP32)
        prod = sb.sb(f"{tag}_prod", [P, 2, DIM], FP32)
        yT = sb.sb(f"{tag}_yt", [P, 2, DIM], FP32)
        y_in = sb.sb(f"{tag}_y_in", [P, GROUP, DIM], FP32)
        rows = sb.sb(f"{tag}_rows", [P, GROUP, ROW], FP32)
        v = sb.sb(f"{tag}_v", [P, BLOCKS, 2 * HEADS], FP32)
        rest = sb.sb(f"{tag}_rest", [P, BLOCKS, 2 * HEADS], FP32)
        p_t = sb.ps(f"{tag}_pt", [P, 2, 512])
        p_y = sb.ps(f"{tag}_py", [P, 2, 512])
        loaded, ready, own = sem(f"{tag}_loaded"), sem(f"{tag}_ready"), sem(f"{tag}_own")
        turned, copied = sem(f"{tag}_turned"), sem(f"{tag}_copied")
        mult, evac, put = sem(f"{tag}_mult"), sem(f"{tag}_evac"), sem(f"{tag}_put")
        vsaved, rows_free = sem(f"{tag}_vsaved"), sem(f"{tag}_rows_free")
        PARTS = ((0, GROUP // 2 + 1), (GROUP // 2 + 1, GROUP))
        y_ok = [sem(f"{tag}_y_ok{i}") for i in range(2)]
        H65 = CH + 1
        with nc.Block() as block:

            @block.gpsimd
            def _(pool):
                for s in (turned, copied, mult, evac, vsaved, rows_free):
                    pool.sem_inc(s, FROM)
                with pool.Fori(0, GROUPS) as c:
                    pool.wait_ge(put, c * 16 + 16)
                    pool.sem_inc(rows_free, 1)

            @block.sync
            def _(sp):
                sp.dma_start(w_sb[:, :, :], W.rearrange("(k p) n -> p k n", p=P)).then_inc(loaded, 16)
                for i, a in enumerate((att_src, att_dst)):
                    sp.dma_start(att[:, i, :], a.partition_broadcast(P)).then_inc(loaded, 16)
                with sp.Fori(0, GROUPS) as c:
                    for i, (a, z) in enumerate(PARTS):
                        sp.wait_ge(turned, c * GROUP + FROM)
                        sp.dma_start(y_in[:, a:z, :], y[:, bass.ds(c * GROUP + a, z - a), 0:DIM])\
                            .then_inc(y_ok[i], 16)
                    sp.wait_ge(evac, through(c, GROUP - 1))
                    sp.dma_start(g.table[bass.ds(c * (GROUP * P), GROUP * P), :]
                                 .rearrange("(b p) r -> p b r", p=P), rows[:, :, :])\
                        .then_inc(put, 16)
                sp.wait_ge(put, 16 * GROUPS)

            @block.tensor
            def _(pe):
                pe.wait_ge(ready, 1)
                with pe.Fori(0, GROUPS) as c:
                    for k in range(GROUP + 1):
                        if k < GROUP:
                            for i, (a, z) in enumerate(PARTS):
                                if k == a:
                                    pe.wait_ge(y_ok[i], c * 16 + 16)
                            pe.wait_ge(copied, free_at(c, k))
                            for i in range(2):
                                last = nc.tensor.transpose(p_t[:, k % 2, i * P:(i + 1) * P],
                                                           y_in[:, k, i * P:(i + 1) * P],
                                                           g.ident[:, :])
                            last.then_inc(turned, 1)
                        if k:
                            pe.wait_ge(copied, through(c, k - 1))
                            pe.wait_ge(vsaved, free_at(c, k - 1))
                            for i in range(2):
                                last = nc.tensor.matmul(p_y[:, (k - 1) % 2, 0:DIM + 2 * HEADS],
                                                        yT[:, (k - 1) % 2, i * P:(i + 1) * P],
                                                        wx[:, i, :], start=(i == 0), stop=(i == 1))
                            last.then_inc(mult, 1)

            @block.scalar
            def _(act):
                act.wait_ge(ready, 1)
                with act.Fori(0, GROUPS) as c:
                    for k in range(GROUP + 1):
                        if k < GROUP:
                            act.wait_ge(turned, through(c, k))
                            act.wait_ge(mult, free_at(c, k))
                            act.activation(yT[:, k % 2, :], p_t[:, k % 2, 0:DIM], ACT.Copy)\
                                .then_inc(copied, 1)
                        if k:
                            if k == 1:
                                act.wait_ge(rows_free, c + FROM)
                            act.wait_ge(mult, through(c, k - 1))
                            act.activation(
                                rows[:, k - 1, :].rearrange("p (h r) -> p h r", h=HEADS)[:, :, 0:H65],
                                p_y[:, (k - 1) % 2, 0:HEADS * H65]
                                .rearrange("p (h r) -> p h r", h=HEADS), ACT.Copy).then_inc(evac, 1)

            @block.vector
            def _(dve):
                w = Own(own)
                r = rows[:, :, :].rearrange("p b (h r) -> p (b h) r", h=HEADS)
                w.step(dve, dve.memset(r[:, :, CH + 1:CH + 2], 1.0))
                w.step(dve, dve.memset(r[:, :, CH + 2:CH + 3], 0.0))
                dve.wait_ge(loaded, 48)
                for k in range(2):
                    w.step(dve, dve.tensor_copy(
                        wx[:, k, 0:HEADS * H65].rearrange("p (h r) -> p h r", h=HEADS)[:, :, 1:H65],
                        w_sb[:, k, :].rearrange("p (h r) -> p h r", h=HEADS)))
                for i in range(2):
                    for k in range(2):
                        w.step(dve, dve.tensor_tensor(prod[:, k, :], w_sb[:, k, :], att[:, i, :],
                                                      ALU.mult))
                        out = (wx[:, k, 0:HEADS * H65:H65], wx[:, k, HEADS * H65:])[i]
                        w.step(dve, dve.tensor_reduce(
                            out, prod[:, k, :].rearrange("p (h r) -> p h r", h=HEADS), AX.X, ALU.add))
                dve.drain().then_inc(ready, 1)
                with dve.Fori(0, GROUPS) as c:
                    for k in range(GROUP):
                        dve.wait_ge(evac, through(c, k))
                        at = bass.ds(c * GROUP + k, 1)
                        dve.tensor_copy(v[:, at, 0:HEADS].rearrange("p a b -> p (a b)"),
                                        p_y[:, k % 2, 0:HEADS * H65:H65])
                        dve.tensor_copy(v[:, at, HEADS:].rearrange("p a b -> p (a b)"),
                                        p_y[:, k % 2, HEADS * H65:HEADS * H65 + HEADS])\
                            .then_inc(vsaved, 1)
                dve.wait_ge(vsaved, BLOCKS + FROM)
                sc = g.scores[:, :, :, :]
                w.step(dve, dve.tensor_copy(sc[:, :, 0, :], v[:, :, :]))
                w.step(dve, dve.tensor_tensor(rest[:, :, :], v[:, :, :], sc[:, :, 0, :], ALU.subtract))
                w.step(dve, dve.tensor_copy(sc[:, :, 1, :], rest[:, :, :]))
                w.step(dve, dve.tensor_tensor(rest[:, :, :], rest[:, :, :], sc[:, :, 1, :],
                                              ALU.subtract))
                w.step(dve, dve.tensor_copy(sc[:, :, 2, :], rest[:, :, :]))


def aggregate_attention(nc, sem, g, tag):
    OHS = 4
    KH = K * HEADS
    HK = K + 1
    CIN, TOP = 2 * KH, 2 * KH + HEADS
    with Memory(nc) as sb:
        G = sb.sb(f"{tag}_rows", [P, SLOTS, K, ROW], FP32)
        idx = sb.sb(f"{tag}_idx", [P, SLOTS, K], U32)
        marks = sb.sb(f"{tag}_marks", [KH, SLOTS, P + 1], FP32)
        places = sb.sb(f"{tag}_places", [P, SLOTS, K * P], BF16)
        turned01 = sb.sb(f"{tag}_turned01", [P, K * P], BF16)
        onehot = sb.sb(f"{tag}_onehot", [P, OHS, P], FP32)
        D = sb.sb(f"{tag}_node_scores", [P, 2, K, 2 * HEADS], FP32)
        sm = sb.sb(f"{tag}_sm", [P, K, HEADS], FP32)
        fwd = sb.sb(f"{tag}_fwd", [KH, P], FP32)
        seg = sb.sb(f"{tag}_seg", [KH, P], FP32)
        diag = sb.sb(f"{tag}_diag", [KH, 2, KH], FP32)
        last_max = sb.sb(f"{tag}_last_max", [P, HEADS, HK], FP32)
        so_far = sb.sb(f"{tag}_so_far", [P, HEADS, HK], FP32)
        first_max = sb.sb(f"{tag}_first_max", [P, HEADS, HK], FP32)
        joined = sb.sb(f"{tag}_joined", [P, HEADS, HK], FP32)
        final = sb.sb(f"{tag}_final", [P, HEADS, HK], FP32)
        t1 = sb.sb(f"{tag}_t1", [P, K, HEADS], FP32)
        t2 = sb.sb(f"{tag}_t2", [P, K, HEADS], FP32)
        A = sb.sb(f"{tag}_alpha", [P, TOP + KH], FP32)
        A2 = sb.sb(f"{tag}_alpha2", [P, TOP + KH], FP32)
        dif = sb.sb(f"{tag}_dif", [P, TOP], FP32)
        ex = sb.sb(f"{tag}_ex", [P, 2, TOP], FP32)
        scale = sb.sb(f"{tag}_scale", [P, HEADS], FP32)
        p_sum = sb.ps(f"{tag}_psum", [P, OHS, 512])
        p_node = sb.ps(f"{tag}_pnode", [P, 2, 512])
        p_seg = sb.ps(f"{tag}_pseg", [P, 512])
        p_top = sb.ps(f"{tag}_ptop", [P, 512])
        idx_ok = sem(f"{tag}_idx_ok")
        rows_in = [sem(f"{tag}_rows_in{b}") for b in range(SLOTS)]
        marks_in = [sem(f"{tag}_marks_in{b}") for b in range(SLOTS)]
        t01_ok, node_ok, sm_ok = sem(f"{tag}_t01"), sem(f"{tag}_node"), sem(f"{tag}_sm_ok")
        pseg_ok, diag_ok, top_ok = sem(f"{tag}_pseg"), sem(f"{tag}_diag_ok"), sem(f"{tag}_top_ok")
        dif_ok, ex_ok = sem(f"{tag}_dif_ok"), sem(f"{tag}_ex_ok")
        extra_ok = sem(f"{tag}_extra_ok")
        weighted = sem(f"{tag}_weighted")
        onehot_ok = sem(f"{tag}_onehot_ok")
        summed = sem(f"{tag}_summed")
        added = sem(f"{tag}_added")
        own, begun = sem(f"{tag}_own"), sem(f"{tag}_begun")
        FREE = SLOTS * K
        NCH, NHEAD, PRE = 22, 3, 27
        LOOPS = (BATCHES - 2) // SLOTS
        assert LOOPS * SLOTS + 2 == BATCHES and SLOTS % 2 == 0

        def all_batches(eng, turn):
            with eng.Fori(0, LOOPS) as i:
                for b in range(SLOTS):
                    turn(i * SLOTS + b, i, b)
            for b in range(2):
                turn(LOOPS * SLOTS + b, LOOPS, b)

        def later(i, b, n):
            i, b = i + (b + n) // SLOTS, (b + n) % SLOTS
            return i * SLOTS + b, i, b

        def blocks_of(q, engine):
            _, vals = nc.values_load_multi_w_load_instructions(
                g.block_of[0:1, bass.ds(q * K, K)], engines=[engine], min_val=0,
                max_val=BLOCKS - 1, skip_runtime_bounds_check_because=SKIP)
            return vals

        def slot(b):
            return G[:, b, :, :].rearrange("p k (h r) -> p k h r", h=HEADS)

        def by_k(t):
            return t.rearrange("p (k h) -> p k h", h=HEADS)

        def per_edge(table, q):
            return table[:, bass.ds(q * K, K)].unsqueeze(2).to_broadcast([P, K, HEADS])

        with nc.Block() as block:

            @block.gpsimd
            def _(pool):
                pool.sem_inc(summed, FREE)
                pool.sem_inc(added, OHS)
                pool.memset(idx[:, :, :], 0).then_inc(begun, 1)
                pool.wait_ge(begun, 1)

                def gather(q, i, b):
                    pool.wait_ge(summed, q * K + K)
                    pool.tensor_copy(idx[:, b, :], g.rows[:, bass.ds(q * K, K)]).then_inc(idx_ok, 1)
                    pool.wait_ge(idx_ok, q + 1)
                    pool.sem_inc(begun, 1)
                    for k in range(K):
                        pool.indirect_dma_start(
                            out=G[:, b, k, :], out_offset=None, in_=g.table,
                            in_offset=bass.IndirectOffsetOnAxis(ap=idx[:, b, k:k + 1], axis=0))\
                            .then_inc(rows_in[b], 16)

                all_batches(pool, gather)

            @block.sync
            def _(sp):
                def load(q, i, b):
                    sp.wait_ge(summed, q * K + K)
                    sp.dma_start(marks[:, b, :],
                                 g.marks[bass.ds(q * K, K), :, :].rearrange("k h e -> (k h) e"))\
                        .then_inc(marks_in[b], 16)
                    sp.dma_start(places[:, b, :],
                                 g.places[bass.ds(q * K, K), :].rearrange("k e -> (k e)")
                                 .partition_broadcast(P)).then_inc(marks_in[b], 16)

                all_batches(sp, load)

            @block.tensor
            def _(pe):
                def node_scores(q, b):
                    blk = blocks_of(q, ENG.PE)
                    pe.wait_ge(t01_ok, q + 1)
                    for k in range(K):
                        last = nc.tensor.matmul(
                            p_node[:, b % 2, k * 6 * HEADS:(k + 1) * 6 * HEADS],
                            turned01[:, k * P:(k + 1) * P],
                            g.scores[:, bass.ds(blk[k], 1), :, :].rearrange("p a t h -> p (a t h)"),
                            start=True, stop=True)
                    last.then_inc(node_ok, 1)

                def turn_scores(q):
                    pe.wait_ge(sm_ok, q + 1)
                    nc.tensor.transpose(p_seg[0:KH, 0:P], flat(sm[:, :, :]), g.ident[:, :])\
                        .then_inc(pseg_ok, 1)

                def turn_tops(q):
                    pe.wait_ge(diag_ok, q + 1)
                    nc.tensor.matmul(p_top[:, KH:3 * KH], g.ones32[:, :], flat(diag[:, :, :]),
                                     start=True, stop=True)
                    nc.tensor.transpose(p_top[:, 0:KH], seg[:, :], g.ident[0:KH, 0:KH])\
                        .then_inc(top_ok, 1)

                def sum_up(q, b, k):
                    pe.wait_ge(onehot_ok, q * K + k + 1)
                    pe.wait_ge(weighted, q * K + k + 1)
                    if k == 0:
                        pe.wait_ge(extra_ok, q + 1)
                    pe.wait_ge(added, q * K + k + 1)
                    nc.tensor.matmul(p_sum[:, k % OHS, 0:ROW], onehot[:, k % OHS, :], G[:, b, k, :],
                                     start=True, stop=True).then_inc(summed, 1)

                def turn(i, b, head=True, tops=True):
                    q = i * SLOTS + b
                    n, _, m = later(i, b, 2)
                    for k in range(K):
                        sum_up(q, b, k)
                        if tops and k == 0:
                            turn_tops(q + 1)
                        if head and k == 5:
                            node_scores(n, m)
                        if head and k == 6:
                            turn_scores(n)

                for q in range(2):
                    node_scores(q, q)
                    turn_scores(q)
                    if q == 0:
                        turn_tops(q)
                with pe.Fori(0, LOOPS) as i:
                    for b in range(SLOTS):
                        turn(i, b)
                turn(LOOPS, 0, head=False)
                turn(LOOPS, 1, head=False, tops=False)

            @block.scalar
            def _(act):
                def weigh(q, i, b):
                    act.wait_ge(dif_ok, q + 1)
                    act.activation(ex[:, b % 2, :], dif[:, :], ACT.Exp).then_inc(ex_ok, 1)
                    act.wait_ge(ex_ok, q + 1)
                    for k in range(K):
                        for h in range(HEADS):
                            part = G[:, b, k, h * HC + 1:(h + 1) * HC - 1]
                            last = act.activation(part, part, ACT.Copy,
                                                  scale=ex[:, b % 2, k * HEADS + h:k * HEADS + h + 1])
                        last.then_inc(weighted, 1)

                all_batches(act, weigh)

            @block.vector
            def _(dve):
                def make_onehot(q, k):
                    s = q * K + k
                    dve.wait_ge(summed, s + (FREE - OHS + 1))
                    dve.tensor_scalar(onehot[:, k % OHS, :], g.iota_f[:, :],
                                      g.place[:, bass.ds(s, 1)], None, ALU.is_equal)\
                        .then_inc(onehot_ok, 1)

                def add(q, k, blk, w):
                    s = q * K + k
                    dve.wait_ge(summed, s + (FREE + 1))
                    if k:
                        dve.wait_ge(added, s + OHS)
                        acc = flat(g.sums[:, bass.ds(blk, 1), :])
                        dve.tensor_tensor(acc, acc, p_sum[:, k % OHS, 0:ROW], ALU.add)\
                            .then_inc(added, 1)
                        return
                    part = p_sum[:, k % OHS, 0:ROW].rearrange("p (h r) -> p h r", h=HEADS)
                    w.step(dve, dve.tensor_scalar(scale[:, :], part[:, :, HC - 1], 1.0, None, ALU.add))
                    dve.wait_ge(added, s + OHS)
                    acc = g.sums[:, bass.ds(blk, 1), :].rearrange("p a (h r) -> p (a h) r", h=HEADS)
                    for h in range(HEADS):
                        last = dve.scalar_tensor_tensor(
                            out=acc[:, h, :], in0=acc[:, h, :], scalar=scale[:, h:h + 1],
                            in1=part[:, h, :], op0=ALU.mult, op1=ALU.add)
                    last.then_inc(added, 1)

                def head(k, n, j, m, w, q=None, blk=None):
                    if k == 4:
                        dve.wait_ge(marks_in[m], j * 32 + 32)
                        dve.tensor_scalar(turned01[:, :], places[:, m, :], g.iota_p[:, 0:1], None,
                                          ALU.is_equal).then_inc(t01_ok, 1)
                    d = D[:, m % 2, :, :]
                    if k == 5:
                        dve.wait_ge(node_ok, n + 1)
                        w.step(dve, dve.tensor_reduce(
                            d, p_node[:, m % 2, 0:6 * KH].rearrange("p (k t h) -> p k h t", k=K, t=3),
                            AX.X, ALU.add))
                        dve.wait_ge(rows_in[m], j * (16 * K) + 16 * K)
                        dve.tensor_tensor(sm[:, :, :], slot(m)[:, :, :, 0], d[:, :, 0:HEADS],
                                          ALU.max).then_inc(sm_ok, 1)
                    if k == 6:
                        dve.wait_ge(pseg_ok, n + 1)
                        w.inc(dve.tensor_tensor_scan(fwd[:, :], marks[:, m, 0:P], p_seg[0:KH, 0:P],
                                                     -BIG, ALU.add, ALU.max))
                    if k == 7:
                        w.settle(dve)
                        w.step(dve, dve.tensor_tensor_scan(seg[:, ::-1], marks[:, m, P:0:-1],
                                                           fwd[:, ::-1], -BIG, ALU.add, ALU.max))
                        dve.tensor_tensor(
                            diag[:, :, :],
                            g.ident[0:KH, 0:KH].unsqueeze(1).to_broadcast([KH, 2, KH]),
                            seg[:, 0:P:P - 1].unsqueeze(2).to_broadcast([KH, 2, KH]), ALU.mult)\
                            .then_inc(diag_ok, 1)

                def tail(k, n, m, w):
                    d = D[:, m % 2, :, :]
                    dst = d[:, :, HEADS:]
                    spread = p_top[:, KH:3 * KH].rearrange("p (a k h) -> p a h k", a=2, h=HEADS)
                    if k == 0:
                        w.step(dve, dve.tensor_copy(last_max[:, :, 0], so_far[:, :, K]))
                        w.inc(dve.tensor_tensor(by_k(A[:, 0:KH]), slot(m)[:, :, :, 0], dst, ALU.add))
                        w.inc(dve.tensor_tensor(by_k(A[:, KH:CIN]), d[:, :, 0:HEADS], dst, ALU.add))
                        w.inc(dve.tensor_tensor(A[:, CIN:TOP], last_max[:, :, 0], dst[:, 0, :],
                                                ALU.add))
                    if k == 1:
                        dve.wait_ge(top_ok, n + 1)
                        w.inc(dve.tensor_copy(last_max[:, :, 1:HK], spread[:, 1]))
                        w.inc(dve.tensor_tensor(
                            first_max[:, :, 0:K], spread[:, 0],
                            g.goes_on[:, bass.ds(n * K, K)].unsqueeze(1).to_broadcast([P, HEADS, K]),
                            ALU.add))
                    if k == 2:
                        w.settle(dve)
                        w.inc(dve.tensor_tensor_scan(
                            flat(so_far[:, :, :]), flat(g.gates[:, bass.ds(n, 1), :]),
                            flat(last_max[:, :, :]), -BIG, ALU.add, ALU.max))
                    if k == 3:
                        w.settle(dve)
                        w.step(dve, dve.tensor_tensor(joined[:, :, :], first_max[:, :, :],
                                                      so_far[:, :, :], ALU.max))
                        w.inc(dve.tensor_tensor_scan(
                            flat(final[:, :, :])[:, ::-1],
                            flat(g.gates_back[:, bass.ds(n, 1), :]),
                            flat(joined[:, :, :])[:, ::-1], -BIG, ALU.add, ALU.max))
                    if k == 4:
                        w.settle(dve)
                        seen = final[:, :, :].rearrange("p h k -> p k h")
                        w.inc(dve.tensor_tensor(t1[:, :, :], per_edge(g.follows, n), seen[:, 0:K, :],
                                                ALU.add))
                        w.step(dve, dve.tensor_tensor(t2[:, :, :], per_edge(g.ends, n),
                                                      seen[:, 1:HK, :], ALU.add))
                        w.step(dve, dve.tensor_tensor(t1[:, :, :], t1[:, :, :], t2[:, :, :], ALU.max))
                        w.inc(dve.tensor_tensor(t2[:, :, :], t1[:, :, :], by_k(p_top[:, 0:KH]),
                                                ALU.max))
                    if k == 5:
                        w.settle(dve)
                        w.step(dve, dve.tensor_tensor(by_k(A[:, TOP:]), t2[:, :, :], dst, ALU.add))
                        w.inc(dve.scalar_tensor_tensor(out=A2[:, :], in0=A[:, :], scalar=SLOPE,
                                                       in1=A[:, :], op0=ALU.mult, op1=ALU.max))
                    if k == 6:
                        w.settle(dve)
                        top = A2[:, TOP:].unsqueeze(1).to_broadcast([P, 2, KH])
                        w.inc(dve.tensor_tensor(
                            dif[:, 0:CIN].rearrange("p (a e) -> p a e", a=2),
                            A2[:, 0:CIN].rearrange("p (a e) -> p a e", a=2), top, ALU.subtract))
                        w.step(dve, dve.tensor_tensor(dif[:, CIN:TOP], A2[:, CIN:TOP],
                                                      A2[:, TOP:TOP + HEADS], ALU.subtract))
                        dve.tensor_scalar(dif[:, :], dif[:, :], 0.0, None, ALU.min)\
                            .then_inc(dif_ok, 1)
                    if k == 7:
                        dve.wait_ge(ex_ok, n + 1)
                        e = ex[:, m % 2, :]
                        w.inc(dve.tensor_tensor(slot(m)[:, :, :, 0], by_k(e[:, KH:CIN]),
                                                per_edge(g.starts, n), ALU.mult))
                        w.settle(dve)
                        dve.scalar_tensor_tensor(
                            out=slot(m)[:, 0, :, HC - 1], in0=e[:, CIN:TOP], scalar=-1.0,
                            in1=g.opens[:, bass.ds(n, 1)].to_broadcast([P, HEADS]),
                            op0=ALU.add, op1=ALU.mult).then_inc(extra_ok, 1)

                def turn(i, b, heads=True, tails=True):
                    q = i * SLOTS + b
                    w = Own(own, q * NCH + PRE - (0 if tails else NHEAD))
                    blk = blocks_of(q, ENG.DVE)
                    n1, _, m1 = later(i, b, 1)
                    n2, j2, m2 = later(i, b, 2)
                    for k in range(K):
                        if tails or k + 2 < K:
                            make_onehot(q, k + 2)
                        if tails:
                            tail(k, n1, m1, w)
                        add(q, k, blk[k], w)
                        if heads:
                            head(k, n2, j2, m2, w)
                    assert w.n == NCH - (0 if heads else NHEAD) or not tails, w.n

                w = Own(own)
                w.inc(dve.memset(g.sums[:, :, :], 0.0))
                w.inc(dve.memset(first_max[:, :, K:HK], -BIG))
                w.inc(dve.memset(so_far[:, :, :], -BIG))
                w.settle(dve)
                dve.wait_ge(added, OHS)
                for k in range(K):
                    head(k, 0, 0, 0, w)
                for k in range(K):
                    tail(k, 0, 0, w)
                for k in range(K):
                    head(k, 1, 0, 1, w)
                assert w.n == PRE, w.n
                make_onehot(0, 0)
                make_onehot(0, 1)
                with dve.Fori(0, LOOPS) as i:
                    for b in range(SLOTS):
                        turn(i, b)
                turn(LOOPS, 0, heads=False)
                turn(LOOPS, 1, heads=False, tails=False)


def aggregate(nc, sem, g, tag, table, rows, weights):
    OHS = 4
    with Memory(nc) as sb:
        G = sb.sb(f"{tag}_rows", [P, SLOTS, K, DIM], FP32)
        idx = sb.sb(f"{tag}_idx", [P, SLOTS, K], U32)
        onehot = sb.sb(f"{tag}_onehot", [P, OHS, P], FP32)
        p_sum = sb.ps(f"{tag}_psum", [P, OHS, 512])
        idx_ok, begun = sem(f"{tag}_idx_ok"), sem(f"{tag}_begun")
        rows_in = [sem(f"{tag}_rows_in{b}") for b in range(SLOTS)]
        onehot_ok = sem(f"{tag}_onehot_ok")
        summed = sem(f"{tag}_summed")
        added = sem(f"{tag}_added")
        FREE = SLOTS * K
        LOOPS = (BATCHES - 2) // SLOTS

        def all_batches(eng, turn):
            with eng.Fori(0, LOOPS) as i:
                for b in range(SLOTS):
                    turn(i * SLOTS + b, i, b)
            for b in range(2):
                turn(LOOPS * SLOTS + b, LOOPS, b)

        with nc.Block() as block:

            @block.gpsimd
            def _(pool):
                pool.sem_inc(summed, FREE)
                pool.sem_inc(added, OHS)
                pool.memset(idx[:, :, :], 0).then_inc(begun, 1)
                pool.wait_ge(begun, 1)

                def gather(q, i, b):
                    pool.wait_ge(summed, q * K + K)
                    pool.tensor_copy(idx[:, b, :], rows[:, bass.ds(q * K, K)]).then_inc(idx_ok, 1)
                    pool.wait_ge(idx_ok, q + 1)
                    pool.sem_inc(begun, 1)
                    for k in range(K):
                        pool.indirect_dma_start(
                            out=G[:, b, k, :], out_offset=None, in_=table,
                            in_offset=bass.IndirectOffsetOnAxis(ap=idx[:, b, k:k + 1], axis=0))\
                            .then_inc(rows_in[b], 16)

                all_batches(pool, gather)

            @block.tensor
            def _(pe):
                def turn(q, i, b):
                    pe.wait_ge(rows_in[b], i * (16 * K) + 16 * K)
                    for k in range(K):
                        pe.wait_ge(onehot_ok, q * K + k + 1)
                        pe.wait_ge(added, q * K + k + 1)
                        nc.tensor.matmul(p_sum[:, k % OHS, 0:DIM], onehot[:, k % OHS, :],
                                         G[:, b, k, :], start=True, stop=True).then_inc(summed, 1)

                all_batches(pe, turn)

            @block.vector
            def _(dve):
                def make_onehot(q, k):
                    s = q * K + k
                    dve.wait_ge(summed, s + (FREE - OHS + 1))
                    if weights is None:
                        dve.tensor_scalar(onehot[:, k % OHS, :], g.iota_f[:, :],
                                          g.place[:, bass.ds(s, 1)], None, ALU.is_equal)\
                            .then_inc(onehot_ok, 1)
                    else:
                        dve.tensor_scalar(onehot[:, k % OHS, :], g.iota_f[:, :],
                                          g.place[:, bass.ds(s, 1)], weights[:, bass.ds(s, 1)],
                                          ALU.is_equal, ALU.mult).then_inc(onehot_ok, 1)

                def turn(q, i, b, last=False):
                    _, blk = nc.values_load_multi_w_load_instructions(
                        g.block_of[0:1, bass.ds(q * K, K)], engines=[ENG.DVE], min_val=0,
                        max_val=BLOCKS - 1, skip_runtime_bounds_check_because=SKIP)
                    for k in range(K):
                        if not (last and k + 2 >= K):
                            make_onehot(q, k + 2)
                        s = q * K + k
                        dve.wait_ge(summed, s + (FREE + 1))
                        dve.wait_ge(added, s + OHS)
                        acc = flat(g.sums[:, bass.ds(blk[k], 1), 0:DIM])
                        dve.tensor_tensor(acc, acc, p_sum[:, k % OHS, 0:DIM], ALU.add)\
                            .then_inc(added, 1)

                dve.memset(g.sums[:, :, :], 0.0)
                dve.drain()
                dve.wait_ge(added, OHS)
                make_onehot(0, 0)
                make_onehot(0, 1)
                with dve.Fori(0, LOOPS) as i:
                    for b in range(SLOTS):
                        turn(i * SLOTS + b, i, b)
                turn(BATCHES - 2, LOOPS, 0)
                turn(BATCHES - 1, LOOPS, 1, last=True)


class Norm:
    STEPS = 3 * GROUP + 2

    def __init__(self, nc, sem, sb, tag, per_group):
        self.nc, self.per = nc, per_group
        self.stats = sb.sb(f"{tag}_stats", [P, GROUP, 6], FP32)
        self.mv = sb.sb(f"{tag}_mv", [P, GROUP, 2], FP32)
        self.std = sb.sb(f"{tag}_std", [P, GROUP], FP32)
        self.inv = sb.sb(f"{tag}_inv", [P, GROUP], FP32)
        self.shift = sb.sb(f"{tag}_shift", [P, GROUP], FP32)
        self.var_ok, self.std_ok = sem(f"{tag}_var_ok"), sem(f"{tag}_std_ok")
        self.held = sem(f"{tag}_held")

    def vector(self, dve, w, c, n, y):
        dve.sem_inc(self.held, 1)
        for k in range(GROUP):
            w.inc(dve.bn_stats(self.stats[:, k, :], y(k)))
        dve.wait_ge(w.sem, w.base + w.n)
        dve.sem_inc(self.held, 1)
        for k in range(GROUP):
            w.inc(dve.bn_aggr(self.mv[:, k, :], self.stats[:, k, :]))
        dve.wait_ge(w.sem, w.base + w.n)
        dve.tensor_scalar(self.std[:, :], self.mv[:, :, 1], LN_EPS, None, ALU.add)\
            .then_inc(self.var_ok, 1)
        dve.wait_ge(self.std_ok, c * self.per + n + 1)
        w.step(dve, dve.reciprocal(self.inv[:, :], self.std[:, :]))
        w.step(dve, dve.scalar_tensor_tensor(out=self.shift[:, :], in0=self.mv[:, :, 0], scalar=-1.0,
                                             in1=self.inv[:, :], op0=ALU.mult, op1=ALU.mult))
        for k in range(GROUP):
            w.inc(dve.tensor_scalar(y(k), y(k), self.inv[:, k:k + 1], self.shift[:, k:k + 1],
                                    ALU.mult, ALU.add))
        dve.wait_ge(w.sem, w.base + w.n)

    def scalar(self, act, c, n):
        act.wait_ge(self.var_ok, c * self.per + n + 1)
        act.activation(self.std[:, :], self.std[:, :], ACT.Sqrt).then_inc(self.std_ok, 1)


def finish_attention(nc, sem, g, tag, bias, guard, norm, store):
    with Memory(nc) as sb:
        own_rows = sb.sb(f"{tag}_own_rows", [P, GROUP, ROW], FP32)
        T = sb.sb(f"{tag}_t", [P, GROUP, DIM], FP32)
        bias_sb = sb.sb(f"{tag}_bias", [P, DIM], FP32)
        den = sb.sb(f"{tag}_den", [P, GROUP * HEADS], FP32)
        lone = sb.sb(f"{tag}_lone", [P, GROUP * HEADS], FP32)
        self_w = sb.sb(f"{tag}_self_w", [P, GROUP * HEADS], FP32)
        bias_in, rows_in, rows_used = sem(f"{tag}_bias_in"), sem(f"{tag}_rows_in"), sem(f"{tag}_used")
        own, done, stored = sem(f"{tag}_own"), sem(f"{tag}_done"), sem(f"{tag}_stored")
        ln = Norm(nc, sem, sb, tag, 1) if norm else None
        NV = 9 + (Norm.STEPS + 1 if norm else 0)
        with nc.Block() as block:

            @block.gpsimd
            def _(pool):
                pool.sem_inc(rows_used, FROM)

            @block.sync
            def _(sp):
                sp.dma_start(bias_sb[:, :], bias.partition_broadcast(P)).then_inc(bias_in, 16)
                with sp.Fori(0, GROUPS) as c:
                    sp.wait_ge(rows_used, c + FROM)
                    sp.dma_start(own_rows[:, :, :],
                                 g.table[bass.ds(c * (GROUP * P), GROUP * P), :]
                                 .rearrange("(b p) r -> p b r", p=P)).then_inc(rows_in, 16)
                    if store:
                        sp.wait_ge(done, c + 1)
                        sp.dma_start(g.nodes[bass.ds(c * (GROUP * P), GROUP * P), :]
                                     .rearrange("(b p) d -> p b d", p=P),
                                     g.X[:, bass.ds(c * GROUP, GROUP), :]).then_inc(stored, 16)
                if store:
                    sp.wait_ge(stored, 16 * GROUPS)

            if norm:
                @block.scalar
                def _(act):
                    with act.Fori(0, GROUPS) as c:
                        ln.scalar(act, c, 0)

            @block.vector
            def _(dve):
                dve.wait_ge(bias_in, 16)
                with dve.Fori(0, GROUPS) as c:
                    w = Own(own, c * NV)
                    blocks = bass.ds(c * GROUP, GROUP)
                    s = g.sums[:, blocks, :].rearrange("p b (h r) -> p (b h) r", h=HEADS)
                    r = own_rows[:, :, :].rearrange("p b (h r) -> p (b h) r", h=HEADS)
                    t = T[:, :, :].rearrange("p b (h r) -> p (b h) r", h=HEADS)

                    def wide(a):
                        return a[:, :].unsqueeze(2).to_broadcast([P, GROUP * HEADS, CH])

                    w.step(dve, dve.tensor_tensor(den[:, :], s[:, :, CH + 1], s[:, :, 0], ALU.add))
                    w.step(dve, dve.tensor_scalar(lone[:, :], den[:, :], 0.5, None, ALU.is_lt))
                    w.step(dve, dve.tensor_tensor(self_w[:, :], s[:, :, 0], lone[:, :], ALU.add))
                    w.step(dve, dve.tensor_tensor(den[:, :], den[:, :], lone[:, :], ALU.add))
                    w.step(dve, dve.tensor_scalar(den[:, :], den[:, :], 1e-16, None, guard))
                    w.step(dve, dve.reciprocal(den[:, :], den[:, :]))
                    dve.wait_ge(rows_in, c * 16 + 16)
                    dve.tensor_tensor(t, r[:, :, 1:CH + 1], wide(self_w), ALU.mult)\
                        .then_inc(rows_used, 1)
                    dve.wait_ge(rows_used, c + 1 + FROM)
                    w.step(dve, dve.tensor_tensor(t, t, s[:, :, 1:CH + 1], ALU.add))
                    w.step(dve, dve.tensor_tensor(t, t, wide(den), ALU.mult))
                    w.step(dve, dve.tensor_tensor(
                        T[:, :, :], T[:, :, :],
                        bias_sb[:, :].unsqueeze(1).to_broadcast([P, GROUP, DIM]), ALU.add))
                    if not norm:
                        dve.tensor_scalar(g.sums[:, blocks, 0:DIM], T[:, :, :], 0.0, None, ALU.max)\
                            .then_inc(done, 1)
                    else:
                        x = g.X[:, blocks, :]
                        w.step(dve, dve.tensor_tensor(x, x, T[:, :, :], ALU.add))
                        ln.vector(dve, w, c, 0,
                                  lambda k: flat(g.X[:, bass.ds(c * GROUP + k, 1), :]))
                        dve.sem_inc(done, 1)
                    assert w.n == NV, w.n


def perceptron(nc, sem, g, W1, b1, W2, b2, eps, gamma, beta):
    with Memory(nc) as sb:
        w1 = sb.sb("mlp_w1", [P, 2, DIM], FP32)
        w2 = sb.sb("mlp_w2", [P, 2, DIM], FP32)
        b1c = sb.sb("mlp_b1", [P, 2], FP32)
        vec = sb.sb("mlp_vec", [P, 3, DIM], FP32)
        one_eps = sb.sb("mlp_eps", [P, 1], FP32)
        Z = sb.sb("mlp_z", [P, GROUP, DIM], FP32)
        R = sb.sb("mlp_r", [P, GROUP, DIM], FP32)
        zT = sb.sb("mlp_zt", [P, 2, DIM], FP32)
        hT = sb.sb("mlp_ht", [P, 2, DIM], FP32)
        p_t = sb.ps("mlp_pt", [P, 2, 512])
        p_h = sb.ps("mlp_ph", [P, 2, 512])
        p_z = sb.ps("mlp_pz", [P, 2, 512])
        loaded, own = sem("mlp_loaded"), sem("mlp_own")
        z_ok, turned, copied = sem("mlp_z_ok"), sem("mlp_turned"), sem("mlp_copied")
        hid, hid_ok, mult, evac = sem("mlp_hid"), sem("mlp_hid_ok"), sem("mlp_mult"), sem("mlp_evac")
        ln = Norm(nc, sem, sb, "mlp_norm", 2)
        NV = 1 + 2 + 1 + 2 * Norm.STEPS
        with nc.Block() as block:

            @block.gpsimd
            def _(pool):
                for s in (turned, copied, hid, hid_ok, mult, evac):
                    pool.sem_inc(s, FROM)

            @block.sync
            def _(sp):
                sp.dma_start(w1[:, :, :], W1.rearrange("(k p) n -> p k n", p=P)).then_inc(loaded, 16)
                sp.dma_start(w2[:, :, :], W2.rearrange("(k p) n -> p k n", p=P)).then_inc(loaded, 16)
                for i in range(2):
                    sp.dma_start(b1c[:, i:i + 1], b1[i * P:(i + 1) * P].rearrange("(p a) -> p a", a=1))\
                        .then_inc(loaded, 16)
                for i, a in enumerate((b2, gamma, beta)):
                    sp.dma_start(vec[:, i, :], a.partition_broadcast(P)).then_inc(loaded, 16)
                sp.dma_start(one_eps[:, :], eps.partition_broadcast(P)).then_inc(loaded, 16)

            @block.tensor
            def _(pe):
                pe.wait_ge(loaded, 16 * 8)
                with pe.Fori(0, GROUPS) as c:
                    pe.wait_ge(z_ok, c + 1)
                    for k in range(GROUP + 2):
                        if k < GROUP:
                            pe.wait_ge(copied, free_at(c, k))
                            for i in range(2):
                                last = nc.tensor.transpose(p_t[:, k % 2, i * P:(i + 1) * P],
                                                           Z[:, k, i * P:(i + 1) * P], g.ident[:, :])
                            last.then_inc(turned, 1)
                        if 1 <= k <= GROUP:
                            j = k - 1
                            pe.wait_ge(copied, through(c, j))
                            pe.wait_ge(hid_ok, free_at(c, j))
                            for o in range(2):
                                for i in range(2):
                                    last = nc.tensor.matmul(
                                        p_h[:, j % 2, o * P:(o + 1) * P], w1[:, i, o * P:(o + 1) * P],
                                        zT[:, j % 2, i * P:(i + 1) * P],
                                        start=(i == 0), stop=(i == 1))
                            last.then_inc(hid, 1)
                        if k >= 2:
                            j = k - 2
                            pe.wait_ge(hid_ok, through(c, j))
                            pe.wait_ge(evac, free_at(c, j))
                            for i in range(2):
                                last = nc.tensor.matmul(p_z[:, j % 2, 0:DIM],
                                                        hT[:, j % 2, i * P:(i + 1) * P],
                                                        w2[:, i, :], start=(i == 0), stop=(i == 1))
                            last.then_inc(mult, 1)

            @block.scalar
            def _(act):
                act.wait_ge(loaded, 16 * 8)
                with act.Fori(0, GROUPS) as c:
                    for k in range(GROUP + 1):
                        if k < GROUP:
                            act.wait_ge(turned, through(c, k))
                            act.wait_ge(hid, free_at(c, k))
                            act.activation(zT[:, k % 2, :], p_t[:, k % 2, 0:DIM], ACT.Copy)\
                                .then_inc(copied, 1)
                        if k:
                            j = k - 1
                            act.wait_ge(hid, through(c, j))
                            act.wait_ge(mult, free_at(c, j))
                            for o in range(2):
                                last = act.activation(hT[:, j % 2, o * P:(o + 1) * P],
                                                      p_h[:, j % 2, o * P:(o + 1) * P], ACT.Relu,
                                                      bias=b1c[:, o:o + 1])
                            last.then_inc(hid_ok, 1)
                    for n in range(2):
                        ln.scalar(act, c, n)

            @block.vector
            def _(dve):
                dve.wait_ge(loaded, 16 * 8)
                o = Own(own)
                o.step(dve, dve.tensor_scalar(one_eps[:, :], one_eps[:, :], 1.0, None, ALU.add))

                def every(i):
                    return vec[:, i:i + 1, :].to_broadcast([P, GROUP, DIM])

                with dve.Fori(0, GROUPS) as c:
                    w = Own(own, c * NV + 1)
                    blocks = bass.ds(c * GROUP, GROUP)
                    x = g.X[:, blocks, :]
                    dve.scalar_tensor_tensor(out=Z[:, :, :], in0=x, scalar=one_eps[:, 0:1],
                                             in1=g.sums[:, blocks, 0:DIM], op0=ALU.mult,
                                             op1=ALU.add).then_inc(z_ok, 1)
                    w.step(dve, dve.tensor_tensor(R[:, :, :], x, every(0), ALU.add))
                    for k in range(GROUP):
                        dve.wait_ge(mult, through(c, k))
                        dve.tensor_tensor(R[:, k, :], R[:, k, :], p_z[:, k % 2, 0:DIM], ALU.add)\
                            .then_inc(evac, 1)
                    dve.wait_ge(evac, through(c, GROUP - 1))
                    ln.vector(dve, w, c, 0, lambda k: R[:, k, :])
                    w.step(dve, dve.tensor_tensor(R[:, :, :], R[:, :, :], every(1), ALU.mult))
                    w.step(dve, dve.tensor_tensor(R[:, :, :], R[:, :, :], every(2), ALU.add))
                    w.step(dve, dve.scalar_tensor_tensor(out=x, in0=R[:, :, :], scalar=0.0, in1=x,
                                                         op0=ALU.max, op1=ALU.add))
                    ln.vector(dve, w, c, 1, lambda k: flat(g.X[:, bass.ds(c * GROUP + k, 1), :]))
                    assert w.n == NV, w.n


def transform(nc, sem, g, weight):
    PAIR = 2
    with Memory(nc) as sb:
        w3 = sb.sb("rel_w", [P, 2, RELS, DIM], FP32)
        x_in = sb.sb("rel_x_in", [P, 2, DIM], FP32)
        xT = sb.sb("rel_xt", [P, 2, DIM], FP32)
        out = sb.sb("rel_out", [P, RELS, DIM], FP32)
        p_t = sb.ps("rel_pt", [P, 2, 512])
        p_y = sb.ps("rel_py", [P, 4, PAIR * DIM])
        loaded, x_ok = sem("rel_loaded"), [sem("rel_x_ok0"), sem("rel_x_ok1")]
        turned, copied, mult = sem("rel_turned"), sem("rel_copied"), sem("rel_mult")
        by_act, by_dve, put = sem("rel_by_act"), sem("rel_by_dve"), [sem("rel_put0"), sem("rel_put1")]
        out_free = [sem("rel_out_free0"), sem("rel_out_free1")]
        NP2 = RELS // PAIR
        HALF = NP2 // 2
        y = g.by_rel.rearrange("(r n) d -> n r d", n=PADN)
        with nc.Block() as block:

            @block.gpsimd
            def _(pool):
                for s in (by_act, by_dve, *out_free):
                    pool.sem_inc(s, FROM)
                with pool.Fori(0, BLOCKS) as j:
                    for half in range(2):
                        pool.wait_ge(put[half], j * 16 + 16)
                        pool.sem_inc(out_free[half], 1)

            @block.sync
            def _(sp):
                for i in range(2):
                    sp.dma_start(w3[:, i, :, :],
                                 weight[:, i * P:(i + 1) * P, :].rearrange("r p d -> p r d"))\
                        .then_inc(loaded, 16)
                def load_x(j, k):
                    sp.dma_start(x_in[:, k, :], flat(g.X[:, bass.ds(j, 1), :])).then_inc(x_ok[k], 16)

                def store(j):
                    for half in range(2):
                        sp.wait_ge(by_act, j * HALF + (half + 1) * (HALF // 2) + FROM)
                        sp.wait_ge(by_dve, j * HALF + (half + 1) * (HALF // 2) + FROM)
                        r = slice(half * RELS // 2, (half + 1) * RELS // 2)
                        sp.dma_start(y[bass.ds(j * P, P), r, :], out[:, r, :]).then_inc(put[half], 16)

                load_x(0, 0)
                load_x(1, 1)
                with sp.Fori(0, BLOCKS // 2 - 1) as i:
                    for k in range(2):
                        sp.wait_ge(turned, i * 2 + k + 1)
                        load_x(i * 2 + k + 2, k)
                        store(i * 2 + k)
                sp.wait_ge(turned, BLOCKS - 2)
                load_x(BLOCKS - 1, 0)
                for j in range(BLOCKS - 3, BLOCKS):
                    store(j)
                for half in range(2):
                    sp.wait_ge(put[half], 16 * BLOCKS)

            @block.tensor
            def _(pe):
                def turn_over(j, u, k):
                    pe.wait_ge(x_ok[k], u * 16 + 16)
                    for i in range(2):
                        last = nc.tensor.transpose(p_t[:, k, i * P:(i + 1) * P],
                                                   x_in[:, k, i * P:(i + 1) * P], g.ident[:, :])
                    last.then_inc(turned, 1)

                def products(j, i, k, more):
                    pe.wait_ge(copied, j + 1)
                    if more:
                        turn_over(j + 1, i + k, 1 - k)
                    for n in range(NP2):
                        reader = (by_act, by_dve)[n % 2]
                        pe.wait_ge(reader, j * HALF + (max(n // 2 - 1, 0) + FROM))
                        for r in range(PAIR):
                            for f in range(2):
                                last = nc.tensor.matmul(
                                    p_y[:, n % 4, r * DIM:(r + 1) * DIM],
                                    xT[:, k, f * P:(f + 1) * P], w3[:, f, n * PAIR + r, :],
                                    start=(f == 0), stop=(f == 1))
                        last.then_inc(mult, 1)

                pe.wait_ge(loaded, 32)
                turn_over(0, 0, 0)
                with pe.Fori(0, BLOCKS // 2) as i:
                    for k in range(2):
                        products(i * 2 + k, i, k, True)
                products(BLOCKS - 1, BLOCKS // 2, 0, False)

            def read_out(eng, copy, mine, sign, j):
                for n in range(mine, NP2, 2):
                    if n in (mine, mine + 4):
                        eng.wait_ge(out_free[n // 4], j + FROM)
                    eng.wait_ge(mult, j * NP2 + n + 1)
                    copy(out[:, n * PAIR:(n + 1) * PAIR, :].rearrange("p r d -> p (r d)"),
                         p_y[:, n % 4, :]).then_inc(sign, 1)

            @block.scalar
            def _(act):
                def copy(a, b):
                    return act.activation(a, b, ACT.Copy)

                def turn(j, k):
                    act.wait_ge(turned, j + 1)
                    copy(xT[:, k, :], p_t[:, k, 0:DIM]).then_inc(copied, 1)

                turn(0, 0)
                with act.Fori(0, BLOCKS // 2) as i:
                    for k in range(2):
                        turn(i * 2 + k + 1, 1 - k)
                        read_out(act, copy, 0, by_act, i * 2 + k)
                read_out(act, copy, 0, by_act, BLOCKS - 1)

            @block.vector
            def _(dve):
                with dve.Fori(0, BLOCKS) as j:
                    read_out(dve, dve.tensor_copy, 1, by_dve, j)


def last_norm(nc, sem, g, out):
    with Memory(nc) as sb:
        own, done, stored = sem("end_own"), sem("end_done"), sem("end_stored")
        ln = Norm(nc, sem, sb, "end", 1)
        NV = 1 + Norm.STEPS
        with nc.Block() as block:

            @block.sync
            def _(sp):
                with sp.Fori(0, GROUPS - 1) as c:
                    sp.wait_ge(done, c + 1)
                    sp.dma_start(out[bass.ds(c * (GROUP * P), GROUP * P), :]
                                 .rearrange("(b p) d -> p b d", p=P),
                                 g.X[:, bass.ds(c * GROUP, GROUP), :]).then_inc(stored, 16)
                sp.wait_ge(done, GROUPS)
                a, z = (GROUPS - 1) * GROUP, BLOCKS - 1
                sp.dma_start(out[a * P:z * P, :].rearrange("(b p) d -> p b d", p=P), g.X[:, a:z, :])\
                    .then_inc(stored, 16)
                sp.dma_start(out[z * P:NODES, :], g.X[0:LAST, z, :]).then_inc(stored, 16)
                sp.wait_ge(stored, 16 * (GROUPS + 1))

            @block.scalar
            def _(act):
                with act.Fori(0, GROUPS) as c:
                    ln.scalar(act, c, 0)

            @block.vector
            def _(dve):
                with dve.Fori(0, GROUPS) as c:
                    w = Own(own, c * NV)
                    x = g.X[:, bass.ds(c * GROUP, GROUP), :]
                    w.step(dve, dve.tensor_tensor(x, x, g.sums[:, bass.ds(c * GROUP, GROUP), 0:DIM],
                                                  ALU.add))
                    ln.vector(dve, w, c, 0, lambda k: flat(g.X[:, bass.ds(c * GROUP + k, 1), :]))
                    dve.sem_inc(done, 1)
                    assert w.n == NV, w.n


class Kept:

    def __init__(self, nc, sb):
        self.X = sb.sb("x", [P, BLOCKS, DIM], FP32)
        self.sums = sb.sb("sums", [P, BLOCKS, ROW], FP32)
        self.scores = sb.sb("scores", [P, BLOCKS, 3, 2 * HEADS], BF16)
        self.rows = sb.sb("src_rows", [P, STEPP], U32)
        self.rel_rows = sb.sb("rel_rows", [P, STEPP], U32)
        self.place = sb.sb("place", [P, STEPP], FP32)
        self.edge_w = sb.sb("edge_w", [P, STEPP], FP32)
        self.follows = sb.sb("follows", [P, STEPP], BF16)
        self.starts = sb.sb("starts", [P, STEPP], BF16)
        self.ends = sb.sb("ends", [P, STEPP], BF16)
        self.goes_on = sb.sb("goes_on", [P, STEPP], BF16)
        self.opens = sb.sb("opens", [P, BATCHES], FP32)
        self.gates = sb.sb("gates", [P, BATCHES, HEADS * (K + 1)], BF16)
        self.gates_back = sb.sb("gates_back", [P, BATCHES, HEADS * (K + 1)], BF16)
        self.block_of = sb.sb("block_of", [1, STEPP], I32)
        self.iota_f = sb.sb("iota_f", [P, P], FP32)
        self.iota_p = sb.sb("iota_p", [P, 1], FP32)
        self.ident = sb.sb("ident", [P, P], FP32)
        self.ones32 = sb.sb("ones32", [K * HEADS, P], FP32)
        self.table = nc.dram_tensor("gat_rows", [PADN, ROW], FP32).ap()
        self.nodes = nc.dram_tensor("node_rows", [PADN, DIM], FP32).ap()
        self.by_rel = nc.dram_tensor("relation_rows", [RELS * PADN, DIM], FP32).ap()
        self.marks = nc.dram_tensor("segment_marks", [CPAD, HEADS, P + 1], FP32).ap()
        self.places = nc.dram_tensor("places_in_block", [CPAD, P], BF16).ap()


def graph_layers(nc, a, out, stages=99):
    keep = Memory(nc)
    with keep as sb:
        used = []

        def sem(name):
            used.append(nc.alloc_semaphore(name))
            return used[-1]

        g = Kept(nc, sb)
        todo = [
            lambda: lay_out_walk(nc, sem, g, a["src"], a["dst"], a["edge_type_16"],
                                 a["edge_weight1"]),
            lambda: load_nodes(nc, sem, g, a["x"]),
            lambda: project(nc, sem, g, "p0", g.X, a["L0_gnn_W"], a["L0_gnn_att_src"]
                            .rearrange("h c -> (h c)"), a["L0_gnn_att_dst"].rearrange("h c -> (h c)")),
            lambda: aggregate_attention(nc, sem, g, "a0"),
            lambda: finish_attention(nc, sem, g, "f0", a["L0_gnn_bias"], ALU.add, True, True),
            lambda: aggregate(nc, sem, g, "a1", g.nodes, g.rows, None),
            lambda: perceptron(nc, sem, g, a["L1_gnn_W1"], a["L1_gnn_b1"], a["L1_gnn_W2"],
                               a["L1_gnn_b2"], a["L1_gnn_eps"], a["L1_gnn_gamma"],
                               a["L1_gnn_beta"]),
            lambda: project(nc, sem, g, "p2", g.X, a["L2_gnn_W1"], a["L2_gnn_att_src1"]
                            .rearrange("a h c -> (a h c)"), a["L2_gnn_att_dst1"]
                            .rearrange("a h c -> (a h c)")),
            lambda: aggregate_attention(nc, sem, g, "a2"),
            lambda: finish_attention(nc, sem, g, "f2", a["L2_gnn_b1"], ALU.max, False, False),
            lambda: project(nc, sem, g, "p3", g.sums, a["L2_gnn_W2"], a["L2_gnn_att_src2"]
                            .rearrange("a h c -> (a h c)"), a["L2_gnn_att_dst2"]
                            .rearrange("a h c -> (a h c)")),
            lambda: aggregate_attention(nc, sem, g, "a3"),
            lambda: finish_attention(nc, sem, g, "f3", a["L2_gnn_b2"], ALU.max, True, False),
            lambda: transform(nc, sem, g, a["L3_gnn_weight"]),
            lambda: aggregate(nc, sem, g, "a4", g.by_rel, g.rel_rows, g.edge_w),
            lambda: last_norm(nc, sem, g, out),
        ]
        for stage in todo[:stages]:
            stage()
            nc.clear_and_free_semaphores(used)
            used.clear()
            nc.all_engine_barrier()
        return g


INPUTS = ["x", "src", "dst", "edge_type_16", "edge_weight1", "L0_gnn_W", "L0_gnn_att_src",
          "L0_gnn_att_dst", "L0_gnn_bias", "L1_gnn_W1", "L1_gnn_b1", "L1_gnn_W2", "L1_gnn_b2",
          "L1_gnn_eps", "L1_gnn_gamma", "L1_gnn_beta", "L2_gnn_W1", "L2_gnn_att_src1",
          "L2_gnn_att_dst1", "L2_gnn_b1", "L2_gnn_W2", "L2_gnn_att_src2", "L2_gnn_att_dst2",
          "L2_gnn_b2", "L3_gnn_weight"]


def kernel(**inputs):
    import numpy as np
    import concourse.bacc as bacc
    from concourse.bass_utils import run_bass_kernel_spmd

    nc = bacc.Bacc("TRN2", target_bir_lowering=False, num_devices=1)
    arrays, args = {}, {}
    for name in INPUTS:
        v = np.ascontiguousarray(np.asarray(inputs[name]))
        if name == "L1_gnn_eps":
            v = v.reshape(1)
        arrays[name] = v
        args[name] = nc.dram_tensor(name, v.shape, mybir.dt.from_np(v.dtype),
                                    kind="ExternalInput").ap()
    out = nc.dram_tensor("out", [NODES, DIM], FP32, kind="ExternalOutput").ap()
    graph_layers(nc, args, out)
    got = run_bass_kernel_spmd(nc, [arrays], core_ids=[0])
    return got.results[0]["out"]
```

```python
from contextlib import ExitStack

import concourse.bass as bass
from concourse import mybir

FP32 = mybir.dt.float32
BF16 = mybir.dt.bfloat16
I32 = mybir.dt.int32
U32 = mybir.dt.uint32
ALU = mybir.AluOpType
ACT = mybir.ActivationFunctionType
AX = mybir.AxisListType
ENG = mybir.EngineType

P = 128
NODES, EDGES, DIM = 6250, 106250, 256
HEADS, CH = 4, 64
RELS = 16
BLOCKS = -(-NODES // P)
LAST = NODES - (BLOCKS - 1) * P
PADN = BLOCKS * P
TILES = -(-EDGES // P)
TAIL = EDGES - (TILES - 1) * P
STEPS = TILES + BLOCKS - 1
K = 15
BATCHES = -(-STEPS // K)
STEPP = BATCHES * K
CHUNKS = -(-STEPP // P)
CPAD = CHUNKS * P
SLOTS = 3
RING = 5
HC = CH + 3
ROW = HEADS * HC
GROUP = 7
GROUPS = BLOCKS // GROUP
BIG = 1.0e30
NOWHERE = 1 << 20
LN_EPS = 1e-5
SLOPE = 0.2
SKIP = "block numbers are counts of 48 comparisons, so 0..48"


def flat(ap):
    return ap.rearrange("p a b -> p (a b)")


class Memory(ExitStack):

    def __init__(self, nc):
        super().__init__()
        self.nc = nc

    def sb(self, name, shape, dtype):
        return self.enter_context(self.nc.sbuf_tensor(f"sb_{name}", shape, dtype))

    def ps(self, name, shape):
        return self.enter_context(self.nc.psum_tensor(f"ps_{name}", shape, FP32))


class Own:

    def __init__(self, sem, base=0):
        self.sem, self.n, self.base = sem, 0, base

    def inc(self, ins):
        self.n += 1
        ins.then_inc(self.sem, 1)
        return self.base + self.n

    def settle(self, eng):
        eng.wait_ge(self.sem, self.base + self.n)

    def step(self, eng, ins):
        self.inc(ins)
        self.settle(eng)


def lay_out_walk(nc, sem, g, src, dst, etype, weight):
    W = 3 * P + 1
    tab = nc.dram_tensor("edge_table", [TILES + 1, W], I32).ap()
    wtab = nc.dram_tensor("weight_table", [TILES + 1, P], FP32).ap()
    full = (TILES - 1) * P
    with Memory(nc) as sb:
        fill_i = sb.sb("w_fill_i", [1, 4 * P], I32)
        fill_f = sb.sb("w_fill_f", [1, 2 * P], FP32)
        first_i = sb.sb("w_first_i", [1, TILES], I32)
        first_f = sb.sb("w_first_f", [1, TILES], FP32)
        ones = sb.sb("w_ones", [P, P], FP32)
        thr = sb.sb("w_thr", [P, 1], FP32)
        pid = sb.sb("w_pid", [P, 1], FP32)
        cmp = sb.sb("w_cmp", [P, TILES], FP32)
        cnt = sb.sb("w_cnt", [P, 4], FP32)
        sidx = sb.sb("w_sidx", [P, CPAD + 1], FP32)
        ind = sb.sb("w_ind", [P, CPAD + 1], FP32)
        bcol = sb.sb("w_bcol", [P, 2 * CHUNKS], FP32)
        newt = sb.sb("w_newt", [P, CHUNKS], FP32)
        sid = sb.sb("w_sid", [P, CHUNKS], FP32)
        tid_f = sb.sb("w_tid_f", [P, CHUNKS], FP32)
        tid = sb.sb("w_tid", [P, CHUNKS], U32)
        rowi = sb.sb("w_rowi", [P, CHUNKS, W], I32)
        roww = sb.sb("w_roww", [P, CHUNKS, P], FP32)
        room = flat(g.X[:, :, :])
        arr = room[:, 0:7 * CPAD].rearrange("p (a c e) -> p a c e", a=7, c=CHUNKS)
        rowf = room[:, 7 * CPAD:7 * CPAD + CHUNKS * W].rearrange("p (c e) -> p c e", c=CHUNKS)
        mrow = sb.sb("w_mrow", [P, CHUNKS, P + 1], FP32)
        dlb = sb.sb("w_dlb", [P, CHUNKS, P], BF16)
        small = sb.sb("w_small", [P, 3, CHUNKS], FP32)
        diags = sb.sb("w_diags", [P, 2, P], FP32)
        along = sb.sb("w_along", [P, 2, STEPP], FP32)
        on_first = sb.sb("w_on_first", [P, 1], FP32)
        p_first = sb.ps("w_p_first", [P, 1024])
        p_bcol = sb.ps("w_p_bcol", [P, 512])
        p_brow = sb.ps("w_p_brow", [1, 1024])
        p_tr = sb.ps("w_p_tr", [P, 2, 512])
        filled, first_in, const = sem("w_filled"), sem("w_first_in"), sem("w_const")
        tabbed, first_bc, starts = sem("w_tabbed"), sem("w_first_bc"), sem("w_starts")
        bdone, tids, rows_in = sem("w_bdone"), sem("w_tids"), sem("w_rows_in")
        own, marked, turned = sem("w_own"), sem("w_marked"), sem("w_turned")
        saved, stored = sem("w_saved"), sem("w_stored")
        NARR = 7
        with nc.Block() as block:

            @block.gpsimd
            def _(pool):
                pool.memset(fill_i[:, 0:2 * P], 0).then_inc(filled, 1)
                pool.memset(fill_i[:, 2 * P:4 * P], NOWHERE).then_inc(filled, 1)
                pool.memset(fill_f[:, :], 0.0).then_inc(filled, 1)
                pool.memset(ones[:, :], 1.0).then_inc(const, 1)
                pool.iota(thr[:, :], [[0, 1]], base=P, channel_multiplier=P,
                          allow_small_or_imprecise_dtypes=True).then_inc(const, 1)
                pool.iota(pid[:, :], [[0, 1]], base=0, channel_multiplier=1,
                          allow_small_or_imprecise_dtypes=True).then_inc(const, 1)
                pool.iota(sidx[:, :], [[1, CPAD + 1]], base=-1, channel_multiplier=0,
                          allow_small_or_imprecise_dtypes=True).then_inc(const, 1)
                pool.iota(sid[:, :], [[P, CHUNKS]], base=0, channel_multiplier=1,
                          allow_small_or_imprecise_dtypes=True).then_inc(const, 1)
                pool.iota(g.iota_f[:, :], [[1, P]], base=0, channel_multiplier=0,
                          allow_small_or_imprecise_dtypes=True).then_inc(const, 1)
                pool.iota(g.iota_p[:, :], [[0, 1]], base=0, channel_multiplier=1,
                          allow_small_or_imprecise_dtypes=True).then_inc(const, 1)
                pool.memset(g.ones[:, :], 1.0).then_inc(const, 1)
                pool.memset(g.ident[:, :], 0.0).then_inc(const, 1)
                pool.wait_ge(const, 9)
                pool.affine_select(out=g.ident[:, :], in_=g.ident[:, :], compare_op=ALU.not_equal,
                                   fill=1.0, base=0, pattern=[[-1, P]], channel_multiplier=1)\
                    .then_inc(const, 1)
                pool.wait_ge(tids, 1)
                pool.wait_ge(tabbed, 16 * 17)
                for c in range(CHUNKS):
                    off = bass.IndirectOffsetOnAxis(ap=tid[:, c:c + 1], axis=0)
                    pool.indirect_dma_start(out=rowi[:, c, :], out_offset=None, in_=tab,
                                            in_offset=off).then_inc(rows_in, 16)
                    pool.indirect_dma_start(out=roww[:, c, :], out_offset=None, in_=wtab,
                                            in_offset=off).then_inc(rows_in, 16)
                pool.wait_ge(rows_in, 32 * CHUNKS)

            @block.sync
            def _(sp):
                sp.dma_start(first_i[:, :], dst.rearrange("(a n) -> a n", a=1)[:, 0:EDGES:P],
                             allow_slow_non_contiguous=True)\
                    .then_inc(first_in, 16)
                for at, a in ((0, src), (P, etype), (2 * P + 1, dst)):
                    sp.dma_start(tab[0:TILES - 1, at:at + P],
                                 a[0:full].rearrange("(t e) -> t e", e=P)).then_inc(tabbed, 16)
                    sp.dma_start(tab[TILES - 1:TILES, at:at + TAIL],
                                 a[full:EDGES].rearrange("(t e) -> t e", t=1)).then_inc(tabbed, 16)
                sp.dma_start(tab[1:TILES, 2 * P:2 * P + 1],
                             dst[P - 1:full].rearrange("(t e) -> t e", e=1)[0:full - P + 1:P, :],
                             allow_slow_non_contiguous=True)\
                    .then_inc(tabbed, 16)
                sp.dma_start(wtab[0:TILES - 1, :],
                             weight[0:full, 0].rearrange("(t e) -> t e", e=P)).then_inc(tabbed, 16)
                sp.dma_start(wtab[TILES - 1:TILES, 0:TAIL],
                             weight[full:EDGES, 0].rearrange("(t e) -> t e", t=1))\
                    .then_inc(tabbed, 16)
                sp.wait_ge(filled, 3)
                sp.dma_start(tab[TILES - 1:TILES, TAIL:P], fill_i[:, 0:P - TAIL]).then_inc(tabbed, 16)
                sp.dma_start(tab[TILES - 1:TILES, P + TAIL:2 * P], fill_i[:, 0:P - TAIL])\
                    .then_inc(tabbed, 16)
                sp.dma_start(tab[TILES - 1:TILES, 2 * P + 1 + TAIL:W],
                             fill_i[:, 2 * P:3 * P - TAIL]).then_inc(tabbed, 16)
                sp.dma_start(wtab[TILES - 1:TILES, TAIL:P], fill_f[:, 0:P - TAIL])\
                    .then_inc(tabbed, 16)
                sp.dma_start(tab[TILES:TILES + 1, 0:2 * P], fill_i[:, 0:2 * P]).then_inc(tabbed, 16)
                sp.dma_start(tab[TILES:TILES + 1, 2 * P:W], fill_i[:, 2 * P:3 * P + 1])\
                    .then_inc(tabbed, 16)
                sp.dma_start(tab[0:1, 2 * P:2 * P + 1], fill_i[:, 3 * P + 2:3 * P + 3])\
                    .then_inc(tabbed, 16)
                sp.dma_start(wtab[TILES:TILES + 1, :], fill_f[:, P:2 * P]).then_inc(tabbed, 16)
                sp.wait_ge(marked, 1)
                for h in range(HEADS):
                    sp.dma_start(g.marks[:, h, :].rearrange("(c p) e -> p c e", p=P), mrow[:, :, :])\
                        .then_inc(stored, 16)
                sp.dma_start(g.places.rearrange("(c p) e -> p c e", p=P), dlb[:, :, :])\
                    .then_inc(stored, 16)
                sp.wait_ge(stored, 16 * (HEADS + 1))

            @block.tensor
            def _(pe):
                pe.wait_ge(const, 1)
                pe.wait_ge(own, 1)
                for a in range(0, TILES, 512):
                    z = min(a + 512, TILES)
                    last = nc.tensor.matmul(p_first[:, a:z], ones[0:1, :], first_f[0:1, a:z],
                                            start=True, stop=True)
                last.then_inc(first_bc, 1)
                pe.wait_ge(starts, 1)
                for c in range(CHUNKS):
                    for late in (0, 1):
                        nc.tensor.matmul(p_bcol[:, 2 * c + late:2 * c + late + 1],
                                         ind[0:BLOCKS - 1, c * P + late:(c + 1) * P + late],
                                         ones[0:BLOCKS - 1, 0:1], start=True, stop=True)
                for a in range(0, STEPP, 512):
                    z = min(a + 512, STEPP)
                    last = nc.tensor.matmul(p_brow[0:1, a:z], ones[0:BLOCKS - 1, 0:1],
                                            ind[0:BLOCKS - 1, a + 1:z + 1], start=True, stop=True)
                last.then_inc(bdone, 1)
                pe.wait_ge(marked, 1)
                pe.wait_ge(const, 10)
                n = 0
                for a in range(NARR):
                    for c in range(CHUNKS):
                        if n >= 2:
                            pe.wait_ge(saved, n - 1)
                        nc.tensor.transpose(p_tr[:, n % 2, 0:P], arr[:, a, c, :], g.ident[:, :])\
                            .then_inc(turned, 1)
                        n += 1

            @block.scalar
            def _(act):
                n = 0
                for a in range(NARR):
                    out = (g.rows, g.rel_rows, g.place, g.edge_w, g.follows, g.starts, g.ends)[a]
                    for c in range(CHUNKS):
                        z = min((c + 1) * P, STEPP)
                        n += 1
                        act.wait_ge(turned, n)
                        act.activation(out[:, c * P:z], p_tr[:, (n - 1) % 2, 0:z - c * P],
                                       ACT.Copy).then_inc(saved, 1)

            @block.vector
            def _(dve):
                w = Own(own)
                dve.wait_ge(first_in, 16)
                w.step(dve, dve.tensor_copy(first_f[:, :], first_i[:, :]))
                dve.wait_ge(const, 8)
                dve.wait_ge(first_bc, 1)
                for n, a in enumerate(range(0, TILES, 512)):
                    z = min(a + 512, TILES)
                    w.step(dve, dve.tensor_scalar(cmp[:, a:z], p_first[:, a:z], thr[:, 0:1], None,
                                                  ALU.is_lt, ALU.add, accum_out=cnt[:, n:n + 1]))
                w.step(dve, dve.tensor_tensor(cnt[:, 0:1], cnt[:, 0:1], cnt[:, 1:2], ALU.add))
                w.step(dve, dve.tensor_scalar(cnt[:, 2:3], cnt[:, 0:1], 1.0, pid[:, 0:1],
                                              ALU.max, ALU.add))
                dve.tensor_scalar(ind[:, :], sidx[:, :], cnt[:, 2:3], None, ALU.is_ge)\
                    .then_inc(starts, 1)
                dve.wait_ge(bdone, 1)
                w.step(dve, dve.tensor_copy(bcol[:, :], p_bcol[:, 0:2 * CHUNKS]))
                w.step(dve, dve.tensor_copy(g.block_of[0:1, :], p_brow[0:1, 0:STEPP]))
                b = bcol[:, :].rearrange("p (c l) -> p c l", l=2)
                w.step(dve, dve.tensor_tensor(tid_f[:, :], sid[:, :], b[:, :, 1], ALU.subtract))
                w.step(dve, dve.tensor_scalar(tid_f[:, :], tid_f[:, :], float(TILES), None, ALU.min))
                dve.tensor_copy(tid[:, :], tid_f[:, :]).then_inc(tids, 1)
                w.step(dve, dve.tensor_tensor(newt[:, :], b[:, :, 0], b[:, :, 1], ALU.is_equal))
                dve.wait_ge(rows_in, 32 * CHUNKS)
                w.step(dve, dve.tensor_copy(rowf[:, :, :], rowi[:, :, :]))
                srcs, types = rowf[:, :, 0:P], rowf[:, :, P:2 * P]
                prev, dsts = rowf[:, :, 2 * P:3 * P], rowf[:, :, 2 * P + 1:W]
                first = rowf[:, :, 2 * P + 1:2 * P + 2]
                rows_a, rel_a, place_a, w_a, foll_a, st_a, end_a = (arr[:, a] for a in range(NARR))
                cont, one, gate = small[:, 0], small[:, 1], small[:, 2]
                w.step(dve, dve.tensor_tensor(cont, rowf[:, :, 2 * P], rowf[:, :, 2 * P + 1],
                                              ALU.is_equal))
                w.step(dve, dve.tensor_tensor(cont, cont, newt[:, :], ALU.mult))
                w.step(dve, dve.tensor_tensor(one, rowf[:, :, 2 * P + 1], rowf[:, :, W - 1],
                                              ALU.is_equal))
                w.step(dve, dve.tensor_tensor(one, one, cont, ALU.mult))
                w.step(dve, dve.tensor_scalar(gate, one, BIG, -BIG, ALU.mult, ALU.add))
                w.step(dve, dve.tensor_copy(rows_a, srcs))
                w.step(dve, dve.scalar_tensor_tensor(out=rel_a, in0=types, scalar=float(PADN),
                                                     in1=srcs, op0=ALU.mult, op1=ALU.add))
                w.step(dve, dve.tensor_scalar(tid_f[:, :], b[:, :, 1], -float(P), None, ALU.mult))
                for c in range(CHUNKS):
                    w.step(dve, dve.tensor_scalar(place_a[:, c, :], dsts[:, c, :], tid_f[:, c:c + 1],
                                                  None, ALU.add))
                w.step(dve, dve.tensor_copy(w_a, roww[:, :, :]))
                w.step(dve, dve.tensor_scalar(dlb[:, :, :], place_a, -1.0, float(P), ALU.max, ALU.min))
                w.step(dve, dve.tensor_tensor(st_a, dsts, prev, ALU.not_equal))
                w.step(dve, dve.memset(mrow[:, :, P:P + 1], 0.0))
                w.step(dve, dve.tensor_scalar(mrow[:, :, 0:P], st_a, -BIG, None, ALU.mult))
                for c in range(CHUNKS):
                    w.step(dve, dve.tensor_scalar(foll_a[:, c, :], dsts[:, c, :], first[:, c, :],
                                                  cont[:, c:c + 1], ALU.is_equal, ALU.mult))
                w.step(dve, dve.tensor_scalar(foll_a, foll_a, BIG, -BIG, ALU.mult, ALU.add))
                for c in range(CHUNKS):
                    w.step(dve, dve.tensor_scalar(end_a[:, c, :], dsts[:, c, :],
                                                  rowf[:, c, W - 1:W], None, ALU.is_equal))
                w.step(dve, dve.tensor_scalar(end_a, end_a, BIG, -BIG, ALU.mult, ALU.add))
                dve.drain().then_inc(marked, 1)
        gd, gt, gs = sem("w_gate_diag"), sem("w_gate_turned"), sem("w_gate_saved")
        with nc.Block() as block:

            @block.vector
            def _(dve):
                for c in range(CHUNKS):
                    z = min((c + 1) * P, STEPP)
                    for i, what in enumerate((small[:, 2], small[:, 0])):
                        dve.tensor_scalar(diags[:, i, :], g.ident[:, :], what[:, c:c + 1], None,
                                          ALU.mult).then_inc(gd, 1)
                    dve.wait_ge(gt, c + 1)
                    dve.tensor_copy(along[:, :, c * P:z],
                                    p_first[:, 0:2 * P].rearrange("p (i s) -> p i s", i=2)
                                    [:, :, 0:z - c * P]).then_inc(gs, 1)
                dve.wait_ge(gs, CHUNKS)
                by_batch = along[:, 0, :].rearrange("p (q k) -> p q k", k=K)
                for gates, tiles in ((g.gates, by_batch), (g.gates_back, by_batch[:, :, ::-1])):
                    dve.memset(gates[:, :, 0::K + 1], -BIG)
                    for h in range(HEADS):
                        dve.tensor_copy(gates[:, :, h * (K + 1) + 1:(h + 1) * (K + 1)], tiles)
                dve.tensor_scalar(g.goes_on[:, :], along[:, 1, :], BIG, -BIG, ALU.mult, ALU.add)
                dve.tensor_scalar(on_first[:, :], pid[:, :], 0.0, None, ALU.is_equal)\
                    .then_inc(gs, 1)
                dve.wait_ge(gs, CHUNKS + 1)
                dve.tensor_scalar(g.opens[:, :], along[:, 1, 0:STEPP:K], on_first[:, 0:1], None,
                                  ALU.mult)

            @block.tensor
            def _(pe):
                for c in range(CHUNKS):
                    pe.wait_ge(gd, 2 * c + 2)
                    if c:
                        pe.wait_ge(gs, c)
                    for i in range(2):
                        last = nc.tensor.matmul(p_first[:, i * P:(i + 1) * P], ones[:, :],
                                                diags[:, i, :], start=True, stop=True)
                    last.then_inc(gt, 1)


def load_nodes(nc, sem, g, x):
    cleared, loaded = sem("x_cleared"), sem("x_loaded")
    with nc.Block() as block:

        @block.vector
        def _(dve):
            dve.memset(g.X[:, BLOCKS - 1, :], 0.0).then_inc(cleared, 1)

        @block.sync
        def _(sp):
            full = (BLOCKS - 1) * P
            sp.dma_start(g.X[:, 0:BLOCKS - 1, :], x[0:full, :].rearrange("(b p) d -> p b d", p=P))\
                .then_inc(loaded, 16)
            sp.wait_ge(cleared, 1)
            sp.dma_start(g.X[0:LAST, BLOCKS - 1, :], x[full:NODES, :]).then_inc(loaded, 16)
            sp.wait_ge(loaded, 32)


FROM = 1


def free_at(c, k):
    return c * GROUP + (max(k - 1, 0) + FROM)


def through(c, k):
    return c * GROUP + (k + 1 + FROM)


class Projection:
    PARTS = ((0, GROUP // 2 + 1), (GROUP // 2 + 1, GROUP))
    H66 = CH + 2

    def __init__(self, nc, sem, sb, g, tag, y, W, att_src, att_dst, y_done=None, p_t=None):
        self.nc, self.g, self.y, self.y_done = nc, g, y, y_done
        self.W, self.att_src, self.att_dst = W, att_src, att_dst
        self.w_sb = sb.sb(f"{tag}_w", [P, 2, DIM], FP32)
        self.wx = sb.sb(f"{tag}_wx", [P, 2, HEADS * self.H66], FP32)
        self.att = sb.sb(f"{tag}_att", [P, 2, DIM], FP32)
        self.prod = sb.sb(f"{tag}_prod", [P, 2, DIM], FP32)
        self.yT = sb.sb(f"{tag}_yt", [P, 2, DIM], FP32)
        self.y_in = sb.sb(f"{tag}_y_in", [P, GROUP, DIM], FP32)
        self.rows = sb.sb(f"{tag}_rows", [P, GROUP, ROW], FP32)
        self.v = sb.sb(f"{tag}_v", [P, BLOCKS, 2 * HEADS], FP32)
        self.rest = sb.sb(f"{tag}_rest", [P, BLOCKS, 2 * HEADS], FP32)
        self.p_t = sb.ps(f"{tag}_pt", [P, 2, 512]) if p_t is None else p_t
        self.p_y = sb.ps(f"{tag}_py", [P, 2, 512])
        self.loaded, self.ready, self.own = sem(f"{tag}_loaded"), sem(f"{tag}_ready"), sem(f"{tag}_own")
        self.turned, self.copied = sem(f"{tag}_turned"), sem(f"{tag}_copied")
        self.mult, self.evac, self.put = sem(f"{tag}_mult"), sem(f"{tag}_evac"), sem(f"{tag}_put")
        self.rows_free = sem(f"{tag}_rows_free")
        self.y_ok = [sem(f"{tag}_y_ok{i}") for i in range(2)]

    def relay(self, pool):
        for s in (self.turned, self.copied, self.mult, self.evac, self.rows_free):
            pool.sem_inc(s, FROM)
        with pool.Fori(0, GROUPS) as c:
            pool.wait_ge(self.put, c * 16 + 16)
            pool.sem_inc(self.rows_free, 1)

    def load_weights(self, sp):
        sp.dma_start(self.w_sb[:, :, :], self.W.rearrange("(k p) n -> p k n", p=P))\
            .then_inc(self.loaded, 16)
        for i, a in enumerate((self.att_src, self.att_dst)):
            sp.dma_start(self.att[:, i, :], a.partition_broadcast(P)).then_inc(self.loaded, 16)

    def load_next(self, sp, c):
        for i, (a, z) in enumerate(self.PARTS):
            sp.wait_ge(self.turned, c * GROUP + (z + FROM))
            sp.dma_start(self.y_in[:, a:z, :],
                         self.y[:, bass.ds(c * GROUP + (GROUP + a), z - a), 0:DIM])\
                .then_inc(self.y_ok[i], 16)

    def load(self, sp, c):
        if self.y_done is not None:
            sp.wait_ge(self.y_done, c + 1)
        for i, (a, z) in enumerate(self.PARTS):
            sp.wait_ge(self.turned, c * GROUP + FROM)
            sp.dma_start(self.y_in[:, a:z, :], self.y[:, bass.ds(c * GROUP + a, z - a), 0:DIM])\
                .then_inc(self.y_ok[i], 16)

    def store(self, sp, c):
        sp.wait_ge(self.evac, through(c, GROUP - 1))
        sp.dma_start(self.g.table[bass.ds(c * (GROUP * P), GROUP * P), :]
                     .rearrange("(b p) r -> p b r", p=P), self.rows[:, :, :])\
            .then_inc(self.put, 16)

    def tensor(self, pe, c):
        nc, p_t, p_y, yT = self.nc, self.p_t, self.p_y, self.yT
        for k in range(GROUP + 1):
            if k < GROUP:
                for i, (a, z) in enumerate(self.PARTS):
                    if k == a:
                        pe.wait_ge(self.y_ok[i], c * 16 + 16)
                pe.wait_ge(self.copied, free_at(c, k))
                for i in range(2):
                    last = nc.tensor.transpose(p_t[:, k % 2, i * P:(i + 1) * P],
                                               self.y_in[:, k, i * P:(i + 1) * P],
                                               self.g.ident[:, :])
                last.then_inc(self.turned, 1)
            if k:
                pe.wait_ge(self.copied, through(c, k - 1))
                pe.wait_ge(self.evac, free_at(c, k - 1))
                for i in range(2):
                    last = nc.tensor.matmul(p_y[:, (k - 1) % 2, 0:HEADS * self.H66],
                                            yT[:, (k - 1) % 2, i * P:(i + 1) * P],
                                            self.wx[:, i, :], start=(i == 0), stop=(i == 1))
                last.then_inc(self.mult, 1)

    def scalar(self, act, c):
        for k in range(GROUP + 1):
            if k < GROUP:
                act.wait_ge(self.turned, through(c, k))
                act.wait_ge(self.mult, free_at(c, k))
                act.activation(self.yT[:, k % 2, :], self.p_t[:, k % 2, 0:DIM], ACT.Copy)\
                    .then_inc(self.copied, 1)
            if k:
                if k == 1:
                    act.wait_ge(self.rows_free, c + FROM)
                act.wait_ge(self.mult, through(c, k - 1))
                y = self.p_y[:, (k - 1) % 2, 0:HEADS * self.H66]\
                    .rearrange("p (h r) -> p h r", h=HEADS)
                act.activation(
                    self.rows[:, k - 1, :].rearrange("p (h r) -> p h r", h=HEADS)[:, :, 0:CH + 1],
                    y[:, :, 0:CH + 1], ACT.Copy)
                act.activation(
                    self.v[:, bass.ds(c * GROUP + k - 1, 1), :]
                    .rearrange("p b (a h) -> p (b h) a", a=2),
                    y[:, :, 0::CH + 1], ACT.Copy).then_inc(self.evac, 1)

    def prepare(self, dve):
        w, wx, w_sb = Own(self.own), self.wx, self.w_sb
        r = self.rows[:, :, :].rearrange("p b (h r) -> p (b h) r", h=HEADS)
        w.step(dve, dve.memset(r[:, :, CH + 1:CH + 2], 1.0))
        w.step(dve, dve.memset(r[:, :, CH + 2:CH + 3], 0.0))
        dve.wait_ge(self.loaded, 48)
        for k in range(2):
            cols = wx[:, k, :].rearrange("p (h r) -> p h r", h=HEADS)
            w.step(dve, dve.tensor_copy(cols[:, :, 1:CH + 1],
                                        w_sb[:, k, :].rearrange("p (h r) -> p h r", h=HEADS)))
            for i in range(2):
                w.step(dve, dve.tensor_tensor(self.prod[:, k, :], w_sb[:, k, :], self.att[:, i, :],
                                              ALU.mult))
                w.step(dve, dve.tensor_reduce(
                    wx[:, k, i * (CH + 1)::self.H66],
                    self.prod[:, k, :].rearrange("p (h r) -> p h r", h=HEADS), AX.X, ALU.add))
        dve.drain().then_inc(self.ready, 1)
        self.prepared = w.n

    def split(self, dve):
        w = Own(self.own, self.prepared)
        v, rest, sc = self.v, self.rest, self.g.scores
        dve.wait_ge(self.evac, BLOCKS + FROM)
        w.step(dve, dve.tensor_copy(sc[:, :, 0, :], v[:, :, :]))
        w.step(dve, dve.tensor_tensor(rest[:, :, :], v[:, :, :], sc[:, :, 0, :], ALU.subtract))
        w.step(dve, dve.tensor_copy(sc[:, :, 1, :], rest[:, :, :]))
        w.step(dve, dve.tensor_tensor(rest[:, :, :], rest[:, :, :], sc[:, :, 1, :], ALU.subtract))
        w.step(dve, dve.tensor_copy(sc[:, :, 2, :], rest[:, :, :]))


def project(nc, sem, g, tag, y, W, att_src, att_dst):
    with Memory(nc) as sb:
        pr = Projection(nc, sem, sb, g, tag, y, W, att_src, att_dst)
        with nc.Block() as block:

            @block.gpsimd
            def _(pool):
                pr.relay(pool)

            @block.sync
            def _(sp):
                pr.load_weights(sp)
                pr.load(sp, 0)
                with sp.Fori(0, GROUPS - 1) as c:
                    pr.load_next(sp, c)
                    pr.store(sp, c)
                pr.store(sp, GROUPS - 1)
                sp.wait_ge(pr.put, 16 * GROUPS)

            @block.tensor
            def _(pe):
                pe.wait_ge(pr.ready, 1)
                with pe.Fori(0, GROUPS) as c:
                    pr.tensor(pe, c)

            @block.scalar
            def _(act):
                act.wait_ge(pr.ready, 1)
                with act.Fori(0, GROUPS) as c:
                    pr.scalar(act, c)

            @block.vector
            def _(dve):
                pr.prepare(dve)
                pr.split(dve)


def aggregate_attention(nc, sem, g, tag, first=False):
    OHS = RING
    KH = K * HEADS
    HK = K + 1
    CIN, TOP = 2 * KH, 2 * KH + HEADS
    with Memory(nc) as sb:
        G = sb.sb(f"{tag}_rows", [P, SLOTS, K, ROW], FP32)
        idx = sb.sb(f"{tag}_idx", [P, SLOTS, K], U32)
        marks = sb.sb(f"{tag}_marks", [KH, P + 1], FP32)
        if first:
            places = sb.sb(f"{tag}_places", [P, K * P], BF16)
            places_in, t01_kept = sem(f"{tag}_places_in"), sem(f"{tag}_t01_kept")
        turned01 = sb.sb(f"{tag}_turned01", [P, K * P], BF16)
        onehot = sb.sb(f"{tag}_onehot", [P, OHS, P], FP32)
        D = sb.sb(f"{tag}_node_scores", [P, K, 2 * HEADS], FP32)
        sm = sb.sb(f"{tag}_sm", [P, P], FP32)
        fwd = sb.sb(f"{tag}_fwd", [KH, P], FP32)
        seg = sb.sb(f"{tag}_seg", [KH, P], FP32)
        diag = sb.sb(f"{tag}_diag", [KH, 2, KH], FP32)
        last_max = sb.sb(f"{tag}_last_max", [P, HEADS, HK], FP32)
        so_far = sb.sb(f"{tag}_so_far", [P, HEADS, HK], FP32)
        first_max = sb.sb(f"{tag}_first_max", [P, HEADS, HK], FP32)
        final = sb.sb(f"{tag}_final", [P, HEADS, HK], FP32)
        t1 = sb.sb(f"{tag}_t1", [P, K, HEADS], FP32)
        t2 = sb.sb(f"{tag}_t2", [P, K, HEADS], FP32)
        A = sb.sb(f"{tag}_alpha", [P, TOP + KH], FP32)
        ex = sb.sb(f"{tag}_ex", [P, SLOTS, TOP], FP32)
        scale = sb.sb(f"{tag}_scale", [P, HEADS], FP32)
        p_sum = sb.ps(f"{tag}_psum", [P, OHS, 512])
        p_node = sb.ps(f"{tag}_pnode", [P, 512])
        p_seg = sb.ps(f"{tag}_pseg", [P, 512])
        p_top = sb.ps(f"{tag}_ptop", [P, 512])
        idx_ok = sem(f"{tag}_idx_ok")
        rows_in = [sem(f"{tag}_rows_in{b}") for b in range(SLOTS)]
        marks_in, t01_in = sem(f"{tag}_marks_in"), sem(f"{tag}_t01_in")
        t01_ok = sem(f"{tag}_t01")
        node_ok = sem(f"{tag}_node")
        sm_ok = sem(f"{tag}_sm_ok")
        pseg_ok, top_ok = sem(f"{tag}_pseg"), sem(f"{tag}_top_ok")
        diag_ok = sem(f"{tag}_diag_ok")
        dif_ok, ex_ok = sem(f"{tag}_dif_ok"), sem(f"{tag}_ex_ok")
        extra_ok = sem(f"{tag}_extra_ok")
        weighted = sem(f"{tag}_weighted")
        onehot_ok = sem(f"{tag}_onehot_ok")
        summed = sem(f"{tag}_summed")
        added = sem(f"{tag}_added")
        own, begun = sem(f"{tag}_own"), sem(f"{tag}_begun")
        FREE = SLOTS * K
        NCH, PRE = 22, 25
        AHEAD = OHS - 1
        LOOPS = (BATCHES - 1) // SLOTS
        PEELED = BATCHES - LOOPS * SLOTS
        assert K % OHS == 0 and K >= 14

        def all_batches(eng, turn):
            with eng.Fori(0, LOOPS) as i:
                for b in range(SLOTS):
                    turn(i * SLOTS + b, i, b)
            for b in range(PEELED):
                turn(LOOPS * SLOTS + b, LOOPS, b)

        def after(i, b):
            i, b = i + (b + 1) // SLOTS, (b + 1) % SLOTS
            return i * SLOTS + b, i, b

        def blocks_of(q, engine):
            _, vals = nc.values_load_multi_w_load_instructions(
                g.block_of[0:1, bass.ds(q * K, K)], engines=[engine], min_val=0,
                max_val=BLOCKS - 1, skip_runtime_bounds_check_because=SKIP)
            return vals

        def slot(b):
            return G[:, b, :, :].rearrange("p k (h r) -> p k h r", h=HEADS)

        def by_k(t):
            return t.rearrange("p (k h) -> p k h", h=HEADS)

        def per_edge(table, q):
            return table[:, bass.ds(q * K, K)].unsqueeze(2).to_broadcast([P, K, HEADS])

        with nc.Block() as block:

            @block.gpsimd
            def _(pool):
                pool.sem_inc(summed, FREE)
                pool.sem_inc(added, OHS)
                pool.sem_inc(t01_ok, 1)
                pool.sem_inc(node_ok, 1)
                pool.sem_inc(diag_ok, 1)
                pool.memset(idx[:, :, :], 0).then_inc(begun, 1)
                pool.wait_ge(begun, 1)

                def gather(q, i, b):
                    pool.wait_ge(summed, q * K + K)
                    pool.tensor_copy(idx[:, b, :], g.rows[:, bass.ds(q * K, K)]).then_inc(idx_ok, 1)
                    pool.wait_ge(idx_ok, q + 1)
                    pool.sem_inc(begun, 1)
                    for k in range(K):
                        pool.indirect_dma_start(
                            out=G[:, b, k, :], out_offset=None, in_=g.table,
                            in_offset=bass.IndirectOffsetOnAxis(ap=idx[:, b, k:k + 1], axis=0))\
                            .then_inc(rows_in[b], 16)

                all_batches(pool, gather)

            @block.sync
            def _(sp):
                def load(q, i, b):
                    if first:
                        sp.wait_ge(t01_ok, q + 1)
                        sp.dma_start(places[:, :], g.places[bass.ds(q * K, K), :]
                                     .rearrange("k e -> (k e)").partition_broadcast(P))\
                            .then_inc(places_in, 16)
                    else:
                        sp.wait_ge(node_ok, q + 1)
                        sp.dma_start(turned01[:, :], flat(g.turned01[bass.ds(q * P, P), :, :]))\
                            .then_inc(t01_in, 16)
                    sp.wait_ge(diag_ok, q + 1)
                    sp.dma_start(marks[:, :], g.marks[bass.ds(q * K, K), :, :]
                                 .rearrange("k h e -> (k h) e")).then_inc(marks_in, 16)
                    if first:
                        sp.wait_ge(t01_ok, q + 2)
                        sp.dma_start(flat(g.turned01[bass.ds(q * P, P), :, :]), turned01[:, :])\
                            .then_inc(t01_kept, 16)

                all_batches(sp, load)
                if first:
                    sp.wait_ge(t01_kept, 16 * BATCHES)

            @block.tensor
            def _(pe):
                def node_scores(q):
                    blk = blocks_of(q, ENG.PE)
                    if first:
                        pe.wait_ge(t01_ok, q + 2)
                    else:
                        pe.wait_ge(t01_in, q * 16 + 16)
                    for k in range(K):
                        last = nc.tensor.matmul(
                            p_node[:, k * 6 * HEADS:(k + 1) * 6 * HEADS],
                            turned01[:, k * P:(k + 1) * P],
                            g.scores[:, bass.ds(blk[k], 1), :, :].rearrange("p a t h -> p (a t h)"),
                            start=True, stop=True)
                    last.then_inc(node_ok, 1)

                def turn_scores(q):
                    pe.wait_ge(sm_ok, q + 1)
                    nc.tensor.transpose(p_seg[:, 0:P], sm[:, :], g.ident[:, :])\
                        .then_inc(pseg_ok, 1)

                def turn_tops(q):
                    pe.wait_ge(diag_ok, q + 2)
                    nc.tensor.matmul(p_top[:, KH:3 * KH], g.ones[:, :], flat(diag[:, :, :]),
                                     start=True, stop=True)
                    nc.tensor.transpose(p_top[:, 0:KH], seg[:, :], g.ident[0:KH, 0:KH])\
                        .then_inc(top_ok, 1)

                def sum_up(q, b, k):
                    pe.wait_ge(onehot_ok, q * K + k + 1)
                    pe.wait_ge(weighted, q * K + k + 1)
                    if k == 0:
                        pe.wait_ge(extra_ok, q + 1)
                    pe.wait_ge(added, q * K + k + 1)
                    nc.tensor.matmul(p_sum[:, k % OHS, 0:ROW], onehot[:, k % OHS, :], G[:, b, k, :],
                                     start=True, stop=True).then_inc(summed, 1)

                def maxima(q):
                    node_scores(q)
                    turn_scores(q)
                    turn_tops(q)

                def turn(q, i, b, last=False):
                    for k in range(K):
                        sum_up(q, b, k)
                        if k in PRODUCTS and not last:
                            PRODUCTS[k](q + 1)

                PRODUCTS = {2: node_scores, 4: turn_scores, 6: turn_tops}
                maxima(0)
                with pe.Fori(0, LOOPS) as i:
                    for b in range(SLOTS):
                        turn(i * SLOTS + b, i, b)
                for b in range(PEELED):
                    turn(LOOPS * SLOTS + b, LOOPS, b, last=b == PEELED - 1)

            @block.scalar
            def _(act):
                def weigh(q, i, b):
                    act.wait_ge(dif_ok, q + 1)
                    act.activation(ex[:, b, :], A[:, 0:TOP], ACT.Exp).then_inc(ex_ok, 1)
                    act.wait_ge(ex_ok, q + 1)
                    for k in range(K):
                        for h in range(HEADS):
                            part = G[:, b, k, h * HC + 1:(h + 1) * HC - 1]
                            last = act.activation(part, part, ACT.Copy,
                                                  scale=ex[:, b, k * HEADS + h:k * HEADS + h + 1])
                        last.then_inc(weighted, 1)

                all_batches(act, weigh)

            @block.vector
            def _(dve):
                def make_onehot(q, k):
                    s = q * K + k
                    dve.wait_ge(summed, s + (FREE - OHS + 1))
                    dve.tensor_scalar(onehot[:, k % OHS, :], g.iota_f[:, :],
                                      g.place[:, bass.ds(s, 1)], None, ALU.is_equal)\
                        .then_inc(onehot_ok, 1)

                def read_scale(q, w):
                    dve.wait_ge(summed, q * K + (FREE + 1))
                    w.inc(dve.tensor_scalar(
                        scale[:, :],
                        p_sum[:, 0, 0:ROW].rearrange("p (h r) -> p h r", h=HEADS)[:, :, HC - 1],
                        1.0, None, ALU.add))

                def add(q, k, blk, w):
                    s = q * K + k
                    dve.wait_ge(summed, s + (FREE + 1))
                    if k:
                        dve.wait_ge(added, s + OHS)
                        acc = flat(g.sums[:, bass.ds(blk, 1), :])
                        dve.tensor_tensor(acc, acc, p_sum[:, k % OHS, 0:ROW], ALU.add)\
                            .then_inc(added, 1)
                        return
                    part = p_sum[:, k % OHS, 0:ROW].rearrange("p (h r) -> p h r", h=HEADS)
                    w.settle(dve)
                    dve.wait_ge(added, s + OHS)
                    acc = g.sums[:, bass.ds(blk, 1), :].rearrange("p a (h r) -> p (a h) r", h=HEADS)
                    for h in range(HEADS):
                        last = dve.scalar_tensor_tensor(
                            out=acc[:, h, :], in0=acc[:, h, :], scalar=scale[:, h:h + 1],
                            in1=part[:, h, :], op0=ALU.mult, op1=ALU.add)
                    last.then_inc(added, 1)

                def head(k, n, j, m, w):
                    if k == 0 and first:
                        if not isinstance(n, int):
                            dve.wait_ge(t01_kept, n * 16)
                        dve.wait_ge(places_in, n * 16 + 16)
                        dve.tensor_scalar(turned01[:, :], places[:, :], g.iota_p[:, 0:1], None,
                                          ALU.is_equal).then_inc(t01_ok, 1)
                    d = D[:, :, :]
                    if k == 1:
                        dve.wait_ge(node_ok, n + 2)
                        w.step(dve, dve.tensor_reduce(
                            d, p_node[:, 0:6 * KH].rearrange("p (k t h) -> p k h t", k=K, t=3),
                            AX.X, ALU.add))
                        dve.wait_ge(rows_in[m], j * (16 * K) + 16 * K)
                        dve.tensor_tensor(by_k(sm[:, 0:KH]), slot(m)[:, :, :, 0], d[:, :, 0:HEADS],
                                          ALU.max).then_inc(sm_ok, 1)
                    if k == 2:
                        dve.wait_ge(pseg_ok, n + 1)
                        dve.wait_ge(marks_in, n * 16 + 16)
                        w.inc(dve.tensor_tensor_scan(fwd[:, :], marks[:, 0:P], p_seg[0:KH, 0:P],
                                                     -BIG, ALU.add, ALU.max))
                    if k == 3:
                        w.settle(dve)
                        w.step(dve, dve.tensor_tensor_scan(seg[:, ::-1], marks[:, P:0:-1],
                                                           fwd[:, ::-1], -BIG, ALU.add, ALU.max))
                        dve.tensor_tensor(
                            diag[:, :, :],
                            g.ident[0:KH, 0:KH].unsqueeze(1).to_broadcast([KH, 2, KH]),
                            seg[:, 0:P:P - 1].unsqueeze(2).to_broadcast([KH, 2, KH]), ALU.mult)\
                            .then_inc(diag_ok, 1)

                def tail(k, n, m, w):
                    d = D[:, :, :]
                    dst = d[:, :, HEADS:]
                    spread = p_top[:, KH:3 * KH].rearrange("p (a k h) -> p a h k", a=2, h=HEADS)
                    if k == 0:
                        w.step(dve, dve.tensor_copy(last_max[:, :, 0], so_far[:, :, K]))
                        w.inc(dve.tensor_tensor(by_k(A[:, 0:KH]), slot(m)[:, :, :, 0], dst, ALU.add))
                        w.inc(dve.tensor_tensor(by_k(A[:, KH:CIN]), d[:, :, 0:HEADS], dst, ALU.add))
                        w.inc(dve.tensor_tensor(A[:, CIN:TOP], last_max[:, :, 0], dst[:, 0, :],
                                                ALU.add))
                    if k == 1:
                        dve.wait_ge(top_ok, n + 1)
                        w.inc(dve.tensor_copy(last_max[:, :, 1:HK], spread[:, 1]))
                        w.inc(dve.tensor_tensor(
                            first_max[:, :, 0:K], spread[:, 0],
                            g.goes_on[:, bass.ds(n * K, K)].unsqueeze(1).to_broadcast([P, HEADS, K]),
                            ALU.add))
                    if k == 2:
                        w.settle(dve)
                        w.inc(dve.tensor_tensor_scan(
                            flat(so_far[:, :, :]), flat(g.gates[:, bass.ds(n, 1), :]),
                            flat(last_max[:, :, :]), -BIG, ALU.add, ALU.max))
                    if k == 3:
                        w.settle(dve)
                        w.step(dve, dve.tensor_tensor(last_max[:, :, :], first_max[:, :, :],
                                                      so_far[:, :, :], ALU.max))
                        w.inc(dve.tensor_tensor_scan(
                            flat(final[:, :, :])[:, ::-1],
                            flat(g.gates_back[:, bass.ds(n, 1), :]),
                            flat(last_max[:, :, :])[:, ::-1], -BIG, ALU.add, ALU.max))
                    if k == 4:
                        w.settle(dve)
                        seen = final[:, :, :].rearrange("p h k -> p k h")
                        w.inc(dve.tensor_tensor(t1[:, :, :], per_edge(g.follows, n), seen[:, 0:K, :],
                                                ALU.add))
                        w.step(dve, dve.tensor_tensor(t2[:, :, :], per_edge(g.ends, n),
                                                      seen[:, 1:HK, :], ALU.add))
                        w.step(dve, dve.tensor_tensor(t1[:, :, :], t1[:, :, :], t2[:, :, :], ALU.max))
                        w.inc(dve.tensor_tensor(t2[:, :, :], t1[:, :, :], by_k(p_top[:, 0:KH]),
                                                ALU.max))
                    if k == 5:
                        w.settle(dve)
                        w.step(dve, dve.tensor_tensor(by_k(A[:, TOP:]), t2[:, :, :], dst, ALU.add))
                        w.inc(dve.scalar_tensor_tensor(out=A[:, :], in0=A[:, :], scalar=SLOPE,
                                                       in1=A[:, :], op0=ALU.mult, op1=ALU.max))
                    if k == 6:
                        w.settle(dve)
                        top = A[:, TOP:].unsqueeze(1).to_broadcast([P, 2, KH])
                        w.inc(dve.tensor_tensor(
                            A[:, 0:CIN].rearrange("p (a e) -> p a e", a=2),
                            A[:, 0:CIN].rearrange("p (a e) -> p a e", a=2), top, ALU.subtract))
                        w.step(dve, dve.tensor_tensor(A[:, CIN:TOP], A[:, CIN:TOP],
                                                      A[:, TOP:TOP + HEADS], ALU.subtract))
                        dve.tensor_scalar(A[:, 0:TOP], A[:, 0:TOP], 0.0, None, ALU.min)\
                            .then_inc(dif_ok, 1)
                    if k == 7:
                        dve.wait_ge(ex_ok, n + 1)
                        e = ex[:, m, :]
                        w.inc(dve.tensor_tensor(slot(m)[:, :, :, 0], by_k(e[:, KH:CIN]),
                                                per_edge(g.starts, n), ALU.mult))
                        w.settle(dve)
                        dve.scalar_tensor_tensor(
                            out=slot(m)[:, 0, :, HC - 1], in0=e[:, CIN:TOP], scalar=-1.0,
                            in1=g.opens[:, bass.ds(n, 1)].to_broadcast([P, HEADS]),
                            op0=ALU.add, op1=ALU.mult).then_inc(extra_ok, 1)

                def maxima(at, n, j, m, w):
                    if at in HEADS_AT:
                        head(HEADS_AT[at], n, j, m, w)
                    if at in TAILS_AT:
                        tail(TAILS_AT[at], n, m, w)

                def turn(q, i, b, last=False):
                    w = Own(own, q * NCH + PRE)
                    blk = blocks_of(q, ENG.DVE)
                    n, j, m = after(i, b)
                    for k in range(K):
                        if not last or k + AHEAD < K:
                            make_onehot(q, k + AHEAD)
                        if k == 0:
                            read_scale(q, w)
                        if not last:
                            maxima(2 * k, n, j, m, w)
                        add(q, k, blk[k], w)
                        if not last:
                            maxima(2 * k + 1, n, j, m, w)
                    assert w.n == NCH or last, w.n

                HEADS_AT = {0: 0, 5: 1, 7: 2, 9: 3}
                TAILS_AT = {10: 0, 11: 1, 13: 2, 14: 3, 15: 4, 16: 5, 17: 6, 24: 7}
                w = Own(own)
                w.inc(dve.memset(g.sums[:, :, :], 0.0))
                w.inc(dve.memset(first_max[:, :, K:HK], -BIG))
                w.inc(dve.memset(so_far[:, :, :], -BIG))
                w.inc(dve.memset(sm[:, :], 0.0))
                w.settle(dve)
                dve.wait_ge(added, OHS)
                for part in range(4):
                    head(part, 0, 0, 0, w)
                for part in range(8):
                    tail(part, 0, 0, w)
                assert w.n == PRE, w.n
                for k in range(AHEAD):
                    make_onehot(0, k)
                with dve.Fori(0, LOOPS) as i:
                    for b in range(SLOTS):
                        turn(i * SLOTS + b, i, b)
                for b in range(PEELED):
                    turn(LOOPS * SLOTS + b, LOOPS, b, last=b == PEELED - 1)


def aggregate(nc, sem, g, tag, table, rows, weights):
    OHS = RING
    with Memory(nc) as sb:
        G = sb.sb(f"{tag}_rows", [P, SLOTS, K, DIM], FP32)
        idx = sb.sb(f"{tag}_idx", [P, SLOTS, K], U32)
        onehot = sb.sb(f"{tag}_onehot", [P, OHS, P], FP32)
        p_sum = sb.ps(f"{tag}_psum", [P, OHS, 512])
        idx_ok, begun = sem(f"{tag}_idx_ok"), sem(f"{tag}_begun")
        rows_in = [sem(f"{tag}_rows_in{b}") for b in range(SLOTS)]
        onehot_ok = sem(f"{tag}_onehot_ok")
        summed = sem(f"{tag}_summed")
        added = sem(f"{tag}_added")
        FREE = SLOTS * K
        AHEAD = OHS - 1
        LOOPS = (BATCHES - 1) // SLOTS
        PEELED = BATCHES - LOOPS * SLOTS

        def all_batches(eng, turn):
            with eng.Fori(0, LOOPS) as i:
                for b in range(SLOTS):
                    turn(i * SLOTS + b, i, b)
            for b in range(PEELED):
                turn(LOOPS * SLOTS + b, LOOPS, b)

        with nc.Block() as block:

            @block.gpsimd
            def _(pool):
                pool.sem_inc(summed, FREE)
                pool.sem_inc(added, OHS)
                pool.memset(idx[:, :, :], 0).then_inc(begun, 1)
                pool.wait_ge(begun, 1)

                def gather(q, i, b):
                    pool.wait_ge(summed, q * K + K)
                    pool.tensor_copy(idx[:, b, :], rows[:, bass.ds(q * K, K)]).then_inc(idx_ok, 1)
                    pool.wait_ge(idx_ok, q + 1)
                    pool.sem_inc(begun, 1)
                    for k in range(K):
                        pool.indirect_dma_start(
                            out=G[:, b, k, :], out_offset=None, in_=table,
                            in_offset=bass.IndirectOffsetOnAxis(ap=idx[:, b, k:k + 1], axis=0))\
                            .then_inc(rows_in[b], 16)

                all_batches(pool, gather)

            @block.tensor
            def _(pe):
                def turn(q, i, b):
                    pe.wait_ge(rows_in[b], i * (16 * K) + 16 * K)
                    for k in range(K):
                        pe.wait_ge(onehot_ok, q * K + k + 1)
                        pe.wait_ge(added, q * K + k + 1)
                        nc.tensor.matmul(p_sum[:, k % OHS, 0:DIM], onehot[:, k % OHS, :],
                                         G[:, b, k, :], start=True, stop=True).then_inc(summed, 1)

                all_batches(pe, turn)

            @block.vector
            def _(dve):
                def make_onehot(q, k):
                    s = q * K + k
                    dve.wait_ge(summed, s + (FREE - OHS + 1))
                    if weights is None:
                        dve.tensor_scalar(onehot[:, k % OHS, :], g.iota_f[:, :],
                                          g.place[:, bass.ds(s, 1)], None, ALU.is_equal)\
                            .then_inc(onehot_ok, 1)
                    else:
                        dve.tensor_scalar(onehot[:, k % OHS, :], g.iota_f[:, :],
                                          g.place[:, bass.ds(s, 1)], weights[:, bass.ds(s, 1)],
                                          ALU.is_equal, ALU.mult).then_inc(onehot_ok, 1)

                def turn(q, i, b, last=False):
                    _, blk = nc.values_load_multi_w_load_instructions(
                        g.block_of[0:1, bass.ds(q * K, K)], engines=[ENG.DVE], min_val=0,
                        max_val=BLOCKS - 1, skip_runtime_bounds_check_because=SKIP)
                    for k in range(K):
                        if not last or k + AHEAD < K:
                            make_onehot(q, k + AHEAD)
                        s = q * K + k
                        dve.wait_ge(summed, s + (FREE + 1))
                        dve.wait_ge(added, s + OHS)
                        acc = flat(g.sums[:, bass.ds(blk[k], 1), 0:DIM])
                        dve.tensor_tensor(acc, acc, p_sum[:, k % OHS, 0:DIM], ALU.add)\
                            .then_inc(added, 1)

                dve.memset(g.sums[:, :, :], 0.0)
                dve.drain()
                dve.wait_ge(added, OHS)
                for k in range(AHEAD):
                    make_onehot(0, k)
                with dve.Fori(0, LOOPS) as i:
                    for b in range(SLOTS):
                        turn(i * SLOTS + b, i, b)
                for b in range(PEELED):
                    turn(LOOPS * SLOTS + b, LOOPS, b, last=b == PEELED - 1)


class Norm:
    STEPS = 3 * GROUP + 2

    def __init__(self, nc, sem, sb, tag, per_group):
        self.nc, self.per = nc, per_group
        self.stats = sb.sb(f"{tag}_stats", [P, GROUP, 6], FP32)
        self.mv = sb.sb(f"{tag}_mv", [P, GROUP, 2], FP32)
        self.std = sb.sb(f"{tag}_std", [P, GROUP], FP32)
        self.inv = sb.sb(f"{tag}_inv", [P, GROUP], FP32)
        self.shift = sb.sb(f"{tag}_shift", [P, GROUP], FP32)
        self.var_ok, self.std_ok = sem(f"{tag}_var_ok"), sem(f"{tag}_std_ok")
        self.held = sem(f"{tag}_held")

    def vector(self, dve, w, c, n, y):
        dve.sem_inc(self.held, 1)
        for k in range(GROUP):
            w.inc(dve.bn_stats(self.stats[:, k, :], y(k)))
        dve.wait_ge(w.sem, w.base + w.n)
        dve.sem_inc(self.held, 1)
        for k in range(GROUP):
            w.inc(dve.bn_aggr(self.mv[:, k, :], self.stats[:, k, :]))
        dve.wait_ge(w.sem, w.base + w.n)
        dve.tensor_scalar(self.std[:, :], self.mv[:, :, 1], LN_EPS, None, ALU.add)\
            .then_inc(self.var_ok, 1)
        dve.wait_ge(self.std_ok, c * self.per + n + 1)
        w.step(dve, dve.reciprocal(self.inv[:, :], self.std[:, :]))
        w.step(dve, dve.scalar_tensor_tensor(out=self.shift[:, :], in0=self.mv[:, :, 0], scalar=-1.0,
                                             in1=self.inv[:, :], op0=ALU.mult, op1=ALU.mult))
        for k in range(GROUP):
            w.inc(dve.tensor_scalar(y(k), y(k), self.inv[:, k:k + 1], self.shift[:, k:k + 1],
                                    ALU.mult, ALU.add))
        dve.wait_ge(w.sem, w.base + w.n)

    def scalar(self, act, c, n):
        act.wait_ge(self.var_ok, c * self.per + n + 1)
        act.activation(self.std[:, :], self.std[:, :], ACT.Sqrt).then_inc(self.std_ok, 1)


class Transform:
    PAIR = 2
    BANKS = 4
    FULL = RELS // PAIR
    BUF = tuple(k % 2 for k in range(GROUP - 1)) + (2,)

    def __init__(self, nc, sem, sb, g, weight, x_done):
        self.nc, self.g, self.weight, self.x_done = nc, g, weight, x_done
        self.w3 = sb.sb("rel_w", [P, 2, RELS, DIM], FP32)
        self.x_in = sb.sb("rel_x_in", [P, GROUP, DIM], FP32)
        self.xT = sb.sb("rel_xt", [P, 3, DIM], FP32)
        self.out = sb.sb("rel_out", [P, RELS, DIM], FP32)
        self.p_t = sb.ps("rel_pt", [P, 512])
        self.p_y = sb.ps("rel_py", [P, self.BANKS, self.PAIR * DIM])
        self.loaded, self.x_ok = sem("rel_loaded"), sem("rel_x_ok")
        self.turned, self.copied, self.mult = sem("rel_turned"), sem("rel_copied"), sem("rel_mult")
        self.read = sem("rel_read")
        self.put = [sem("rel_put0"), sem("rel_put1")]
        self.out_free = [sem("rel_out_free0"), sem("rel_out_free1")]

    def relay(self, pool):
        pool.sem_inc(self.read, self.BANKS)
        for s in self.out_free:
            pool.sem_inc(s, FROM)
        with pool.Fori(0, BLOCKS) as j:
            for half in range(2):
                pool.wait_ge(self.put[half], j * 16 + 16)
                pool.sem_inc(self.out_free[half], 1)

    def load_weights(self, sp):
        for i in range(2):
            sp.dma_start(self.w3[:, i, :, :],
                         self.weight[:, i * P:(i + 1) * P, :].rearrange("r p d -> p r d"))\
                .then_inc(self.loaded, 16)

    def load(self, sp, c):
        if not isinstance(c, int):
            sp.wait_ge(self.turned, c * GROUP)
        sp.wait_ge(self.x_done, c + 1)
        sp.dma_start(self.x_in[:, :, :], self.g.X[:, bass.ds(c * GROUP, GROUP), :])\
            .then_inc(self.x_ok, 16)

    def store(self, sp, j):
        y = self.g.by_rel.rearrange("(r n) d -> n r d", n=PADN)
        for half in range(2):
            sp.wait_ge(self.read, j * self.FULL + ((half + 1) * (self.FULL // 2) + self.BANKS))
            r = slice(half * RELS // 2, (half + 1) * RELS // 2)
            sp.dma_start(y[bass.ds(j * P, P), r, :], self.out[:, r, :]).then_inc(self.put[half], 16)

    def turn_over(self, pe, c, k):
        if k == 0:
            pe.wait_ge(self.x_ok, c * 16 + 16)
        for i in range(2):
            last = self.nc.tensor.transpose(self.p_t[:, i * P:(i + 1) * P],
                                            self.x_in[:, k, i * P:(i + 1) * P], self.g.ident[:, :])
        last.then_inc(self.turned, 1)

    def tensor(self, pe, c, last_group=False):
        for k in range(GROUP):
            j = c * GROUP + k
            pe.wait_ge(self.copied, j + 1)
            if k + 1 < GROUP:
                self.turn_over(pe, c, k + 1)
            elif not last_group:
                self.turn_over(pe, c + 1, 0)
            for n in range(self.FULL):
                pe.wait_ge(self.read, j * self.FULL + n + 1)
                for r in range(self.PAIR):
                    for f in range(2):
                        last = self.nc.tensor.matmul(
                            self.p_y[:, n % self.BANKS, r * DIM:(r + 1) * DIM],
                            self.xT[:, self.BUF[k], f * P:(f + 1) * P],
                            self.w3[:, f, n * self.PAIR + r, :], start=(f == 0), stop=(f == 1))
                last.then_inc(self.mult, 1)

    def copy_turned(self, act, c, k):
        act.wait_ge(self.turned, c * GROUP + k + 1)
        act.activation(self.xT[:, self.BUF[k], :], self.p_t[:, 0:DIM], ACT.Copy)\
            .then_inc(self.copied, 1)

    def scalar(self, act, c, k, last=False):
        j = c * GROUP + k
        if k + 1 < GROUP:
            self.copy_turned(act, c, k + 1)
        elif not last:
            self.copy_turned(act, c + 1, 0)
        for n in range(self.FULL):
            if n % (self.FULL // 2) == 0:
                act.wait_ge(self.out_free[n // (self.FULL // 2)], j + FROM)
            act.wait_ge(self.mult, j * self.FULL + n + 1)
            act.activation(self.out[:, n * self.PAIR:(n + 1) * self.PAIR, :]
                           .rearrange("p r d -> p (r d)"), self.p_y[:, n % self.BANKS, :], ACT.Copy)\
                .then_inc(self.read, 1)


def finish_attention(nc, sem, g, tag, bias, guard, norm, then=None, rel=None):
    with Memory(nc) as sb:
        own_rows = sb.sb(f"{tag}_own_rows", [P, GROUP, ROW], FP32)
        T = sb.sb(f"{tag}_t", [P, GROUP, DIM], FP32)
        bias_sb = sb.sb(f"{tag}_bias", [P, DIM], FP32)
        den = sb.sb(f"{tag}_den", [P, GROUP * HEADS], FP32)
        lone = sb.sb(f"{tag}_lone", [P, GROUP * HEADS], FP32)
        self_w = sb.sb(f"{tag}_self_w", [P, GROUP * HEADS], FP32)
        bias_in, rows_in, rows_used = sem(f"{tag}_bias_in"), sem(f"{tag}_rows_in"), sem(f"{tag}_used")
        own, done, stored = sem(f"{tag}_own"), sem(f"{tag}_done"), sem(f"{tag}_stored")
        ln = Norm(nc, sem, sb, tag, 1) if norm else None
        NV = 9 + (Norm.STEPS + 1 if norm else 0)
        pr = Projection(nc, sem, sb, g, then[0], g.sums, *then[1:], y_done=done) if then else None
        tr = Transform(nc, sem, sb, g, rel, done) if rel is not None else None
        with nc.Block() as block:

            @block.gpsimd
            def _(pool):
                pool.sem_inc(rows_used, FROM)
                if then:
                    pr.relay(pool)
                if tr:
                    tr.relay(pool)

            @block.sync
            def _(sp):
                if then:
                    pr.load_weights(sp)
                sp.dma_start(bias_sb[:, :], bias.partition_broadcast(P)).then_inc(bias_in, 16)

                def load(c):
                    sp.wait_ge(rows_used, c + FROM)
                    sp.dma_start(own_rows[:, :, :],
                                 g.table[bass.ds(c * (GROUP * P), GROUP * P), :]
                                 .rearrange("(b p) r -> p b r", p=P)).then_inc(rows_in, 16)

                if then:
                    load(0)
                    with sp.Fori(0, GROUPS - 1) as c:
                        load(c + 1)
                        pr.load(sp, c)
                        pr.store(sp, c)
                    pr.load(sp, GROUPS - 1)
                    pr.store(sp, GROUPS - 1)
                    sp.wait_ge(pr.put, 16 * GROUPS)
                    return
                if tr:
                    load(0)
                    tr.load_weights(sp)
                    tr.load(sp, 0)
                    with sp.Fori(0, GROUPS - 1) as c:
                        load(c + 1)
                        for k in range(GROUP):
                            if k == GROUP - 2:
                                tr.load(sp, c + 1)
                            tr.store(sp, c * GROUP + k)
                    for k in range(GROUP):
                        tr.store(sp, (GROUPS - 1) * GROUP + k)
                    for half in range(2):
                        sp.wait_ge(tr.put[half], 16 * BLOCKS)
                    return

                def keep(c):
                    sp.wait_ge(done, c + 1)
                    sp.dma_start(g.nodes[bass.ds(c * (GROUP * P), GROUP * P), :]
                                 .rearrange("(b p) d -> p b d", p=P),
                                 g.X[:, bass.ds(c * GROUP, GROUP), :]).then_inc(stored, 16)

                load(0)
                with sp.Fori(0, GROUPS - 1) as c:
                    load(c + 1)
                    keep(c)
                keep(GROUPS - 1)
                sp.wait_ge(stored, 16 * GROUPS)

            if then:
                @block.tensor
                def _(pe):
                    pe.wait_ge(pr.ready, 1)
                    with pe.Fori(0, GROUPS) as c:
                        pr.tensor(pe, c)

                @block.scalar
                def _(act):
                    act.wait_ge(pr.ready, 1)
                    with act.Fori(0, GROUPS) as c:
                        pr.scalar(act, c)

            if tr:
                @block.tensor
                def _(pe):
                    pe.wait_ge(tr.loaded, 32)
                    tr.turn_over(pe, 0, 0)
                    with pe.Fori(0, GROUPS - 1) as c:
                        tr.tensor(pe, c)
                    tr.tensor(pe, GROUPS - 1, last_group=True)

                @block.scalar
                def _(act):
                    ln.scalar(act, 0, 0)
                    tr.copy_turned(act, 0, 0)
                    with act.Fori(0, GROUPS - 1) as c:
                        for k in range(GROUP):
                            tr.scalar(act, c, k)
                            if k == 1:
                                ln.scalar(act, c + 1, 0)
                    for k in range(GROUP):
                        tr.scalar(act, GROUPS - 1, k, last=k == GROUP - 1)

            elif norm:
                @block.scalar
                def _(act):
                    with act.Fori(0, GROUPS) as c:
                        ln.scalar(act, c, 0)

            @block.vector
            def _(dve):
                if then:
                    pr.prepare(dve)
                dve.wait_ge(bias_in, 16)
                with dve.Fori(0, GROUPS) as c:
                    w = Own(own, c * NV)
                    blocks = bass.ds(c * GROUP, GROUP)
                    s = g.sums[:, blocks, :].rearrange("p b (h r) -> p (b h) r", h=HEADS)
                    r = own_rows[:, :, :].rearrange("p b (h r) -> p (b h) r", h=HEADS)
                    t = T[:, :, :].rearrange("p b (h r) -> p (b h) r", h=HEADS)

                    def wide(a):
                        return a[:, :].unsqueeze(2).to_broadcast([P, GROUP * HEADS, CH])

                    w.step(dve, dve.tensor_tensor(den[:, :], s[:, :, CH + 1], s[:, :, 0], ALU.add))
                    w.step(dve, dve.tensor_scalar(lone[:, :], den[:, :], 0.5, None, ALU.is_lt))
                    w.step(dve, dve.tensor_tensor(self_w[:, :], s[:, :, 0], lone[:, :], ALU.add))
                    w.step(dve, dve.tensor_tensor(den[:, :], den[:, :], lone[:, :], ALU.add))
                    w.step(dve, dve.tensor_scalar(den[:, :], den[:, :], 1e-16, None, guard))
                    w.step(dve, dve.reciprocal(den[:, :], den[:, :]))
                    dve.wait_ge(rows_in, c * 16 + 16)
                    dve.tensor_tensor(t, r[:, :, 1:CH + 1], wide(self_w), ALU.mult)\
                        .then_inc(rows_used, 1)
                    dve.wait_ge(rows_used, c + 1 + FROM)
                    w.step(dve, dve.tensor_tensor(t, t, s[:, :, 1:CH + 1], ALU.add))
                    w.step(dve, dve.tensor_tensor(t, t, wide(den), ALU.mult))
                    w.step(dve, dve.tensor_tensor(
                        T[:, :, :], T[:, :, :],
                        bias_sb[:, :].unsqueeze(1).to_broadcast([P, GROUP, DIM]), ALU.add))
                    if not norm:
                        dve.tensor_scalar(g.sums[:, blocks, 0:DIM], T[:, :, :], 0.0, None, ALU.max)\
                            .then_inc(done, 1)
                    else:
                        x = g.X[:, blocks, :]
                        w.step(dve, dve.tensor_tensor(x, x, T[:, :, :], ALU.add))
                        ln.vector(dve, w, c, 0,
                                  lambda k: flat(g.X[:, bass.ds(c * GROUP + k, 1), :]))
                        dve.sem_inc(done, 1)
                    assert w.n == NV, w.n
                if then:
                    pr.split(dve)


def perceptron(nc, sem, g, W1, b1, W2, b2, eps, gamma, beta, then):
    with Memory(nc) as sb:
        w1 = sb.sb("mlp_w1", [P, 2, DIM], FP32)
        w2 = sb.sb("mlp_w2", [P, 2, DIM], FP32)
        b1c = sb.sb("mlp_b1", [P, 2], FP32)
        vec = sb.sb("mlp_vec", [P, 3, DIM], FP32)
        one_eps = sb.sb("mlp_eps", [P, 1], FP32)
        Z = sb.sb("mlp_z", [P, GROUP, DIM], FP32)
        mlp_out = sb.sb("mlp_out", [P, GROUP, DIM], FP32)
        R = sb.sb("mlp_r", [P, GROUP, DIM], FP32)
        zT = sb.sb("mlp_zt", [P, 2, DIM], FP32)
        hT = sb.sb("mlp_ht", [P, 2, DIM], FP32)
        p_t = sb.ps("mlp_pt", [P, 2, 512])
        p_h = sb.ps("mlp_ph", [P, 2, 512])
        p_z = sb.ps("mlp_pz", [P, 2, 512])
        loaded, own = sem("mlp_loaded"), sem("mlp_own")
        z_ok, turned, copied = sem("mlp_z_ok"), sem("mlp_turned"), sem("mlp_copied")
        hid, hid_ok, mult, evac = sem("mlp_hid"), sem("mlp_hid_ok"), sem("mlp_mult"), sem("mlp_evac")
        ln = Norm(nc, sem, sb, "mlp_norm", 2)
        out_free = sem("mlp_out_free")
        NV = 1 + 2 + 1 + 2 * Norm.STEPS
        done = sem("mlp_done")
        pr = Projection(nc, sem, sb, g, then[0], g.X, *then[1:], y_done=done, p_t=p_t)
        with nc.Block() as block:

            @block.gpsimd
            def _(pool):
                for s in (turned, copied, hid, hid_ok, mult, evac):
                    pool.sem_inc(s, FROM)
                pool.sem_inc(out_free, 1)
                pr.relay(pool)

            @block.sync
            def _(sp):
                sp.dma_start(w1[:, :, :], W1.rearrange("(k p) n -> p k n", p=P)).then_inc(loaded, 16)
                sp.dma_start(w2[:, :, :], W2.rearrange("(k p) n -> p k n", p=P)).then_inc(loaded, 16)
                for i in range(2):
                    sp.dma_start(b1c[:, i:i + 1], b1[i * P:(i + 1) * P].rearrange("(p a) -> p a", a=1))\
                        .then_inc(loaded, 16)
                for i, a in enumerate((b2, gamma, beta)):
                    sp.dma_start(vec[:, i, :], a.partition_broadcast(P)).then_inc(loaded, 16)
                sp.dma_start(one_eps[:, :], eps.partition_broadcast(P)).then_inc(loaded, 16)
                pr.load_weights(sp)
                with sp.Fori(0, GROUPS) as c:
                    pr.load(sp, c)
                    pr.store(sp, c)
                sp.wait_ge(pr.put, 16 * GROUPS)

            @block.tensor
            def _(pe):
                def layers(c):
                    pe.wait_ge(z_ok, c + 1)
                    for k in range(GROUP + 2):
                        if k < GROUP:
                            pe.wait_ge(copied, free_at(c, k))
                            for i in range(2):
                                last = nc.tensor.transpose(p_t[:, k % 2, i * P:(i + 1) * P],
                                                           Z[:, k, i * P:(i + 1) * P], g.ident[:, :])
                            last.then_inc(turned, 1)
                        if 1 <= k <= GROUP:
                            j = k - 1
                            pe.wait_ge(copied, through(c, j))
                            pe.wait_ge(hid_ok, free_at(c, j))
                            for o in range(2):
                                for i in range(2):
                                    last = nc.tensor.matmul(
                                        p_h[:, j % 2, o * P:(o + 1) * P], w1[:, i, o * P:(o + 1) * P],
                                        zT[:, j % 2, i * P:(i + 1) * P],
                                        start=(i == 0), stop=(i == 1))
                            last.then_inc(hid, 1)
                        if k >= 2:
                            j = k - 2
                            pe.wait_ge(hid_ok, through(c, j))
                            pe.wait_ge(evac, free_at(c, j))
                            for i in range(2):
                                last = nc.tensor.matmul(p_z[:, j % 2, 0:DIM],
                                                        hT[:, j % 2, i * P:(i + 1) * P],
                                                        w2[:, i, :], start=(i == 0), stop=(i == 1))
                            last.then_inc(mult, 1)

                pe.wait_ge(loaded, 16 * 8)
                pe.wait_ge(pr.ready, 1)
                layers(0)
                layers(1)
                with pe.Fori(0, GROUPS - 2) as c:
                    layers(c + 2)
                    pr.tensor(pe, c)
                for c in (GROUPS - 2, GROUPS - 1):
                    pr.tensor(pe, c)

            @block.scalar
            def _(act):
                def layers(c, roots=None):
                    for k in range(GROUP + 2):
                        if k < GROUP:
                            act.wait_ge(turned, through(c, k))
                            act.wait_ge(hid, free_at(c, k))
                            act.activation(zT[:, k % 2, :], p_t[:, k % 2, 0:DIM], ACT.Copy)\
                                .then_inc(copied, 1)
                        if 1 <= k <= GROUP:
                            j = k - 1
                            act.wait_ge(hid, through(c, j))
                            act.wait_ge(mult, free_at(c, j))
                            for o in range(2):
                                last = act.activation(hT[:, j % 2, o * P:(o + 1) * P],
                                                      p_h[:, j % 2, o * P:(o + 1) * P], ACT.Relu,
                                                      bias=b1c[:, o:o + 1])
                            last.then_inc(hid_ok, 1)
                        if k >= 2:
                            j = k - 2
                            if j == 0:
                                act.wait_ge(out_free, c + 1)
                            act.wait_ge(mult, through(c, j))
                            act.activation(mlp_out[:, j, :], p_z[:, j % 2, 0:DIM], ACT.Copy)\
                                .then_inc(evac, 1)
                        if roots is not None and k in (3, 8):
                            ln.scalar(act, roots, k // 5)

                act.wait_ge(loaded, 16 * 8)
                act.wait_ge(pr.ready, 1)
                layers(0)
                layers(1, 0)
                with act.Fori(0, GROUPS - 2) as c:
                    layers(c + 2, c + 1)
                    pr.scalar(act, c)
                for n in range(2):
                    ln.scalar(act, GROUPS - 1, n)
                    pr.scalar(act, GROUPS - 2 + n)

            @block.vector
            def _(dve):
                pr.prepare(dve)
                dve.wait_ge(loaded, 16 * 8)
                o = Own(own)
                o.step(dve, dve.tensor_scalar(one_eps[:, :], one_eps[:, :], 1.0, None, ALU.add))

                def every(i):
                    return vec[:, i:i + 1, :].to_broadcast([P, GROUP, DIM])

                def make_z(c):
                    blocks = bass.ds(c * GROUP, GROUP)
                    dve.scalar_tensor_tensor(out=Z[:, :, :], in0=g.X[:, blocks, :],
                                             scalar=one_eps[:, 0:1],
                                             in1=g.sums[:, blocks, 0:DIM], op0=ALU.mult,
                                             op1=ALU.add).then_inc(z_ok, 1)

                def group(c, last=False):
                    w = Own(own, c * NV + 1)
                    blocks = bass.ds(c * GROUP, GROUP)
                    x = g.X[:, blocks, :]
                    w.step(dve, dve.tensor_tensor(R[:, :, :], x, every(0), ALU.add))
                    dve.wait_ge(evac, through(c, GROUP - 1))
                    dve.tensor_tensor(R[:, :, :], R[:, :, :], mlp_out[:, :, :], ALU.add)\
                        .then_inc(out_free, 1)
                    if not last:
                        make_z(c + 1)
                    dve.wait_ge(out_free, c + 2)
                    ln.vector(dve, w, c, 0, lambda k: R[:, k, :])
                    w.step(dve, dve.tensor_tensor(R[:, :, :], R[:, :, :], every(1), ALU.mult))
                    w.step(dve, dve.tensor_tensor(R[:, :, :], R[:, :, :], every(2), ALU.add))
                    w.step(dve, dve.scalar_tensor_tensor(out=x, in0=R[:, :, :], scalar=0.0, in1=x,
                                                         op0=ALU.max, op1=ALU.add))
                    ln.vector(dve, w, c, 1, lambda k: flat(g.X[:, bass.ds(c * GROUP + k, 1), :]))
                    dve.sem_inc(done, 1)
                    assert w.n == NV, w.n

                make_z(0)
                with dve.Fori(0, GROUPS - 1) as c:
                    group(c)
                group(GROUPS - 1, last=True)
                pr.split(dve)


def last_norm(nc, sem, g, out):
    with Memory(nc) as sb:
        own, done, stored = sem("end_own"), sem("end_done"), sem("end_stored")
        ln = Norm(nc, sem, sb, "end", 1)
        NV = 1 + Norm.STEPS
        with nc.Block() as block:

            @block.sync
            def _(sp):
                with sp.Fori(0, GROUPS - 1) as c:
                    sp.wait_ge(done, c + 1)
                    sp.dma_start(out[bass.ds(c * (GROUP * P), GROUP * P), :]
                                 .rearrange("(b p) d -> p b d", p=P),
                                 g.X[:, bass.ds(c * GROUP, GROUP), :]).then_inc(stored, 16)
                sp.wait_ge(done, GROUPS)
                a, z = (GROUPS - 1) * GROUP, BLOCKS - 1
                sp.dma_start(out[a * P:z * P, :].rearrange("(b p) d -> p b d", p=P), g.X[:, a:z, :])\
                    .then_inc(stored, 16)
                sp.dma_start(out[z * P:NODES, :], g.X[0:LAST, z, :]).then_inc(stored, 16)
                sp.wait_ge(stored, 16 * (GROUPS + 1))

            @block.scalar
            def _(act):
                with act.Fori(0, GROUPS) as c:
                    ln.scalar(act, c, 0)

            @block.vector
            def _(dve):
                with dve.Fori(0, GROUPS) as c:
                    w = Own(own, c * NV)
                    x = g.X[:, bass.ds(c * GROUP, GROUP), :]
                    w.step(dve, dve.tensor_tensor(x, x, g.sums[:, bass.ds(c * GROUP, GROUP), 0:DIM],
                                                  ALU.add))
                    ln.vector(dve, w, c, 0, lambda k: flat(g.X[:, bass.ds(c * GROUP + k, 1), :]))
                    dve.sem_inc(done, 1)
                    assert w.n == NV, w.n


class Kept:

    def __init__(self, nc, sb, attention):
        self.X = sb.sb("x", [P, BLOCKS, DIM], FP32)
        self.sums = sb.sb("sums", [P, BLOCKS, ROW], FP32)
        self.scores = sb.sb("scores", [P, BLOCKS, 3, 2 * HEADS], BF16)
        self.rows = sb.sb("src_rows", [P, STEPP], U32)
        self.rel_rows = sb.sb("rel_rows", [P, STEPP], U32)
        self.place = sb.sb("place", [P, STEPP], FP32)
        self.edge_w = sb.sb("edge_w", [P, STEPP], FP32)
        self.block_of = sb.sb("block_of", [1, STEPP], I32)
        self.iota_f = sb.sb("iota_f", [P, P], FP32)
        self.iota_p = sb.sb("iota_p", [P, 1], FP32)
        self.ident = sb.sb("ident", [P, P], FP32)
        self.ones = sb.sb("ones", [K * HEADS, P], FP32)
        self.follows = attention.sb("follows", [P, STEPP], BF16)
        self.starts = attention.sb("starts", [P, STEPP], BF16)
        self.ends = attention.sb("ends", [P, STEPP], BF16)
        self.goes_on = attention.sb("goes_on", [P, STEPP], BF16)
        self.opens = attention.sb("opens", [P, BATCHES], FP32)
        self.gates = attention.sb("gates", [P, BATCHES, HEADS * (K + 1)], BF16)
        self.gates_back = attention.sb("gates_back", [P, BATCHES, HEADS * (K + 1)], BF16)
        self.table = nc.dram_tensor("gat_rows", [PADN, ROW], FP32).ap()
        self.nodes = nc.dram_tensor("node_rows", [PADN, DIM], FP32).ap()
        self.by_rel = nc.dram_tensor("relation_rows", [RELS * PADN, DIM], FP32).ap()
        self.marks = nc.dram_tensor("segment_marks", [CPAD, HEADS, P + 1], FP32).ap()
        self.places = nc.dram_tensor("places_in_block", [CPAD, P], BF16).ap()
        self.turned01 = nc.dram_tensor("edge_to_node", [BATCHES * P, K, P], BF16).ap()


def graph_layers(nc, a, out, stages=99):
    with Memory(nc) as sb, Memory(nc) as attention:
        used = []

        def sem(name):
            used.append(nc.alloc_semaphore(name))
            return used[-1]

        g = Kept(nc, sb, attention)
        todo = [
            lambda: lay_out_walk(nc, sem, g, a["src"], a["dst"], a["edge_type_16"],
                                 a["edge_weight1"]),
            lambda: load_nodes(nc, sem, g, a["x"]),
            lambda: project(nc, sem, g, "p0", g.X, a["L0_gnn_W"], a["L0_gnn_att_src"]
                            .rearrange("h c -> (h c)"), a["L0_gnn_att_dst"].rearrange("h c -> (h c)")),
            lambda: aggregate_attention(nc, sem, g, "a0", first=True),
            lambda: finish_attention(nc, sem, g, "f0", a["L0_gnn_bias"], ALU.add, True),
            lambda: aggregate(nc, sem, g, "a1", g.nodes, g.rows, None),
            lambda: perceptron(nc, sem, g, a["L1_gnn_W1"], a["L1_gnn_b1"], a["L1_gnn_W2"],
                               a["L1_gnn_b2"], a["L1_gnn_eps"], a["L1_gnn_gamma"],
                               a["L1_gnn_beta"],
                               ("p2", a["L2_gnn_W1"],
                                a["L2_gnn_att_src1"].rearrange("a h c -> (a h c)"),
                                a["L2_gnn_att_dst1"].rearrange("a h c -> (a h c)"))),
            lambda: aggregate_attention(nc, sem, g, "a2"),
            lambda: finish_attention(nc, sem, g, "f2", a["L2_gnn_b1"], ALU.max, False,
                                     ("p3", a["L2_gnn_W2"],
                                      a["L2_gnn_att_src2"].rearrange("a h c -> (a h c)"),
                                      a["L2_gnn_att_dst2"].rearrange("a h c -> (a h c)"))),
            lambda: aggregate_attention(nc, sem, g, "a3"),
            attention.close,
            lambda: finish_attention(nc, sem, g, "f3", a["L2_gnn_b2"], ALU.max, True,
                                     rel=a["L3_gnn_weight"]),
            lambda: aggregate(nc, sem, g, "a4", g.by_rel, g.rel_rows, g.edge_w),
            lambda: last_norm(nc, sem, g, out),
        ]
        for stage in todo[:stages]:
            stage()
            nc.clear_and_free_semaphores(used)
            used.clear()
            nc.all_engine_barrier()
        return g


INPUTS = ["x", "src", "dst", "edge_type_16", "edge_weight1", "L0_gnn_W", "L0_gnn_att_src",
          "L0_gnn_att_dst", "L0_gnn_bias", "L1_gnn_W1", "L1_gnn_b1", "L1_gnn_W2", "L1_gnn_b2",
          "L1_gnn_eps", "L1_gnn_gamma", "L1_gnn_beta", "L2_gnn_W1", "L2_gnn_att_src1",
          "L2_gnn_att_dst1", "L2_gnn_b1", "L2_gnn_W2", "L2_gnn_att_src2", "L2_gnn_att_dst2",
          "L2_gnn_b2", "L3_gnn_weight"]


def kernel(**inputs):
    import numpy as np
    import concourse.bacc as bacc
    from concourse.bass_utils import run_bass_kernel_spmd

    nc = bacc.Bacc("TRN2", target_bir_lowering=False, num_devices=1)
    arrays, args = {}, {}
    for name in INPUTS:
        v = np.ascontiguousarray(np.asarray(inputs[name]))
        if name == "L1_gnn_eps":
            v = v.reshape(1)
        arrays[name] = v
        args[name] = nc.dram_tensor(name, v.shape, mybir.dt.from_np(v.dtype),
                                    kind="ExternalInput").ap()
    out = nc.dram_tensor("out", [NODES, DIM], FP32, kind="ExternalOutput").ap()
    graph_layers(nc, args, out)
    got = run_bass_kernel_spmd(nc, [arrays], core_ids=[0])
    return got.results[0]["out"]
```
